# Optimizing a Trainium2 kernel written in Bass

```python
import numpy as np
import jax
import jax.numpy as jnp

def _softmax(x, axis=-1):
    return jax.nn.softmax(x, axis=axis)

def _gelu(x):
    return jax.nn.gelu(x, approximate=True)

def _silu(x):
    return jax.nn.silu(x)

def _sigmoid(x):
    return jax.nn.sigmoid(x)

def _layernorm(x, axis=-1, eps=1e-05):
    m = jnp.mean(x, axis=axis, keepdims=True)
    v = jnp.var(x, axis=axis, keepdims=True)
    return (x - m) / jnp.sqrt(v + eps)

def _scatter_add(tgt, idx, src, axis=0):
    return tgt.at[idx].add(src)

def _segment_sum(src, seg, n):
    return jax.ops.segment_sum(src, seg, n)
kernel_name = 'mk_decoder_preln_d1_seqx_r8_08f2de'

def setup_inputs(seed: int=0):
    np.random.seed(seed)
    _w = jnp.asarray

    def _rec_inputs():
        import jax
        import jax.numpy as jnp
        _rk = jax.random.key(seed)
        x = 7.22e-05 + 1 * jax.random.normal(jax.random.fold_in(_rk, 1), (16, 128, 256), jnp.float32)
        _lenS = 128 - jax.random.randint(jax.random.fold_in(_rk, 7), (16,), 0, max(1, 128 // 4) + 1, jnp.int32)
        _lenS2 = 128 - jax.random.randint(jax.random.fold_in(_rk, 8), (16,), 0, max(1, 128 // 4) + 1, jnp.int32)
        _ctx_2048P = jax.random.normal(jax.random.fold_in(_rk, 11), (16, 16, 256), jnp.float32)
        _ctx_2048c = jax.random.dirichlet(jax.random.fold_in(_rk, 511), 0.3 * jnp.ones((16,), jnp.float32), (16, 128))
        _ctx_2048t = jnp.einsum('bsk,bkd->bsd', _ctx_2048c, _ctx_2048P)
        _ctx_2048t = _ctx_2048t * jax.lax.rsqrt(jnp.mean(jnp.square(_ctx_2048t)) + 1e-12) * 0.953939
        ctx_2048 = 4.13588e-05 + 0.999923 * (_ctx_2048t + 0.3 * jax.random.normal(jax.random.fold_in(_rk, 611), (16, 128, 256), jnp.float32))
        return (x, ctx_2048)
    x, ctx_2048 = _rec_inputs()

    def _L0_attn_setup():
        import jax, jax.numpy as jnp
        import numpy as np
        EMBED_DIM = 256
        NUM_HEADS = 16
        HEAD_DIM = EMBED_DIM // NUM_HEADS
        SCALE = EMBED_DIM ** (-0.5)
        key = jax.random.key(seed)
        ks = jax.random.split(key, 9)
        d = EMBED_DIM
        s = 1.0 / np.sqrt(d)
        inp = {'x': jax.random.normal(ks[0], (2, 256, d), dtype=jnp.float32), 'wq': jax.random.uniform(ks[1], (d, d), jnp.float32, -s, s), 'bq': jnp.zeros((d,), jnp.float32), 'wk': jax.random.uniform(ks[2], (d, d), jnp.float32, -s, s), 'bk': jnp.zeros((d,), jnp.float32), 'wv': jax.random.uniform(ks[3], (d, d), jnp.float32, -s, s), 'bv': jnp.zeros((d,), jnp.float32), 'wo': jax.random.uniform(ks[4], (d, d), jnp.float32, -s, s), 'bo': jnp.zeros((d,), jnp.float32)}
        return inp
    _L0_attn_all = _L0_attn_setup()
    _L0_attn_in = {k: v for k, v in _L0_attn_all.items() if k in ('wq', 'bq', 'wk', 'bk', 'wv', 'bv', 'wo', 'bo')}
    del _L0_attn_all

    def _L0_xattn_setup():
        import jax, jax.numpy as jnp
        import numpy as np
        NUM_FEATURES = 128
        NUM_HEADS = 16
        HEAD_DIM = NUM_FEATURES // NUM_HEADS
        B, SQ, SKV = (4, 256, 256)

        def _split_heads(x):
            b, s, _ = x.shape
            return x.reshape(b, s, NUM_HEADS, HEAD_DIM).transpose(0, 2, 1, 3)
        key = jax.random.key(seed)
        ks = jax.random.split(key, 8)
        w_scale = 1.0 / np.sqrt(NUM_FEATURES)
        return {'query': jax.random.normal(ks[0], (B, NUM_FEATURES, SQ), dtype=jnp.float32), 'key': jax.random.normal(ks[1], (B, NUM_FEATURES, SKV), dtype=jnp.float32), 'value': jax.random.normal(ks[2], (B, NUM_FEATURES, SKV), dtype=jnp.float32), 'Wq': jax.random.normal(ks[3], (NUM_FEATURES, NUM_FEATURES), dtype=jnp.float32) * w_scale, 'bq': jnp.zeros((NUM_FEATURES,), dtype=jnp.float32), 'Wk': jax.random.normal(ks[4], (NUM_FEATURES, NUM_FEATURES), dtype=jnp.float32) * w_scale, 'bk': jnp.zeros((NUM_FEATURES,), dtype=jnp.float32), 'Wv': jax.random.normal(ks[5], (NUM_FEATURES, NUM_FEATURES), dtype=jnp.float32) * w_scale, 'bv': jnp.zeros((NUM_FEATURES,), dtype=jnp.float32), 'Wo': jax.random.normal(ks[6], (NUM_FEATURES, NUM_FEATURES), dtype=jnp.float32) * w_scale, 'bo': jnp.zeros((NUM_FEATURES,), dtype=jnp.float32)}
    _L0_xattn_all = _L0_xattn_setup()
    _L0_xattn_in = {k: v for k, v in _L0_xattn_all.items() if k in ('Wq', 'bq', 'Wk', 'bk', 'Wv', 'bv', 'Wo', 'bo')}
    del _L0_xattn_all

    def _L0_ffn_setup():
        import jax, jax.numpy as jnp
        import numpy as np
        D = 256
        M = 128
        E = 32
        K = 6
        G = 8
        KG = 4
        SH = 256
        SCALE = 2.5

        def _route(xf, Wr, br):
            T = xf.shape[0]
            s = jax.nn.sigmoid(xf @ Wr.T + br)
            sg = s.reshape(T, G, E // G)
            group_w = jax.lax.top_k(sg, 2)[0].sum(-1)
            top_g = jax.lax.top_k(group_w, KG)[1]
            gmask = jnp.zeros((T, G), bool).at[jnp.arange(T)[:, None], top_g].set(True)
            masked = jnp.where(gmask[:, :, None], sg, 0.0).reshape(T, E)
            idx = jax.lax.top_k(masked, K)[1]
            w = jnp.take_along_axis(s, idx, axis=1)
            w = w / (w.sum(-1, keepdims=True) + 1e-20)
            return (idx, w * SCALE)
        key = jax.random.key(seed)
        ks = jax.random.split(key, 7)
        w = 0.02
        return {'hidden_tensor': jax.random.normal(ks[0], (2, 256, D), dtype=jnp.float32), 'Wr': jax.random.normal(ks[1], (E, D), dtype=jnp.float32) * w, 'br': jax.random.normal(ks[2], (E,), dtype=jnp.float32) * w, 'W1': jax.random.normal(ks[3], (E, M, D), dtype=jnp.float32) * w, 'W2': jax.random.normal(ks[4], (E, D, M), dtype=jnp.float32) * w, 'Ws1': jax.random.normal(ks[5], (SH, D), dtype=jnp.float32) * w, 'Ws2': jax.random.normal(ks[6], (D, SH), dtype=jnp.float32) * w}
    _L0_ffn_all = _L0_ffn_setup()
    _L0_ffn_in = {k: v for k, v in _L0_ffn_all.items() if k in ('Wr', 'br', 'W1', 'W2', 'Ws1', 'Ws2')}
    del _L0_ffn_all
    return {'x': x, 'ctx_2048': ctx_2048, 'L0_attn_wq': _L0_attn_in['wq'], 'L0_attn_bq': _L0_attn_in['bq'], 'L0_attn_wk': _L0_attn_in['wk'], 'L0_attn_bk': _L0_attn_in['bk'], 'L0_attn_wv': _L0_attn_in['wv'], 'L0_attn_bv': _L0_attn_in['bv'], 'L0_attn_wo': _L0_attn_in['wo'], 'L0_attn_bo': _L0_attn_in['bo'], 'L0_xattn_Wq': _L0_xattn_in['Wq'], 'L0_xattn_bq': _L0_xattn_in['bq'], 'L0_xattn_Wk': _L0_xattn_in['Wk'], 'L0_xattn_bk': _L0_xattn_in['bk'], 'L0_xattn_Wv': _L0_xattn_in['Wv'], 'L0_xattn_bv': _L0_xattn_in['bv'], 'L0_xattn_Wo': _L0_xattn_in['Wo'], 'L0_xattn_bo': _L0_xattn_in['bo'], 'L0_ffn_Wr': _L0_ffn_in['Wr'], 'L0_ffn_br': _L0_ffn_in['br'], 'L0_ffn_W1': _L0_ffn_in['W1'], 'L0_ffn_W2': _L0_ffn_in['W2'], 'L0_ffn_Ws1': _L0_ffn_in['Ws1'], 'L0_ffn_Ws2': _L0_ffn_in['Ws2']}

def reference(x, ctx_2048, L0_attn_wq, L0_attn_bq, L0_attn_wk, L0_attn_bk, L0_attn_wv, L0_attn_bv, L0_attn_wo, L0_attn_bo, L0_xattn_Wq, L0_xattn_bq, L0_xattn_Wk, L0_xattn_bk, L0_xattn_Wv, L0_xattn_bv, L0_xattn_Wo, L0_xattn_bo, L0_ffn_Wr, L0_ffn_br, L0_ffn_W1, L0_ffn_W2, L0_ffn_Ws1, L0_ffn_Ws2):
    import jax
    import jax.numpy as jnp

    def _L0_attn_ref(x, wq, bq, wk, bk, wv, bv, wo, bo):
        import jax, jax.numpy as jnp
        import numpy as np
        EMBED_DIM = 256
        NUM_HEADS = 16
        HEAD_DIM = EMBED_DIM // NUM_HEADS
        SCALE = EMBED_DIM ** (-0.5)
        b, t, d = x.shape
        h, hd = (NUM_HEADS, HEAD_DIM)
        q = (x @ wq + bq).reshape(b, t, h, hd).transpose(0, 2, 1, 3)
        k = (x @ wk + bk).reshape(b, t, h, hd).transpose(0, 2, 1, 3)
        v = (x @ wv + bv).reshape(b, t, h, hd).transpose(0, 2, 1, 3)
        scores = jnp.einsum('bhqd,bhkd->bhqk', q, k) * SCALE
        probs = jax.nn.softmax(scores, axis=-1)
        attn = jnp.einsum('bhqk,bhkd->bhqd', probs, v)
        attn = attn.transpose(0, 2, 1, 3).reshape(b, t, d)
        return attn @ wo + bo

    def _L0_xattn_ref(query, key, value, Wq, bq, Wk, bk, Wv, bv, Wo, bo):
        import jax, jax.numpy as jnp
        import numpy as np
        NUM_FEATURES = 128
        NUM_HEADS = 16
        HEAD_DIM = NUM_FEATURES // NUM_HEADS
        B, SQ, SKV = (4, 256, 256)

        def _split_heads(x):
            b, s, _ = x.shape
            return x.reshape(b, s, NUM_HEADS, HEAD_DIM).transpose(0, 2, 1, 3)
        q_in = query.transpose(0, 2, 1)
        k_in = key.transpose(0, 2, 1)
        v_in = value.transpose(0, 2, 1)
        q = _split_heads(jnp.einsum('bsf,of->bso', q_in, Wq) + bq)
        k = _split_heads(jnp.einsum('bsf,of->bso', k_in, Wk) + bk)
        v = _split_heads(jnp.einsum('bsf,of->bso', v_in, Wv) + bv)
        scale = 1.0 / jnp.sqrt(jnp.float32(NUM_FEATURES))
        scores = jnp.einsum('bhqd,bhkd->bhqk', q, k) * scale
        attn = jax.nn.softmax(scores, axis=-1)
        out = jnp.einsum('bhqk,bhkd->bhqd', attn, v)
        b = out.shape[0]
        out = out.transpose(0, 2, 1, 3).reshape(b, -1, NUM_FEATURES)
        out = jnp.einsum('bsf,of->bso', out, Wo) + bo
        return out.transpose(0, 2, 1)

    def _L0_ffn_ref(hidden_tensor, Wr, br, W1, W2, Ws1, Ws2):
        import jax, jax.numpy as jnp
        import numpy as np
        D = 256
        M = 128
        E = 32
        K = 6
        G = 8
        KG = 4
        SH = 256
        SCALE = 2.5

        def _route(xf, Wr, br):
            T = xf.shape[0]
            s = jax.nn.sigmoid(xf @ Wr.T + br)
            sg = s.reshape(T, G, E // G)
            group_w = jax.lax.top_k(sg, 2)[0].sum(-1)
            top_g = jax.lax.top_k(group_w, KG)[1]
            gmask = jnp.zeros((T, G), bool).at[jnp.arange(T)[:, None], top_g].set(True)
            masked = jnp.where(gmask[:, :, None], sg, 0.0).reshape(T, E)
            idx = jax.lax.top_k(masked, K)[1]
            w = jnp.take_along_axis(s, idx, axis=1)
            w = w / (w.sum(-1, keepdims=True) + 1e-20)
            return (idx, w * SCALE)
        B, Tlen, C = hidden_tensor.shape
        xf = hidden_tensor.reshape(-1, C).astype(jnp.float32)
        T = xf.shape[0]
        idx, w = _route(xf, Wr, br)
        gate = jnp.zeros((T, E), w.dtype).at[jnp.arange(T)[:, None], idx].add(w)

        def step(acc, ew):
            w1, w2, g = ew
            h = jnp.square(jax.nn.relu(xf @ w1.T)) @ w2.T
            return (acc + g[:, None] * h, None)
        acc, _ = jax.lax.scan(step, jnp.zeros_like(xf), (W1, W2, gate.T))
        moe_out = acc.reshape(B, Tlen, C).astype(hidden_tensor.dtype)
        shared = jnp.square(jax.nn.relu(hidden_tensor @ Ws1.T)) @ Ws2.T
        return shared + moe_out
    x = x + _L0_attn_ref(_layernorm(x, axis=-1), L0_attn_wq, L0_attn_bq, L0_attn_wk, L0_attn_bk, L0_attn_wv, L0_attn_bv, L0_attn_wo, L0_attn_bo)
    x = x + _L0_xattn_ref(_layernorm(x, axis=-1), ctx_2048, ctx_2048, L0_xattn_Wq, L0_xattn_bq, L0_xattn_Wk, L0_xattn_bk, L0_xattn_Wv, L0_xattn_bv, L0_xattn_Wo, L0_xattn_bo)
    x = x + _L0_ffn_ref(_layernorm(x, axis=-1), L0_ffn_Wr, L0_ffn_br, L0_ffn_W1, L0_ffn_W2, L0_ffn_Ws1, L0_ffn_Ws2)
    return x

_drawn_inputs = setup_inputs


def setup_inputs(seed=0):
    import zlib

    import numpy as np

    out = dict(_drawn_inputs(seed))
    spreads = {'L0_attn_bq': (0.0, 0.8),
     'L0_attn_bk': (0.0, 0.8),
     'L0_attn_bv': (0.0, 0.1),
     'L0_attn_bo': (0.0, 0.1),
     'L0_xattn_bq': (0.0, 0.8),
     'L0_xattn_bk': (0.0, 0.8),
     'L0_xattn_bv': (0.0, 0.1),
     'L0_xattn_bo': (0.0, 0.1)}
    factors = {'L0_attn_wq': 8.0, 'L0_attn_wk': 8.0, 'L0_ffn_br': 7.96}
    for name, (base, spread) in spreads.items():
        noise = np.random.default_rng([zlib.crc32(name.encode()), seed]).standard_normal(out[name].shape)
        drawn = base * np.exp(spread * noise) if base else spread * noise
        out[name] = jnp.asarray(drawn.astype(out[name].dtype))
    for name, factor in factors.items():
        out[name] = (out[name] * factor).astype(out[name].dtype)
    return out
```

```python
from contextlib import ExitStack

import concourse.bass as bass
from concourse import mybir

F32 = mybir.dt.float32
F32R = mybir.dt.float32r
BF16 = mybir.dt.bfloat16
ALU = mybir.AluOpType
ACT = mybir.ActivationFunctionType
AX = mybir.AxisListType

P = 128
EPS = 1e-5
ROUTED_SCALE = 2.5
FIRST, LAST = 4, 16
STAGES = ("SA", "SB", "X1", "X2", "R")

SLOTS = """
p1 0, ln3a, ln1a
x2c 0, p1 1, ln3b, ln1b
x2c 1, p1 2, x3T
x2c 2, x2c 3, p1 3, xT
x2c 4, mT, logits
x2c 5, x1c 0, xpv 0, qk
x2c 6, x1c 1, gates 0
x2c 7, x1c 2, v
x2c 8, p2 0, x1c 3, gates 1
x2c 9, p2 1, x1c 4, xpv 1
x2c 10, p2 2, x1c 5, gates 2
x2c 11, p2 3, x1c 6
x2c 12, x1c 7, x1c 8, pv, gates 3
x2c 13, x1c 9, xpv 2, norm
x2c 14, x1c 10, attnT, gates 4
x2c 15, x1c 11, wo
x1c 12, gates 5, ln2a, xpv 3
x1c 13, ln2b, xnorm 0, xnorm 1
x1c 14, xqk, gT
x1c 15, xattnT, xv, xmT, y
"""
SCRIPT = [s.strip() for line in SLOTS.strip().splitlines() for s in line.split(",")]
SCORES, EXPS = ("p1", "x1c"), ("p2", "x2c")
STAGE_OF = {"p1": "SB", "p2": "SB", "mT": "SB", "pv": "SB", "norm": "SB", "attnT": "SB", "wo": "SB", "ln2a": "SB",
            "ln2b": "SB", "xqk": "SB", "ln1a": "SA", "ln1b": "SA", "xT": "SA", "qk": "SA", "v": "SA",
            "x1c": "X1", "xmT": "X1", "xv": "X1", "x2c": "X2", "xpv": "X2", "xnorm": "X2", "xattnT": "X2", "y": "X2",
            "ln3a": "R", "ln3b": "R", "x3T": "R", "logits": "R", "gates": "R", "gT": "R"}


def decoder_layer(nc, x, ctx_in, wqkv, qk_bias, v_bias, wo, bo, xw, xqk_bias, xv_bias, xbo, wr, br, experts, eye,
                  out, gates_dram):
    B, T, D = x.shape
    H = 16
    HD = D // H
    XH = T // H
    E = wr.shape[2]
    NE = experts.shape[0]
    SCALE = float(D) ** -0.5
    XSCALE = float(T) ** -0.5
    NX = D // P
    assert T == P and D == 2 * P and 3 * 2 * HD == 96 and 3 * 4 * XH == 96 and NE % 2 == 0

    class Turn:

        def __init__(self, pair, parity):
            self.it = pair * 2 + parity
            self.pair = pair
            self.parity = parity

        def batch(self, stage, back=0):
            return self.it - (STAGES.index(stage) + back)

        def side(self, stage):
            return (self.parity + STAGES.index(stage)) % 2

        def earlier_on_side(self, stage):
            return self.pair + (self.parity - STAGES.index(stage)) // 2

        def has(self, stage):
            return not isinstance(self.it, int) or 0 <= self.batch(stage) < B

        def steps(self):
            for s in SCRIPT:
                name, _, n = s.partition(" ")
                if self.has(STAGE_OF[name]):
                    yield name, int(n or 0)

    def turns(eng):
        for it in range(FIRST):
            yield Turn(it // 2, it % 2)
        with eng.Fori(FIRST // 2, LAST // 2) as pair:
            yield Turn(pair, 0)
            yield Turn(pair, 1)
        for it in range(LAST, B + len(STAGES) - 1):
            yield Turn(it // 2, it % 2)

    def ring(turn, kinds, step, n):
        def each(it):
            return sum(1 for s in SCRIPT if s.split()[0] in kinds and 0 <= it - STAGES.index(STAGE_OF[s.split()[0]]) < B)
        if isinstance(turn.it, int):
            before = sum(each(it) for it in range(turn.it))
        else:
            before = (turn.it - FIRST) * each(FIRST) + sum(each(it) for it in range(FIRST))
        within = [s for s in turn.steps() if s[0] in kinds].index((step, n))
        return within % 2, before + within + 1

    with ExitStack() as stack:
        def sb(name, shape, dt=F32):
            return stack.enter_context(nc.sbuf_tensor(name, shape, dt))

        def sem(name):
            return stack.enter_context(nc.semaphore(name))

        xres = sb("xres", [P, B, D])
        ctx_sb = [sb(f"ctx{i}", [P, D]) for i in range(2)]
        wqkv_sb = sb("wqkv_sb", [P, 2, 6, P])
        qkb_sb = sb("qkb_sb", [P, 4])
        vb_sb = sb("vb_sb", [P, 2])
        wo_sb = sb("wo_sb", [P, 2, D])
        bo_sb = sb("bo_sb", [P, D])
        xw_sb = sb("xw_sb", [P, 4, P])
        xqkb_sb = sb("xqkb_sb", [P, 2])
        xvb_sb = sb("xvb_sb", [P, 1])
        xbo_sb = sb("xbo_sb", [P, 1])
        wr_sb = sb("wr_sb", [P, 2, E])
        br_sb = sb("br_sb", [P, E])
        eye_sb = sb("eye_sb", [P, P])
        stats = [sb(f"stats{i}", [P, 6]) for i in range(3)]
        mean_var = [sb(f"mean_var{i}", [P, 2]) for i in range(3)]
        var_eps = [sb(f"var_eps{i}", [P, 1]) for i in range(3)]
        rstd = [sb(f"rstd{i}", [P, 1]) for i in range(3)]
        xn = [sb(f"xn{i}", [P, D]) for i in range(3)]
        exponents = sb("exponents", [P, E + 1])
        xnT = sb("xnT", [P, 2, T])
        qk_full = sb("qk_full", [P, 4, T])
        qk_hi = sb("qk_hi", [P, 4, T])
        qk_lo = sb("qk_lo", [P, 4, T])
        Q3 = [sb(f"Q3_{i}", [98, 8, 2, T]) for i in range(2)]
        K3 = [sb(f"K3_{i}", [98, 8, T]) for i in range(2)]
        V1 = [sb(f"V1_{i}", [P, H, 32]) for i in range(2)]
        negmax = sb("negmax", [P, H])
        max_hi = sb("max_hi", [H, T])
        max_lo = sb("max_lo", [H, T])
        probs = sb("probs", [P, H, T])
        pv_sb = sb("pv_sb", [P, 4, T])
        rsum = sb("rsum", [P, H])
        attn = sb("attn", [P, D])
        attnT = sb("attnT", [P, 2, T])
        x_bo = sb("x_bo", [P, D])
        xqk_full = sb("xqk_full", [P, 2, D])
        xqk_hi = sb("xqk_hi", [P, 2, D])
        xqk_lo = sb("xqk_lo", [P, 2, D])
        XQ3 = [sb(f"XQ3_{i}", [98, 4, 4, D]) for i in range(2)]
        XK3 = [sb(f"XK3_{i}", [98, 4, D]) for i in range(2)]
        XV1 = [sb(f"XV1_{i}", [P, NX, H, 32]) for i in range(2)]
        xnegmax = sb("xnegmax", [P, NX, H])
        xmax_hi = sb("xmax_hi", [H, D])
        xmax_lo = sb("xmax_lo", [H, D])
        xprobs = sb("xprobs", [P, NX, H, D])
        xpv_sb = sb("xpv_sb", [P, 4, D])
        xrsum = sb("xrsum", [P, NX, H])
        xattn = sb("xattn", [P, NX, P])
        xattnT = sb("xattnT", [P, D])
        x3T_now = sb("x3T_now", [P, 2, T])
        x3T = sb("x3T", [P, 2, B * T])
        logits = sb("logits", [P, E])
        neg_exp = sb("neg_exp", [P, E])
        one_plus = sb("one_plus", [P, E])
        sig = sb("sig", [P, E])
        pair_max = sb("pair_max", [P, 8, 2])
        pair_min = sb("pair_min", [P, 8, 2])
        top1 = sb("top1", [P, 8])
        top2a = sb("top2a", [P, 8])
        top2b = sb("top2b", [P, 8])
        top2 = sb("top2", [P, 8])
        group_w = sb("group_w", [P, 4 + 8])
        top_groups = sb("top_groups", [P, 8])
        groups_marked = sb("groups_marked", [P, 4 + 8])
        masked = sb("masked", [P, 2 + E])
        top_experts = sb("top_experts", [P, 8])
        experts_marked = sb("experts_marked", [P, 2 + E])
        chosen = sb("chosen", [P, E])
        total = sb("total", [P, 1])
        total_eps = sb("total_eps", [P, 1])
        inv_total = sb("inv_total", [P, 1])
        gates = sb("gates", [P, E])
        root_gates = sb("root_gates", [P, E])
        gatesT = sb("gatesT", [E, T])
        w_sb = [sb(f"w_sb{i}", [P, 4, P]) for i in range(2)]
        groot = [probs[:, 8 * i:8 * i + 8, :].rearrange("p (a h) t -> p a (h t)", a=2) for i in range(2)]
        act1 = [xprobs[:, 0, 2 * i:2 * i + 2, :].rearrange("p a t -> p (a t)") for i in range(4)]
        act2 = [xprobs[:, 1, 2 * i:2 * i + 2, :].rearrange("p a t -> p (a t)") for i in range(4)]
        zeros = sb("zeros", [P, 512], BF16)
        ones = sb("ones", [64, (NE - E) * B * T // 64])

        bank = [stack.enter_context(nc.psum_tensor(f"bank{i}", [P, 512], F32)) for i in range(8)]
        score_ring, exp_ring, pv_bank, A, Bk = bank[0:2], bank[2:4], bank[4:6], bank[6], bank[7]

        loaded_w, loaded_x, loaded_ctx = sem("loaded_w"), sem("loaded_x"), [sem("loaded_ctx0"), sem("loaded_ctx1")]
        cleared, consts_set, pool_consts = sem("cleared"), sem("consts_set"), sem("pool_consts")
        st_done = [sem(f"stats{i}_done") for i in range(3)]
        mv_done = [sem(f"mean_var{i}_done") for i in range(3)]
        ve_done = [sem(f"var_eps{i}_done") for i in range(3)]
        rstd_done = [sem(f"rstd{i}_done") for i in range(3)]
        xn_done = [sem(f"xn{i}_done") for i in range(3)]
        scores_in, scores_max = sem("scores_in"), sem("scores_max")
        exps_in, exps_done = sem("exps_in"), sem("exps_done")
        xT_in, xnT_done = sem("xT_in"), sem("xnT_done")
        qk_in, qk_full_done, qk_hi_done, qk_lo_done = sem("qk_in"), sem("qk_full_done"), sem("qk_hi_done"), sem("qk_lo_done")
        q_placed, k_placed = sem("q_placed"), sem("k_placed")
        v_in, v_done = sem("v_in"), sem("v_done")
        mT_in, max_hi_done, max_lo_done, max_placed = sem("mT_in"), sem("max_hi_done"), sem("max_lo_done"), sem("max_placed")
        pv_in, pv_copied, norm_in = sem("pv_in"), sem("pv_copied"), sem("norm_in")
        rsum_done, attn_done, attnT_in, attnT_done = sem("rsum_done"), sem("attn_done"), sem("attnT_in"), sem("attnT_done")
        wo_in, x_bo_done, x1_done = sem("wo_in"), sem("x_bo_done"), sem("x1_done")
        xqk_in, xqk_full_done, xqk_hi_done, xqk_lo_done = sem("xqk_in"), sem("xqk_full_done"), sem("xqk_hi_done"), sem("xqk_lo_done")
        xq_placed, xk_placed = sem("xq_placed"), sem("xk_placed")
        xmT_in, xmax_hi_done, xmax_lo_done, xmax_placed = sem("xmT_in"), sem("xmax_hi_done"), sem("xmax_lo_done"), sem("xmax_placed")
        xv_in, xv_done = sem("xv_in"), sem("xv_done")
        xpv_in = sem("xpv_in")
        xpv_copied = sem("xpv_copied")
        xnorm_in, xrsum_done, xattn_done = sem("xnorm_in"), sem("xrsum_done"), sem("xattn_done")
        xattnT_in, xattnT_done, y_in, x2_done = sem("xattnT_in"), sem("xattnT_done"), sem("y_in"), sem("x2_done")
        x3T_in, x3T_now_done, x3T_kept = sem("x3T_in"), sem("x3T_now_done"), sem("x3T_kept")
        logits_in, logits_done, neg_exp_done = sem("logits_in"), sem("logits_done"), sem("neg_exp_done")
        gate_steps = sem("gate_steps")
        root_done, gT_in, gatesT_done, gates_stored = sem("root_done"), sem("gT_in"), sem("gatesT_done"), sem("gates_stored")
        GATE_STEPS = 19
        GATE_PARTS = (0, 4, 8, 11, 14, 16)
        ones_stored = sem("ones_stored")
        passed = sem("passed")
        w_loaded = [sem("w_loaded0"), sem("w_loaded1")]
        groot_loaded = [sem("groot_loaded0"), sem("groot_loaded1")]
        hidden_in, act1_done, act2_done, expert_added = sem("hidden_in"), sem("act1_done"), sem("act2_done"), sem("expert_added")
        half_in, half_added, out_stored = sem("half_in"), sem("half_added"), sem("out_stored")

        def after(eng, s, batch, n=1, k=0, by=1):
            if isinstance(batch, int) and batch < 0:
                return
            eng.wait_ge(s, (batch * n + k + 1) * by)

        def after_alone(eng, s, batch, n=1, k=0, by=1):
            if isinstance(batch, int):
                after(eng, s, batch, n, k, by)
            else:
                after(eng, s, batch, n, k, by)
                eng.sem_inc(passed, 1)

        A_USES = [("x3T", x3T_now_done, 1, 0), ("xT", xnT_done, 1, 0), ("v", v_done, 1, 0),
                  ("norm", attn_done, 1, 0), ("wo", x1_done, 1, 0), ("xnorm0", xattn_done, 2, 0), ("gT", gatesT_done, 1, 0),
                  ("xattnT", xattnT_done, 1, 0), ("xv", xv_done, 1, 0)]
        B_USES = [("mT", max_lo_done, 1, 0), ("logits", logits_done, 1, 0), ("qk", qk_full_done, 1, 0),
                  ("attnT", attnT_done, 1, 0), ("xnorm1", xattn_done, 2, 1), ("xqk", xqk_full_done, 1, 0),
                  ("xmT", xmax_lo_done, 1, 0), ("y", x2_done, 1, 0)]
        used = [s.replace("xnorm ", "xnorm") for s in SCRIPT]
        assert all([used.index(u[0]) for u in uses] == sorted(used.index(u[0]) for u in uses) for uses in (A_USES, B_USES))

        def bank_free(eng, turn, uses, name):
            at = [u[0] for u in uses].index(name)
            order = [(u, 0) for u in reversed(uses[:at])] + [(u, 1) for u in reversed(uses)]
            for (use, s, n, k), back in order:
                b = turn.batch(STAGE_OF[use.rstrip("01")], back)
                if not isinstance(b, int) or 0 <= b < B:
                    after(eng, s, b, n, k)
                    return

        block = stack.enter_context(nc.Block())

        @block.sync
        def _(sp):
            for dst, src in ((xres[:, 0, :], x[0]), (eye_sb[:], eye)):
                sp.dma_start(dst, src).then_inc(loaded_x, 16)
            for dst, src in ((wqkv_sb[:], wqkv), (qkb_sb[:], qk_bias), (vb_sb[:], v_bias), (wo_sb[:], wo), (bo_sb[:], bo),
                             (xw_sb[:], xw), (xqkb_sb[:], xqk_bias), (xvb_sb[:], xv_bias), (xbo_sb[:], xbo), (wr_sb[:], wr),
                             (br_sb[:], br), (xres[:, 1:B, :], x[1:B].rearrange("b t d -> t b d"))):
                sp.dma_start(dst, src).then_inc(loaded_w, 16)
            for i in range(2):
                sp.dma_start(ctx_sb[i][:], ctx_in[i]).then_inc(loaded_ctx[i], 16)
            sp.wait_ge(consts_set, 1)
            for turn in turns(sp):
                for name, n in turn.steps():
                    b, side = turn.batch(STAGE_OF[name]), turn.side(STAGE_OF[name])
                    if name == "qk":
                        after_alone(sp, qk_hi_done, b)
                        after_alone(sp, qk_lo_done, b)
                        after_alone(sp, pv_in, b - 2)
                        for c, qs in enumerate((qk_hi, qk_hi, qk_lo)):
                            for odd in range(2):
                                r = 32 * c + 16 * odd
                                sp.dma_start(Q3[side][r:r + 16, :, odd, :], qs[:, odd, :]).then_inc(q_placed, 16)
                    elif name == "xqk":
                        after_alone(sp, xqk_hi_done, b)
                        after_alone(sp, xqk_lo_done, b)
                        after_alone(sp, xpv_in, b - 2, 4, 3)
                        for c, qs in enumerate((xqk_hi, xqk_hi, xqk_lo)):
                            for hh in range(4):
                                r = 32 * c + 8 * hh
                                sp.dma_start(XQ3[side][r:r + 8, :, hh, :],
                                             qs[32 * hh:32 * hh + 32, 0, :]).then_inc(xq_placed, 16)
                    elif name == "xv" and not (isinstance(b, int) and b + 2 >= B):
                        after_alone(sp, xv_in, b)
                        sp.dma_start(ctx_sb[side][:], ctx_in[b + 2]).then_inc(loaded_ctx[side], 16)
                    elif name == "gT":
                        after_alone(sp, gatesT_done, b)
                        sp.dma_start(gates_dram[0:E, bass.ds(b * T, T)], gatesT[:]).then_inc(gates_stored, 16)
            sp.wait_ge(gates_stored, B * 16)
            sp.wait_ge(ones_stored, 16)

            def load(j, half, it):
                for side in range(2):
                    if not (isinstance(it, int) and it == 0):
                        sp.wait_ge(expert_added, it * 4 - 2 + 2 * side)
                    sp.dma_start(w_sb[side][:], experts[j * 2 + side]).then_inc(w_loaded[side], 16)
                    row = gates_dram[bass.ds(j * 2 + side, 1), 1024 * half:1024 * half + 1024]
                    sp.dma_start(probs[:, 8 * side:8 * side + 8, :].rearrange("p h t -> p (h t)"),
                                 row.to_broadcast([P, 1024])).then_inc(groot_loaded[side], 16)

            load(0, 0, 0)
            with sp.Fori(1, NE // 2) as j:
                load(j, 0, j)
            with sp.Fori(0, NE // 2) as j:
                load(j, 1, j + NE // 2)
            for half in range(2):
                for t in range(8):
                    i = 8 * half + t
                    sp.wait_ge(half_added, i + 1)
                    sp.dma_start(out[i], xres[:, i, :]).then_inc(out_stored, 16)
            sp.wait_ge(out_stored, 16 * B)

        @block.gpsimd
        def _(pool):
            nc.gpsimd.memset(exponents[:, 0:E], 0.5)
            nc.gpsimd.memset(exponents[:, E:E + 1], -0.5)
            nc.gpsimd.memset(ones[:], 1.0).then_inc(pool_consts, 1)
            pool.wait_ge(pool_consts, 1)
            pool.dma_start(gates_dram[E:NE, :].rearrange("e (a t) -> (e a) t", a=64 // (NE - E)), ones[:]).then_inc(ones_stored, 16)
            for turn in turns(pool):
                for name, n in turn.steps():
                    b, side = turn.batch(STAGE_OF[name]), turn.side(STAGE_OF[name])
                    if name in ("ln1a", "ln2a", "ln3a"):
                        i = int(name[2]) - 1
                        after_alone(pool, mv_done[i], b)
                        nc.gpsimd.tensor_scalar(var_eps[i][:], mean_var[i][:, 1:2], EPS, None, ALU.add).then_inc(ve_done[i], 1)
                        after(pool, ve_done[i], b)
                        nc.gpsimd.tensor_tensor(rstd[i][:], var_eps[i][:], exponents[:, E:E + 1],
                                                ALU.pow).then_inc(rstd_done[i], 1)
                    elif name == "qk":
                        after(pool, qk_hi_done, b)
                        after(pool, q_placed, b - 1, 6, 5, 16)
                        after(pool, k_placed, b - 1, 6, 5, 16)
                        nc.gpsimd.tensor_tensor(qk_lo[:].bitcast(F32R), qk_full[:], qk_hi[:], ALU.subtract).then_inc(qk_lo_done, 1)
                        after_alone(pool, qk_lo_done, b)
                        after_alone(pool, pv_in, b - 2)
                        for c, ks in enumerate((qk_hi, qk_lo, qk_hi)):
                            for odd in range(2):
                                r = 32 * c + 16 * odd
                                pool.dma_start(K3[side][r:r + 16, :, :], ks[:, 2 + odd, :]).then_inc(k_placed, 16)
                    elif name == "p2" and n == 0:
                        if isinstance(b, int):
                            pool.wait_ge(loaded_w, 12 * 16)
                        after(pool, x1_done, b - 1)
                        nc.gpsimd.tensor_tensor(x_bo[:], xres[:, b, :], bo_sb[:], ALU.add).then_inc(x_bo_done, 1)
                    elif name == "xqk":
                        after(pool, xqk_hi_done, b)
                        after(pool, xq_placed, b - 1, 12, 11, 16)
                        after(pool, xk_placed, b - 1, 3, 2, 16)
                        nc.gpsimd.tensor_tensor(xqk_lo[:].bitcast(F32R), xqk_full[:], xqk_hi[:],
                                                ALU.subtract).then_inc(xqk_lo_done, 1)
                        after_alone(pool, xqk_lo_done, b)
                        after_alone(pool, xpv_in, b - 2, 4, 3)
                        for c, ks in enumerate((xqk_hi, xqk_lo, xqk_hi)):
                            pool.dma_start(XK3[side][32 * c:32 * c + 32, :, :], ks[:, 1, :]).then_inc(xk_placed, 16)
                    elif name == "x3T":
                        after(pool, x3T_now_done, b)
                        nc.gpsimd.tensor_copy(x3T[:, :, bass.ds(b * T, T)], x3T_now[:]).then_inc(x3T_kept, 1)
                    elif name == "gates" and n == 5:
                        after(pool, gate_steps, b, GATE_STEPS, GATE_STEPS - 1)
                        after(pool, gT_in, b - 1)
                        nc.gpsimd.tensor_tensor(root_gates[:], gates[:], exponents[:, 0:E], ALU.pow).then_inc(root_done, 1)

        @block.scalar
        def _(act):
            nc.scalar.preload_act_table(ACT.Exp)
            for turn in turns(act):
                for name, n in turn.steps():
                    b, side = turn.batch(STAGE_OF[name]), turn.side(STAGE_OF[name])
                    if name == "xT":
                        after(act, xT_in, b)
                        after(act, v_in, b - 1)
                        nc.scalar.copy(xnT[:], A[:, 0:2 * T].rearrange("p (c t) -> p c t", c=2)).then_inc(xnT_done, 1)
                    elif name == "qk":
                        after(act, qk_full_done, b)
                        after(act, qk_lo_done, b - 1)
                        after(act, q_placed, b - 1, 6, 5, 16)
                        after(act, k_placed, b - 1, 6, 5, 16)
                        nc.scalar.copy(qk_hi[:].bitcast(F32R), qk_full[:]).then_inc(qk_hi_done, 1)
                    elif name == "v":
                        after(act, v_in, b)
                        after(act, pv_in, b - 2)
                        act.wait_ge(consts_set, 1)
                        nc.scalar.copy(V1[side][:, :, 0:HD], A[:, 0:D].rearrange("p (h d) -> p h d", h=H)).then_inc(v_done, 1)
                    elif name == "mT":
                        after(act, mT_in, b)
                        after(act, max_placed, b - 1, 2, 1, 16)
                        nc.scalar.copy(max_hi[:].bitcast(F32R), Bk[0:H, 0:T]).then_inc(max_hi_done, 1)
                        after(act, max_hi_done, b)
                        act.dma_start(Q3[side][96:97], max_hi[:]).then_inc(max_placed, 16)
                        after(act, max_lo_done, b)
                        act.dma_start(Q3[side][97:98], max_lo[:]).then_inc(max_placed, 16)
                    elif name == "p2":
                        slot, k = ring(turn, EXPS, name, n)
                        act.wait_ge(exps_in, k)
                        if n == 0:
                            after(act, pv_in, b - 1)
                        nc.scalar.activation(probs[:, 4 * n:4 * n + 4, :], exp_ring[slot][:]
                                             .rearrange("p (h t) -> p h t", h=4), ACT.Exp, scale=SCALE).then_inc(exps_done, 1)
                    elif name == "x2c":
                        g, kt, pair = n // 4, n // 2 % 2, n % 2
                        slot, k = ring(turn, EXPS, name, n)
                        act.wait_ge(exps_in, k)
                        if n % 4 == 0:
                            after(act, xpv_in, b - 1, 4, g)
                        h = 4 * g + 2 * pair
                        nc.scalar.activation(xprobs[:, kt, h:h + 2, :], exp_ring[slot][:]
                                             .rearrange("p (h t) -> p h t", h=2), ACT.Exp, scale=XSCALE).then_inc(exps_done, 1)
                    elif name == "pv":
                        after(act, pv_in, b)
                        after(act, norm_in, b - 1)
                        nc.scalar.copy(pv_sb[:], pv_bank[0][:].rearrange("p (g t) -> p g t", g=4)).then_inc(pv_copied, 1)
                    elif name == "xpv" and n % 2:
                        after(act, xpv_in, b, 4, n)
                        after(act, xnorm_in, b - 1, 2, 1)
                        nc.scalar.copy(xpv_sb[:, n - 1:n + 1, :], pv_bank[n // 2][:].rearrange("p (g t) -> p g t", g=2))\
                          .then_inc(xpv_copied, 1)
                    elif name == "xqk":
                        after(act, xqk_full_done, b)
                        after(act, xqk_lo_done, b - 1)
                        after(act, xq_placed, b - 1, 12, 11, 16)
                        after(act, xk_placed, b - 1, 3, 2, 16)
                        nc.scalar.copy(xqk_hi[:].bitcast(F32R), xqk_full[:]).then_inc(xqk_hi_done, 1)
                    elif name == "xmT":
                        after(act, xmT_in, b)
                        after(act, xmax_placed, b - 1, 2, 1, 16)
                        nc.scalar.copy(xmax_hi[:].bitcast(F32R), Bk[0:H, 0:D]).then_inc(xmax_hi_done, 1)
                        after(act, xmax_hi_done, b)
                        act.dma_start(XQ3[side][96:97], xmax_hi[:]).then_inc(xmax_placed, 16)
                        after(act, xmax_lo_done, b)
                        act.dma_start(XQ3[side][97:98], xmax_lo[:]).then_inc(xmax_placed, 16)
                    elif name == "xattnT":
                        after(act, xattnT_in, b)
                        after(act, y_in, b - 1)
                        nc.scalar.activation(xattnT[:], A[:, 0:D], ACT.Identity, bias=xvb_sb[:, 0:1]).then_inc(xattnT_done, 1)
                    elif name == "xv":
                        after(act, xv_in, b)
                        after(act, xpv_in, b - 2, 4, 3)
                        nc.scalar.copy(XV1[side][:, :, :, 0:XH], A[:, 0:D].rearrange("p (k h d) -> p k h d", k=NX, h=H))\
                          .then_inc(xv_done, 1)
                    elif name == "x3T":
                        after(act, x3T_in, b)
                        after(act, x3T_kept, b - 1)
                        after(act, logits_in, b - 1)
                        nc.scalar.copy(x3T_now[:], A[:, 0:2 * T].rearrange("p (c t) -> p c t", c=2)).then_inc(x3T_now_done, 1)
                    elif name == "logits":
                        after(act, logits_done, b)
                        nc.scalar.activation(neg_exp[:], logits[:], ACT.Exp, scale=-1.0).then_inc(neg_exp_done, 1)
                    elif name == "gT":
                        after(act, gT_in, b)
                        after(act, gates_stored, b - 1, 1, 0, 16)
                        nc.scalar.copy(gatesT[:], A[0:E, 0:T]).then_inc(gatesT_done, 1)

            def squares(it):
                for u in range(4):
                    act.wait_ge(act1_done, it * 4 + u + 1)
                    if not (isinstance(it, int) and it == 0):
                        act.wait_ge(expert_added, it * 4 + u - 3)
                    nc.scalar.activation(act2[u], act1[u], ACT.Square).then_inc(act2_done, 1)

            squares(0)
            with act.Fori(1, NE) as it:
                squares(it)


        @block.vector
        def _(dve):
            nc.vector.memset(zeros[:], 0.0)
            for i in range(2):
                nc.vector.memset(Q3[i][:], 0.0)
                nc.vector.memset(XQ3[i][:], 0.0)
                nc.vector.memset(K3[i][96:98], 1.0)
                nc.vector.memset(XK3[i][96:98], 1.0)
                nc.vector.memset(V1[i][:], 0.0)
                nc.vector.memset(XV1[i][:], 0.0)
            for c in range(4):
                nc.vector.memset(group_w[:, c:c + 1], 9.0 - c)
            nc.vector.memset(masked[:, 0:1], 9.0)
            nc.vector.memset(masked[:, 1:2], 8.0).then_inc(cleared, 1)
            dve.wait_ge(cleared, 1)
            for i in range(2):
                nc.vector.memset(V1[i][:, :, HD:HD + 1], 1.0)
                last = nc.vector.memset(XV1[i][:, :, :, XH:XH + 1], 1.0)
            last.then_inc(consts_set, 1)

            def norm_stats(i, b):
                after_alone(dve, st_done[i], b - 1)
                nc.vector.bn_stats(stats[i][:], xres[:, b, :]).then_inc(st_done[i], 1)
                after_alone(dve, st_done[i], b)
                nc.vector.bn_aggr(mean_var[i][:], stats[i][:]).then_inc(mv_done[i], 1)

            def norm_rows(i, b):
                after(dve, rstd_done[i], b)
                nc.vector.tensor_scalar(xn[i][:], xres[:, b, :], mean_var[i][:, 0:1], rstd[i][:], ALU.subtract,
                                        ALU.mult).then_inc(xn_done[i], 1)

            def choose_experts(b, part):
                taken = [GATE_PARTS[part]]

                def step(ins, alone=False):
                    taken[0] += 1
                    ins.then_inc(gate_steps, 1)
                    (after_alone if alone else after)(dve, gate_steps, b, GATE_STEPS, taken[0] - 1)

                if part == 0:
                    after(dve, neg_exp_done, b)
                    step(nc.vector.tensor_scalar(one_plus[:], neg_exp[:], 1.0, None, ALU.add))
                    step(nc.vector.reciprocal(sig[:], one_plus[:]))
                    sg = sig[:].rearrange("p (g a c) -> p g a c", g=8, a=2)
                    nc.vector.tensor_tensor(pair_max[:], sg[:, :, :, 0], sg[:, :, :, 1], ALU.max).then_inc(gate_steps, 1)
                    nc.vector.tensor_tensor(pair_min[:], sg[:, :, :, 0], sg[:, :, :, 1], ALU.min).then_inc(gate_steps, 1)
                    taken[0] += 2
                elif part == 1:
                    after(dve, gate_steps, b, GATE_STEPS, 3)
                    nc.vector.tensor_tensor(top1[:], pair_max[:, :, 0], pair_max[:, :, 1], ALU.max).then_inc(gate_steps, 1)
                    nc.vector.tensor_tensor(top2a[:], pair_max[:, :, 0], pair_max[:, :, 1], ALU.min).then_inc(gate_steps, 1)
                    taken[0] += 2
                    step(nc.vector.tensor_tensor(top2b[:], pair_min[:, :, 0], pair_min[:, :, 1], ALU.max))
                    nc.vector.tensor_tensor(top2[:], top2a[:], top2b[:], ALU.max).then_inc(gate_steps, 1)
                    taken[0] += 1
                elif part == 2:
                    after(dve, gate_steps, b, GATE_STEPS, 7)
                    step(nc.vector.tensor_tensor(group_w[:, 4:12], top1[:], top2[:], ALU.add), alone=True)
                    step(nc.vector.max(top_groups[:], group_w[:]), alone=True)
                    nc.vector.match_replace(groups_marked[:], top_groups[:], group_w[:], -1.0).then_inc(gate_steps, 1)
                    taken[0] += 1
                elif part == 3:
                    after(dve, gate_steps, b, GATE_STEPS, 10)
                    step(nc.vector.scalar_tensor_tensor(
                        out=masked[:, 2:2 + E].rearrange("p (g a) -> p g a", g=8),
                        in0=groups_marked[:, 4:12].unsqueeze(2).to_broadcast([P, 8, 4]), scalar=-1.0,
                        in1=sig[:].rearrange("p (g a) -> p g a", g=8), op0=ALU.is_equal, op1=ALU.mult), alone=True)
                    step(nc.vector.max(top_experts[:], masked[:]), alone=True)
                    nc.vector.match_replace(experts_marked[:], top_experts[:], masked[:], -1.0).then_inc(gate_steps, 1)
                    taken[0] += 1
                elif part == 4:
                    after(dve, gate_steps, b, GATE_STEPS, 13)
                    step(nc.vector.scalar_tensor_tensor(out=chosen[:], in0=experts_marked[:, 2:2 + E], scalar=-1.0,
                                                        in1=sig[:], op0=ALU.is_equal, op1=ALU.mult))
                    nc.vector.tensor_reduce(total[:], chosen[:], AX.X, ALU.add).then_inc(gate_steps, 1)
                    taken[0] += 1
                else:
                    after(dve, gate_steps, b, GATE_STEPS, 15)
                    step(nc.vector.tensor_scalar(total_eps[:], total[:], 1e-20, None, ALU.add))
                    step(nc.vector.reciprocal(inv_total[:], total_eps[:]))
                    after(dve, root_done, b - 1)
                    nc.vector.tensor_scalar(gates[:], chosen[:], inv_total[:], ROUTED_SCALE, ALU.mult,
                                            ALU.mult).then_inc(gate_steps, 1)
                    taken[0] += 1
                assert taken[0] == (GATE_PARTS + (GATE_STEPS,))[part + 1]

            for turn in turns(dve):
                for name, n in turn.steps():
                    b, side = turn.batch(STAGE_OF[name]), turn.side(STAGE_OF[name])
                    if name in ("ln1a", "ln2a", "ln3a"):
                        if name == "ln1a" and isinstance(b, int):
                            dve.wait_ge(loaded_x, 32)
                            if b > 0:
                                dve.wait_ge(loaded_w, 12 * 16)
                        if name == "ln2a":
                            after_alone(dve, x1_done, b)
                        if name == "ln3a":
                            after_alone(dve, x2_done, b)
                        norm_stats(int(name[2]) - 1, b)
                    elif name in ("ln1b", "ln2b", "ln3b"):
                        after(dve, {"ln1b": xT_in, "ln2b": xqk_in, "ln3b": x3T_in}[name], b - 1)
                        norm_rows(int(name[2]) - 1, b)
                    elif name == "qk":
                        if isinstance(b, int):
                            dve.wait_ge(loaded_w, 12 * 16)
                        after(dve, qk_in, b)
                        after(dve, qk_lo_done, b - 1)
                        nc.vector.tensor_tensor(qk_full[:], Bk[:].rearrange("p (c t) -> p c t", c=4),
                                                qkb_sb[:].unsqueeze(2).to_broadcast([P, 4, T]), ALU.add).then_inc(qk_full_done, 1)
                    elif name in SCORES:
                        slot, k = ring(turn, SCORES, name, n)
                        dve.wait_ge(scores_in, k)
                        if name == "p1":
                            if n == 0:
                                after(dve, mT_in, b - 1)
                            to = negmax[:, 4 * n:4 * n + 4]
                        else:
                            if n == 0:
                                after(dve, xmT_in, b - 1)
                            to = xnegmax[:, :, n]
                        c = 4 if name == "p1" else NX
                        nc.vector.tensor_reduce(to, score_ring[slot][:].rearrange("p (c t) -> p c t", c=c), AX.X, ALU.max,
                                                negate=True).then_inc(scores_max, 1)
                    elif name == "mT":
                        after(dve, max_hi_done, b)
                        after(dve, max_placed, b - 1, 2, 1, 16)
                        nc.vector.tensor_tensor(max_lo[:].bitcast(F32R), Bk[0:H, 0:T], max_hi[:], ALU.subtract)\
                          .then_inc(max_lo_done, 1)
                    elif name == "norm":
                        after(dve, norm_in, b)
                        a = A[:].rearrange("p (h c) -> p h c", h=H)
                        after(dve, attn_done, b - 1)
                        nc.vector.reciprocal(rsum[:].unsqueeze(2), a[:, :, HD:HD + 1]).then_inc(rsum_done, 1)
                        after(dve, rsum_done, b)
                        after(dve, attnT_in, b - 1)
                        nc.vector.tensor_tensor(attn[:].rearrange("p (h d) -> p h d", h=H), a[:, :, 0:HD],
                                                rsum[:].unsqueeze(2).to_broadcast([P, H, HD]), ALU.mult).then_inc(attn_done, 1)
                    elif name == "attnT":
                        after(dve, attnT_in, b)
                        after(dve, wo_in, b - 1)
                        nc.vector.tensor_tensor(attnT[:], Bk[:, 0:D].rearrange("p (c t) -> p c t", c=2),
                                                vb_sb[:].unsqueeze(2).to_broadcast([P, 2, T]), ALU.add).then_inc(attnT_done, 1)
                    elif name == "wo":
                        after(dve, wo_in, b)
                        after(dve, x_bo_done, b)
                        nc.vector.tensor_tensor(xres[:, b, :], A[:, 0:D], x_bo[:], ALU.add).then_inc(x1_done, 1)
                    elif name == "xqk":
                        after(dve, xqk_in, b)
                        after(dve, xqk_lo_done, b - 1)
                        nc.vector.tensor_tensor(xqk_full[:], Bk[:].rearrange("p (c t) -> p c t", c=2),
                                                xqkb_sb[:].unsqueeze(2).to_broadcast([P, 2, D]), ALU.add).then_inc(xqk_full_done, 1)
                    elif name == "xmT":
                        after(dve, xmax_hi_done, b)
                        after(dve, xmax_placed, b - 1, 2, 1, 16)
                        nc.vector.tensor_tensor(xmax_lo[:].bitcast(F32R), Bk[0:H, 0:D], xmax_hi[:], ALU.subtract)\
                          .then_inc(xmax_lo_done, 1)
                    elif name == "xnorm":
                        after(dve, xnorm_in, b, 2, n)
                        a = (A, Bk)[n][:].rearrange("p (h c) -> p h c", h=H)
                        after(dve, xattn_done, b - 1, 2, n)
                        nc.vector.reciprocal(xrsum[:, n, :].unsqueeze(2), a[:, :, XH:XH + 1]).then_inc(xrsum_done, 1)
                        after(dve, xrsum_done, b, 2, n)
                        after(dve, xattnT_in, b - 1)
                        nc.vector.tensor_tensor(xattn[:, n, :].rearrange("p (h d) -> p h d", h=H), a[:, :, 0:XH],
                                                xrsum[:, n, :].unsqueeze(2).to_broadcast([P, H, XH]), ALU.mult)\
                          .then_inc(xattn_done, 1)
                    elif name == "y":
                        after(dve, y_in, b)
                        nc.vector.scalar_tensor_tensor(out=xres[:, b, :], in0=Bk[:, 0:D], scalar=xbo_sb[:, 0:1],
                                                       in1=xres[:, b, :], op0=ALU.add, op1=ALU.add).then_inc(x2_done, 1)
                    elif name == "logits":
                        after(dve, logits_in, b)
                        after(dve, neg_exp_done, b - 1)
                        nc.vector.tensor_tensor(logits[:], Bk[:, 0:E], br_sb[:], ALU.add).then_inc(logits_done, 1)
                    elif name == "gates":
                        choose_experts(b, n)

            def gated_relus(it):
                for u in range(4):
                    side, blk = u // 2, u % 2
                    if blk == 0:
                        dve.wait_ge(groot_loaded[side], (it + 1) * 16)
                    dve.wait_ge(hidden_in, it * 4 + u + 1)
                    if not (isinstance(it, int) and it == 0):
                        dve.wait_ge(act2_done, it * 4 + u - 3)
                    nc.vector.scalar_tensor_tensor(out=act1[u], in0=bank[4 + u][:], scalar=0.0, in1=groot[side][:, blk, :],
                                                   op0=ALU.max, op1=ALU.mult).then_inc(act1_done, 1)

            def add_half(half):
                dve.wait_ge(half_in, half + 1)
                for t in range(8):
                    nc.vector.tensor_tensor(xres[:, 8 * half + t, :], bank[t // 2][:, (t % 2) * D:(t % 2 + 1) * D],
                                            xres[:, 8 * half + t, :], ALU.add).then_inc(half_added, 1)

            gated_relus(0)
            with dve.Fori(1, NE // 2) as it:
                gated_relus(it)
            add_half(0)
            with dve.Fori(NE // 2, NE) as it:
                gated_relus(it)
            add_half(1)

        @block.tensor
        def _(pe):
            def r(ap):
                return ap.bitcast(F32R)

            def ring_slot(turn, kinds, name, n, read):
                slot, k = ring(turn, kinds, name, n)
                if not isinstance(k, int) or k > 2:
                    pe.wait_ge(read, k - 2)
                return slot

            pe.wait_ge(loaded_x, 32)
            pe.wait_ge(loaded_w, 12 * 16)
            pe.wait_ge(consts_set, 1)
            for turn in turns(pe):
                for name, n in turn.steps():
                    b, side = turn.batch(STAGE_OF[name]), turn.side(STAGE_OF[name])
                    if name == "p1":
                        if n == 0:
                            after(pe, q_placed, b, 6, 5, 16)
                            after(pe, k_placed, b, 6, 5, 16)
                        slot = ring_slot(turn, SCORES, name, n, scores_max)
                        for i in range(4):
                            h = 4 * n + i
                            mm = pe.matmul(score_ring[slot][:, i * T:(i + 1) * T], r(Q3[side][0:96, h // 2, h % 2, :]),
                                           r(K3[side][0:96, h // 2, :]), start=True, stop=True)
                        mm.then_inc(scores_in, 1)
                    elif name == "p2":
                        if n == 0:
                            after(pe, max_placed, b, 2, 1, 16)
                        slot = ring_slot(turn, EXPS, name, n, exps_done)
                        for i in range(2):
                            g = 2 * n + i
                            mm = pe.matmul(exp_ring[slot][:, i * 2 * T:(i + 1) * 2 * T], r(K3[side][:, g, :]),
                                           r(Q3[side][:, g, :, :]), start=True, stop=True)
                        mm.then_inc(exps_in, 1)
                    elif name == "x1c":
                        if n == 0:
                            after(pe, xq_placed, b, 12, 11, 16)
                            after(pe, xk_placed, b, 3, 2, 16)
                        slot = ring_slot(turn, SCORES, name, n, scores_max)
                        for qt in range(NX):
                            mm = pe.matmul(score_ring[slot][:, qt * D:(qt + 1) * D],
                                           r(XQ3[side][0:96, n // 4, n % 4, qt * P:(qt + 1) * P]),
                                           r(XK3[side][0:96, n // 4, :]), start=True, stop=True)
                        mm.then_inc(scores_in, 1)
                    elif name == "x2c":
                        if n == 0:
                            after(pe, xmax_placed, b, 2, 1, 16)
                        g, kt, pair = n // 4, n // 2 % 2, n % 2
                        slot = ring_slot(turn, EXPS, name, n, exps_done)
                        pe.matmul(exp_ring[slot][:], r(XK3[side][:, g, kt * P:(kt + 1) * P]),
                                  r(XQ3[side][:, g, 2 * pair:2 * pair + 2, :]), start=True, stop=True).then_inc(exps_in, 1)
                    elif name == "xT":
                        after(pe, xn_done[0], b)
                        bank_free(pe, turn, A_USES, "xT")
                        for c in range(2):
                            mm = pe.transpose(A[:, c * T:(c + 1) * T], xn[0][:, c * P:(c + 1) * P], eye_sb[:])
                        mm.then_inc(xT_in, 1)
                    elif name == "qk":
                        after(pe, xnT_done, b)
                        bank_free(pe, turn, B_USES, "qk")
                        for m in range(4):
                            for c in range(2):
                                mm = pe.matmul(Bk[:, m * T:(m + 1) * T], wqkv_sb[:, c, m, :], xnT[:, c, :],
                                               start=(c == 0), stop=(c == 1))
                        mm.then_inc(qk_in, 1)
                    elif name == "v":
                        bank_free(pe, turn, A_USES, "v")
                        for c in range(2):
                            mm = pe.matmul(A[:, 0:D], xnT[:, c, :], wqkv_sb[:, c, 4:6, :], start=(c == 0), stop=(c == 1))
                        mm.then_inc(v_in, 1)
                    elif name == "mT":
                        pe.wait_ge(scores_max, ring(turn, SCORES, "p1", 3)[1])
                        bank_free(pe, turn, B_USES, "mT")
                        pe.transpose(Bk[0:H, 0:T], negmax[:], eye_sb[:]).then_inc(mT_in, 1)
                    elif name == "pv":
                        pe.wait_ge(exps_done, ring(turn, EXPS, "p2", 3)[1])
                        after(pe, v_done, b)
                        after(pe, pv_copied, b - 1)
                        if turn.has("X2"):
                            after(pe, xpv_copied, turn.batch("X2"), 2, 0)
                        else:
                            after(pe, xpv_copied, min(turn.batch("X2"), B - 1), 2, 0)
                        for g in range(4):
                            for j in range(4):
                                h = 4 * g + j
                                mm = pe.matmul(pv_bank[0][32 * j:32 * j + 32, g * T:(g + 1) * T], V1[side][:, h, :],
                                               probs[:, h, :], start=True, stop=True)
                        mm.then_inc(pv_in, 1)
                    elif name == "norm":
                        after(pe, pv_copied, b)
                        bank_free(pe, turn, A_USES, "norm")
                        for g in range(4):
                            mm = pe.transpose(A[:, g * P:(g + 1) * P], pv_sb[:, g, :], eye_sb[:])
                        mm.then_inc(norm_in, 1)
                    elif name == "attnT":
                        after(pe, attn_done, b)
                        bank_free(pe, turn, B_USES, "attnT")
                        for c in range(2):
                            mm = pe.transpose(Bk[:, c * T:(c + 1) * T], attn[:, c * P:(c + 1) * P], eye_sb[:])
                        mm.then_inc(attnT_in, 1)
                    elif name == "wo":
                        after(pe, attnT_done, b)
                        bank_free(pe, turn, A_USES, "wo")
                        for c in range(2):
                            mm = pe.matmul(A[:, 0:D], attnT[:, c, :], wo_sb[:, c, :], start=(c == 0), stop=(c == 1))
                        mm.then_inc(wo_in, 1)
                    elif name == "xqk":
                        after(pe, xn_done[1], b)
                        pe.wait_ge(loaded_ctx[side], (turn.earlier_on_side("SB") + 1) * 16)
                        bank_free(pe, turn, B_USES, "xqk")
                        pe.matmul(Bk[:, 0:D], xw_sb[:, 0, :], xn[1][:], start=True, stop=True)
                        pe.matmul(Bk[:, D:2 * D], xw_sb[:, 1, :], ctx_sb[side][:], start=True, stop=True).then_inc(xqk_in, 1)
                    elif name == "xv":
                        bank_free(pe, turn, A_USES, "xv")
                        for kt in range(NX):
                            mm = pe.matmul(A[:, kt * P:(kt + 1) * P], ctx_sb[side][:, kt * P:(kt + 1) * P], xw_sb[:, 2, :],
                                           start=True, stop=True)
                        mm.then_inc(xv_in, 1)
                    elif name == "xmT":
                        pe.wait_ge(scores_max, ring(turn, SCORES, "x1c", 15)[1])
                        bank_free(pe, turn, B_USES, "xmT")
                        for qt in range(NX):
                            mm = pe.transpose(Bk[0:H, qt * P:(qt + 1) * P], xnegmax[:, qt, :], eye_sb[:])
                        mm.then_inc(xmT_in, 1)
                    elif name == "xpv":
                        pe.wait_ge(exps_done, ring(turn, EXPS, "x2c", 4 * n + 3)[1])
                        if n == 0:
                            after(pe, xv_done, b)
                            if not isinstance(b, int) or 0 <= turn.batch("SB", 1) < B:
                                after(pe, pv_copied, turn.batch("SB", 1))
                            after(pe, xpv_copied, b - 1, 2, 0)
                        if n == 2:
                            after(pe, xpv_copied, b - 1, 2, 1)
                        for kt in range(NX):
                            for j in range(4):
                                h = 4 * n + j
                                mm = pe.matmul(pv_bank[n // 2][32 * j:32 * j + 32, (n % 2) * D:(n % 2 + 1) * D],
                                               XV1[side][:, kt, h, :], xprobs[:, kt, h, :], start=(kt == 0), stop=(kt == NX - 1))
                        mm.then_inc(xpv_in, 1)
                    elif name == "xnorm":
                        if n == 0:
                            after(pe, xpv_copied, b, 2, 1)
                        bank_free(pe, turn, (A_USES, B_USES)[n], f"xnorm{n}")
                        for g in range(4):
                            mm = pe.transpose((A, Bk)[n][:, g * P:(g + 1) * P], xpv_sb[:, g, n * P:(n + 1) * P], eye_sb[:])
                        mm.then_inc(xnorm_in, 1)
                    elif name == "xattnT":
                        after(pe, xattn_done, b, 2, 1)
                        bank_free(pe, turn, A_USES, "xattnT")
                        for qt in range(NX):
                            mm = pe.transpose(A[:, qt * P:(qt + 1) * P], xattn[:, qt, :], eye_sb[:])
                        mm.then_inc(xattnT_in, 1)
                    elif name == "y":
                        after(pe, xattnT_done, b)
                        bank_free(pe, turn, B_USES, "y")
                        pe.matmul(Bk[:, 0:D], xw_sb[:, 3, :], xattnT[:], start=True, stop=True).then_inc(y_in, 1)
                    elif name == "x3T":
                        after(pe, xn_done[2], b)
                        bank_free(pe, turn, A_USES, "x3T")
                        for c in range(2):
                            mm = pe.transpose(A[:, c * T:(c + 1) * T], xn[2][:, c * P:(c + 1) * P], eye_sb[:])
                        mm.then_inc(x3T_in, 1)
                    elif name == "logits":
                        after(pe, x3T_now_done, b)
                        bank_free(pe, turn, B_USES, "logits")
                        for c in range(2):
                            mm = pe.matmul(Bk[:, 0:E], x3T_now[:, c, :], wr_sb[:, c, :], start=(c == 0), stop=(c == 1))
                        mm.then_inc(logits_in, 1)
                    elif name == "gT":
                        after(pe, root_done, b)
                        bank_free(pe, turn, A_USES, "gT")
                        pe.transpose(A[0:E, 0:T], root_gates[:], eye_sb[:]).then_inc(gT_in, 1)

            pe.wait_ge(x2_done, B)
            pe.wait_ge(gatesT_done, B)
            pe.wait_ge(x3T_kept, B)

            def clear_half(half):
                if half:
                    pe.wait_ge(half_added, 8 * half)
                for i in range(4):
                    pe.matmul(bank[i][:], zeros[:, 0:P], zeros[:], start=True, stop=False, skip_group_check=True)

            def expert_pair(it, half):
                def hidden(u):
                    side, blk = u // 2, u % 2
                    if blk == 0:
                        pe.wait_ge(w_loaded[side], (it + 1) * 16)
                    if not (isinstance(it, int) and it == 0):
                        pe.wait_ge(act1_done, it * 4 + u - 3)
                    at = 1024 * half + 512 * blk
                    for c in range(2):
                        mm = pe.matmul(bank[4 + u][:], w_sb[side][:, c, :], x3T[:, c, at:at + 512], start=(c == 0), stop=(c == 1))
                    mm.then_inc(hidden_in, 1)

                def output(u):
                    side, blk = u // 2, u % 2
                    pe.wait_ge(act2_done, it * 4 + u + 1)
                    for t in range(4):
                        tile = 4 * blk + t
                        mm = pe.matmul(bank[tile // 2][:, (tile % 2) * D:(tile % 2 + 1) * D], act2[u][:, t * P:(t + 1) * P],
                                       w_sb[side][:, 2:4, :], start=False, stop=False, skip_group_check=True)
                    mm.then_inc(expert_added, 1)

                hidden(0)
                hidden(1)
                output(0)
                hidden(2)
                output(1)
                hidden(3)
                output(2)
                output(3)

            def close_half():
                for i in range(4):
                    mm = pe.matmul(bank[i][:], zeros[:, 0:P], zeros[:], start=False, stop=True, skip_group_check=True)
                mm.then_inc(half_in, 1)

            clear_half(0)
            expert_pair(0, 0)
            with pe.Fori(1, NE // 2) as it:
                expert_pair(it, 0)
            close_half()
            clear_half(1)
            with pe.Fori(NE // 2, NE) as it:
                expert_pair(it, 1)
            close_half()


def kernel(**inputs):
    import numpy as np
    import concourse.bacc as bacc
    from concourse.bass_utils import run_bass_kernel_spmd

    def f(name):
        return np.asarray(inputs[name])

    rows = np.arange(P)
    order = [(2 * (rows % 8) + odd) * 16 + rows // 8 for odd in range(2)]
    wq, wk, wv = f("L0_attn_wq"), f("L0_attn_wk"), f("L0_attn_wv")
    bq, bk = f("L0_attn_bq"), f("L0_attn_bk")
    cols = [wq[:, order[0]], wq[:, order[1]], wk[:, order[0]], wk[:, order[1]], wv[:, 0:P], wv[:, P:2 * P]]
    wqkv = np.stack(cols, axis=1).reshape(2, P, 6, P).transpose(1, 0, 2, 3)
    qk_bias = np.stack([bq[order[0]], bq[order[1]], bk[order[0]], bk[order[1]]], axis=1)
    xorder = (4 * (rows % 4) + rows // 32) * 8 + rows // 4 % 8
    xw = np.stack([f("L0_xattn_Wq")[xorder].T, f("L0_xattn_Wk")[xorder].T, f("L0_xattn_Wv").T, f("L0_xattn_Wo").T], axis=1)
    xqk_bias = np.stack([f("L0_xattn_bq")[xorder], f("L0_xattn_bk")[xorder]], axis=1)
    W1 = np.concatenate([f("L0_ffn_W1"), f("L0_ffn_Ws1").reshape(2, P, 256)])
    W2 = np.concatenate([f("L0_ffn_W2"), f("L0_ffn_Ws2").reshape(256, 2, P).transpose(1, 0, 2)])
    w1 = W1.transpose(0, 2, 1).reshape(-1, 2, P, P).transpose(0, 2, 1, 3)
    w2 = W2.transpose(0, 2, 1).reshape(-1, P, 2, P)
    arrays = {
        "x": f("x"), "ctx_in": f("ctx_2048"), "wqkv": wqkv, "qk_bias": qk_bias,
        "v_bias": f("L0_attn_bv").reshape(2, P).T,
        "wo": f("L0_attn_wo").reshape(2, P, 256).transpose(1, 0, 2),
        "bo": np.broadcast_to(f("L0_attn_bo"), (P, 256)),
        "xw": xw, "xqk_bias": xqk_bias, "xv_bias": f("L0_xattn_bv")[:, None], "xbo": f("L0_xattn_bo")[:, None],
        "wr": f("L0_ffn_Wr").T.reshape(2, P, -1).transpose(1, 0, 2),
        "br": np.broadcast_to(f("L0_ffn_br"), (P, 32)),
        "experts": np.concatenate([w1, w2], axis=2), "eye": np.eye(P, dtype=np.float32),
    }
    arrays = {k: np.ascontiguousarray(v) for k, v in arrays.items()}
    nc = bacc.Bacc("TRN2", target_bir_lowering=False, num_devices=1)
    args = [nc.dram_tensor(k, v.shape, mybir.dt.from_np(v.dtype), kind="ExternalInput").ap() for k, v in arrays.items()]
    out = nc.dram_tensor("out", (16, P, 256), F32, kind="ExternalOutput").ap()
    gates_dram = nc.dram_tensor("gates_dram", (34, 16 * P), F32, kind="Internal").ap()
    decoder_layer(nc, *args, out, gates_dram)
    r = run_bass_kernel_spmd(nc, [arrays], core_ids=[0])
    return r.results[0]["out"]
```

```python
from contextlib import ExitStack

import concourse.bass as bass
from concourse import mybir

F32 = mybir.dt.float32
F32R = mybir.dt.float32r
BF16 = mybir.dt.bfloat16
ALU = mybir.AluOpType
ACT = mybir.ActivationFunctionType
AX = mybir.AxisListType

P = 128
EPS = 1e-5
ROUTED_SCALE = 2.5
FIRST, LAST = 4, 16
STAGES = ("SA", "SB", "X1", "X2", "R")

ORDER = {
    "PE": """
    xv, x2c 0, p1 0, p1 1, p1 2, p1 3, x2c 1, p1 4, p1 5, x2c 2, x3T, p1 6, p1 7, x2c 3,
    logits, xT, x2c 4, mT, xpv 0, x2c 5, x2c 6, qk 0, x2c 7, x1c 0, x1c 1, x2c 8, qk 1, x1c 2,
    xpv 1, p2 0, x1c 3, qk 2, x2c 9, x1c 4, x2c 10, x1c 5, qk 3, p2 1, p2 2, x1c 6, v, x1c 7,
    p2 3, pv 0, pv 1, x1c 8, x2c 11, pv 2, pv 3, x1c 9, x2c 12, x1c 10, norm, x2c 13, xpv 2, attnT,
    x2c 14, x1c 11, x2c 15, x1c 12, wo, xpv 3, x1c 13, x1c 14, xnorm 0, x1c 15, xnorm 1, xqk, xattnT, xmT,
    gT, y
    """,
    "DVE": """
    ln3s, ln1s, ln1a, ln3a, p1 0, p1 1, p1 2, p1 3, ln1b, ln3b, p1 4, p1 5, p1 6, p1 7,
    logits, gates 0, mT, gates 1, gates 2, gates 3, x1c 0, gates 4, x1c 1, gates 5, x1c 2, gates 6, gates 7, x1c 3,
    gates 8, x1c 4, gates 9, x1c 5, gates 10, qk, x1c 6, gates 11, gates 12, x1c 7, gates 13, x1c 8, gates 14, gates 15,
    x1c 9, x1c 10, rsum, norm, attnT, x1c 11, x1c 12, wo, ln2s, ln2a, x1c 13, x1c 14, xrsum 0, xnorm 0,
    xrsum 1, ln2b, xnorm 1, x1c 15, xqk, xmT, y
    """,
    "ACT": """
    x2c 0, x2c 1, xv, x2c 2, x3T, x2c 3, mT, logits, x2c 4, xT, x2c 5, x2c 6, x2c 7, x2c 8,
    xpv 1, p2 0, x2c 9, x2c 10, p2 1, p2 2, qk, v, p2 3, x2c 11, pv, x2c 12, x2c 13, x2c 14,
    x2c 15, xpv 3, xqk, xmT, xattnT, gT
    """,
    "Pool": """
    ln1a, ln3a, x3T, x_bo, qk, root 0, root 1, ln2a, root 2, root 3, xqk
    """,
    "SP": """
    max_rows, k_rows, q_rows, xmax_rows, xk_rows, xq_rows, gT, xv
    """,
}
ORDER = {engine: [s.strip() for s in text.replace("\n", " ").split(",")] for engine, text in ORDER.items()}
SCORES, EXPS = ("p1", "x1c"), ("p2", "x2c")
STEPS_OF = {
    "SA": "ln1s ln1a ln1b xT qk k_rows q_rows v",
    "SB": "p1 mT max_rows p2 x_bo pv rsum norm attnT wo ln2s ln2a ln2b xqk xk_rows xq_rows",
    "X1": "x1c xv xmT xmax_rows",
    "X2": "x2c xpv xrsum xnorm xattnT y",
    "R": "ln3s ln3a ln3b x3T logits gates root gT",
}
STAGE_OF = {name: stage for stage, names in STEPS_OF.items() for name in names.split()}


def decoder_layer(nc, x, ctx_in, wqkv, qk_bias, v_bias, wo, bo, xw, xqk_bias, xv_bias, xbo, wr, br, experts, eye,
                  out, gates_dram):
    B, T, D = x.shape
    H = 16
    HD = D // H
    XH = T // H
    E = wr.shape[2]
    NE = experts.shape[0]
    SCALE = float(D) ** -0.5
    XSCALE = float(T) ** -0.5
    NX = D // P
    assert T == P and D == 2 * P and 3 * 2 * HD == 96 and 3 * 4 * XH == 96 and NE % 2 == 0

    class Turn:

        def __init__(self, pair, parity):
            self.it = pair * 2 + parity
            self.pair = pair
            self.parity = parity

        def batch(self, stage, back=0):
            return self.it - (STAGES.index(stage) + back)

        def side(self, stage):
            return (self.parity + STAGES.index(stage)) % 2

        def earlier_on_side(self, stage):
            return self.pair + (self.parity - STAGES.index(stage)) // 2

        def has(self, stage):
            return not isinstance(self.it, int) or 0 <= self.batch(stage) < B

        def steps(self, engine):
            for s in ORDER[engine]:
                name, _, n = s.partition(" ")
                if self.has(STAGE_OF[name]):
                    yield name, int(n or 0)

    def turns(eng):
        for it in range(FIRST):
            yield Turn(it // 2, it % 2)
        with eng.Fori(FIRST // 2, LAST // 2) as pair:
            yield Turn(pair, 0)
            yield Turn(pair, 1)
        for it in range(LAST, B + len(STAGES) - 2):
            yield Turn(it // 2, it % 2)

    ROUTED = 6
    routing = Turn((B + len(STAGES) - 2) // 2, (B + len(STAGES) - 2) % 2)

    def ring(turn, kinds, step, n):
        def each(it):
            return sum(1 for s in ORDER["PE"] if s.split()[0] in kinds and 0 <= it - STAGES.index(STAGE_OF[s.split()[0]]) < B)
        if isinstance(turn.it, int):
            before = sum(each(it) for it in range(turn.it))
        else:
            before = (turn.it - FIRST) * each(FIRST) + sum(each(it) for it in range(FIRST))
        within = [s for s in turn.steps("PE") if s[0] in kinds].index((step, n))
        return within % 2, before + within + 1

    with ExitStack() as stack:
        def sb(name, shape, dt=F32):
            return stack.enter_context(nc.sbuf_tensor(name, shape, dt))

        def sem(name):
            return stack.enter_context(nc.semaphore(name))

        xres = sb("xres", [P, B, D])
        ctx_sb = [sb(f"ctx{i}", [P, D]) for i in range(2)]
        wqkv_sb = sb("wqkv_sb", [P, 2, 6, P])
        qkb_sb = sb("qkb_sb", [P, 4])
        vb_sb = sb("vb_sb", [P, 2])
        wo_sb = sb("wo_sb", [P, 2, D])
        bo_sb = sb("bo_sb", [P, D])
        xw_sb = sb("xw_sb", [P, 4, P])
        xqkb_sb = sb("xqkb_sb", [P, 2])
        xvb_sb = sb("xvb_sb", [P, 1])
        xbo_sb = sb("xbo_sb", [P, 1])
        wr_sb = sb("wr_sb", [P, 2, E])
        br_sb = sb("br_sb", [P, E])
        eye_sb = sb("eye_sb", [P, P])
        stats = [sb(f"stats{i}", [P, 6]) for i in range(3)]
        mean_var = [sb(f"mean_var{i}", [P, 2]) for i in range(3)]
        var_eps = [sb(f"var_eps{i}", [P, 1]) for i in range(3)]
        rstd = [sb(f"rstd{i}", [P, 1]) for i in range(3)]
        xn = [sb(f"xn{i}", [P, D]) for i in range(3)]
        exponents = sb("exponents", [P, E + 1])
        xnT = sb("xnT", [P, 2, T])
        qk_full = sb("qk_full", [P, 4, T])
        qk_hi = sb("qk_hi", [P, 4, T])
        qk_lo = sb("qk_lo", [P, 4, T])
        Q3 = [sb(f"Q3_{i}", [P, 8, 2, T]) for i in range(2)]
        K3 = [sb(f"K3_{i}", [P, 8, T]) for i in range(2)]
        V1 = [sb(f"V1_{i}", [P, H, 32]) for i in range(2)]
        negmax = sb("negmax", [P, H])
        max_hi = sb("max_hi", [H, T])
        max_lo = sb("max_lo", [H, T])
        probs = sb("probs", [P, H, T])
        pv_sb = sb("pv_sb", [P, 4, T])
        rsum = sb("rsum", [P, H])
        attn = sb("attn", [P, D])
        attnT = sb("attnT", [P, 2, T])
        x_bo = sb("x_bo", [P, D])
        xqk_full = sb("xqk_full", [P, 2, D])
        xqk_hi = sb("xqk_hi", [P, 2, D])
        xqk_lo = sb("xqk_lo", [P, 2, D])
        XQ3 = [sb(f"XQ3_{i}", [P, 4, 4, D]) for i in range(2)]
        XK3 = [sb(f"XK3_{i}", [P, 4, D]) for i in range(2)]
        XV1 = [sb(f"XV1_{i}", [P, NX, H, 32]) for i in range(2)]
        xnegmax = sb("xnegmax", [P, NX, H])
        xmax_hi = sb("xmax_hi", [H, D])
        xmax_lo = sb("xmax_lo", [H, D])
        xprobs = sb("xprobs", [P, NX, H, D])
        xpv_sb = sb("xpv_sb", [P, 4, D])
        xrsum = sb("xrsum", [P, NX, H])
        xattn = sb("xattn", [P, NX, P])
        xattnT = sb("xattnT", [P, D])
        x3T_now = sb("x3T_now", [P, 2, T])
        x3T = sb("x3T", [P, 2, B * T])
        logits = sb("logits", [P, E])
        neg_exp = sb("neg_exp", [P, E])
        one_plus = sb("one_plus", [P, E])
        sig = sb("sig", [P, E])
        pair_max = sb("pair_max", [P, 8, 2])
        pair_min = sb("pair_min", [P, 8, 2])
        top1 = sb("top1", [P, 8])
        top2a = sb("top2a", [P, 8])
        top2b = sb("top2b", [P, 8])
        top2 = sb("top2", [P, 8])
        group_w = sb("group_w", [P, 4 + 8])
        top_groups = sb("top_groups", [P, 8])
        groups_marked = sb("groups_marked", [P, 4 + 8])
        masked = sb("masked", [P, 2 + E])
        top_experts = sb("top_experts", [P, 8])
        experts_marked = sb("experts_marked", [P, 2 + E])
        chosen = sb("chosen", [P, E])
        total = sb("total", [P, 1])
        total_eps = sb("total_eps", [P, 1])
        inv_total = sb("inv_total", [P, 1])
        gates = sb("gates", [P, E])
        root_gates = sb("root_gates", [P, E])
        gatesT = sb("gatesT", [E, T])
        w_sb = [sb(f"w_sb{i}", [P, 4, P]) for i in range(2)]
        groot = [probs[:, 8 * i:8 * i + 8, :].rearrange("p (a h) t -> p a (h t)", a=2) for i in range(2)]
        act1, act2 = [[xprobs[:, k, 2 * i:2 * i + 2, :].rearrange("p a t -> p (a t)") for i in range(4)] for k in range(2)]
        act2_hi = [K3[i // 2][:, i % 2 * 4:i % 2 * 4 + 4, :].rearrange("p a t -> p (a t)") for i in range(4)]
        act2_lo = [XK3[i // 2][:, i % 2 * 2:i % 2 * 2 + 2, :].rearrange("p a t -> p (a t)") for i in range(4)]
        w_hi, w_lo = [[Q3[i][:, 2 * k:2 * k + 2].rearrange("p a b t -> p (a b) t") for i in range(2)] for k in range(2)]
        x3_hi, x3_lo = [XQ3[i][:].rearrange("p a b d -> p (a b d)").rearrange("p (c t) -> p c t", c=2) for i in range(2)]
        zeros = sb("zeros", [P, 512], BF16)
        ones = sb("ones", [64, (NE - E) * B * T // 64])

        bank = [stack.enter_context(nc.psum_tensor(f"bank{i}", [P, 512], F32)) for i in range(8)]
        score_ring, exp_ring, pv_bank, A, Bk = bank[0:2], bank[2:4], bank[4:6], bank[6], bank[7]

        loaded_rest = sem("loaded_rest")
        loaded_w, loaded_x, loaded_ctx = sem("loaded_w"), sem("loaded_x"), [sem("loaded_ctx0"), sem("loaded_ctx1")]
        cleared, consts_set, pool_consts = sem("cleared"), sem("consts_set"), sem("pool_consts")
        st_done = [sem(f"stats{i}_done") for i in range(3)]
        mv_done = [sem(f"mean_var{i}_done") for i in range(3)]
        ve_done = [sem(f"var_eps{i}_done") for i in range(3)]
        rstd_done = [sem(f"rstd{i}_done") for i in range(3)]
        xn_done = [sem(f"xn{i}_done") for i in range(3)]
        scores_in, scores_max = sem("scores_in"), sem("scores_max")
        exps_in, exps_done = sem("exps_in"), sem("exps_done")
        xT_in, xnT_done = sem("xT_in"), sem("xnT_done")
        qk_in, qk_full_done, qk_hi_done, qk_lo_done = sem("qk_in"), sem("qk_full_done"), sem("qk_hi_done"), sem("qk_lo_done")
        q_placed, k_placed = sem("q_placed"), sem("k_placed")
        v_in, v_done = sem("v_in"), sem("v_done")
        mT_in, max_hi_done, max_lo_done, max_placed = sem("mT_in"), sem("max_hi_done"), sem("max_lo_done"), sem("max_placed")
        pv_in, pv_copied, norm_in = sem("pv_in"), sem("pv_copied"), sem("norm_in")
        rsum_done, attn_done, attnT_in, attnT_done = sem("rsum_done"), sem("attn_done"), sem("attnT_in"), sem("attnT_done")
        wo_in, x_bo_done, x1_done = sem("wo_in"), sem("x_bo_done"), sem("x1_done")
        xqk_in, xqk_full_done, xqk_hi_done, xqk_lo_done = sem("xqk_in"), sem("xqk_full_done"), sem("xqk_hi_done"), sem("xqk_lo_done")
        xq_placed, xk_placed = sem("xq_placed"), sem("xk_placed")
        xmT_in, xmax_hi_done, xmax_lo_done, xmax_placed = sem("xmT_in"), sem("xmax_hi_done"), sem("xmax_lo_done"), sem("xmax_placed")
        xv_in, xv_done = sem("xv_in"), sem("xv_done")
        xpv_in = sem("xpv_in")
        xpv_copied = sem("xpv_copied")
        xnorm_in, xrsum_done, xattn_done = sem("xnorm_in"), sem("xrsum_done"), sem("xattn_done")
        xattnT_in, xattnT_done, y_in, x2_done = sem("xattnT_in"), sem("xattnT_done"), sem("y_in"), sem("x2_done")
        x3T_in, x3T_now_done, x3T_kept = sem("x3T_in"), sem("x3T_now_done"), sem("x3T_kept")
        logits_in, logits_done, neg_exp_done = sem("logits_in"), sem("logits_done"), sem("neg_exp_done")
        gate_steps = sem("gate_steps")
        root_done, gT_in, gatesT_done, gates_stored = sem("root_done"), sem("gT_in"), sem("gatesT_done"), sem("gates_stored")
        GATE_PARTS = (0, 1, 2, 4) + tuple(range(7, 20))
        GATE_STEPS, ROOT_STEPS = GATE_PARTS[-1], 4
        ones_stored = sem("ones_stored")
        passed = sem("passed")
        w_loaded = [sem("w_loaded0"), sem("w_loaded1")]
        groot_loaded = [sem("groot_loaded0"), sem("groot_loaded1")]
        w1_hi_done, w2_hi_done = sem("w1_hi_done"), sem("w2_hi_done")
        w1_split, w2_split = sem("w1_split"), sem("w2_split")
        x3_hi_done, x3_split = sem("x3_hi_done"), sem("x3_split")
        hidden_in, act1_done, act2_done, expert_added = sem("hidden_in"), sem("act1_done"), sem("act2_done"), sem("expert_added")
        act2_hi_done, act2_split = sem("act2_hi_done"), sem("act2_split")
        half_in, half_added, out_stored = sem("half_in"), sem("half_added"), sem("out_stored")

        def after(eng, s, batch, n=1, k=0, by=1):
            if isinstance(batch, int) and batch < 0:
                return
            eng.wait_ge(s, (batch * n + k + 1) * by)

        def after_alone(eng, s, batch, n=1, k=0, by=1):
            if isinstance(batch, int):
                after(eng, s, batch, n, k, by)
            else:
                after(eng, s, batch, n, k, by)
                eng.sem_inc(passed, 1)

        A_USES = [("x3T", x3T_now_done, 1, 0), ("xT", xnT_done, 1, 0), ("v", v_done, 1, 0),
                  ("norm", attn_done, 1, 0), ("wo", x1_done, 1, 0), ("xnorm0", xattn_done, 2, 0), ("gT", gatesT_done, 1, 0),
                  ("xattnT", xattnT_done, 1, 0), ("xv", xv_done, 1, 0)]
        B_USES = [("mT", max_lo_done, 1, 0), ("logits", logits_done, 1, 0), ("qk", qk_full_done, 1, 0),
                  ("attnT", attnT_done, 1, 0), ("xnorm1", xattn_done, 2, 1), ("xqk", xqk_full_done, 1, 0),
                  ("xmT", xmax_lo_done, 1, 0), ("y", x2_done, 1, 0)]
        used = [s.replace("xnorm ", "xnorm") for s in ORDER["PE"]]
        for uses in (A_USES, B_USES):
            uses.sort(key=lambda use: next(i for i, s in enumerate(used) if s.split()[0] == use[0]))

        def bank_free(eng, turn, uses, name):
            at = [u[0] for u in uses].index(name)
            order = [(u, 0) for u in reversed(uses[:at])] + [(u, 1) for u in reversed(uses)]
            for (use, s, n, k), back in order:
                b = turn.batch(STAGE_OF[use.rstrip("01")], back)
                if not isinstance(b, int) or 0 <= b < B:
                    after(eng, s, b, n, k)
                    return

        block = stack.enter_context(nc.Block())

        @block.sync
        def _(sp):
            for dst, src in ((xres[:, 0, :], x[0]), (eye_sb[:], eye)):
                sp.dma_start(dst, src).then_inc(loaded_x, 16)
            for dst, src in ((wqkv_sb[:], wqkv), (qkb_sb[:], qk_bias), (vb_sb[:], v_bias), (wo_sb[:], wo), (bo_sb[:], bo),
                             (xw_sb[:], xw), (xqkb_sb[:], xqk_bias), (xvb_sb[:], xv_bias), (xbo_sb[:], xbo), (wr_sb[:], wr),
                             (br_sb[:], br)):
                sp.dma_start(dst, src).then_inc(loaded_w, 16)
            sp.dma_start(xres[:, 1:B, :], x[1:B].rearrange("b t d -> t b d")).then_inc(loaded_rest, 16)
            for i in range(2):
                sp.dma_start(ctx_sb[i][:], ctx_in[i]).then_inc(loaded_ctx[i], 16)
            for i in range(2):
                sp.dma_start(w_sb[i][:], experts[i]).then_inc(w_loaded[i], 16)

            def step(turn, name, n=0):
                b, side = turn.batch(STAGE_OF[name]), turn.side(STAGE_OF[name])
                if name == "k_rows":
                    if isinstance(b, int) and b < 2:
                        sp.wait_ge(consts_set, b + 1)
                    after_alone(sp, qk_lo_done, b)
                    after_alone(sp, pv_in, b - 2)
                    for c, ks in enumerate((qk_hi, qk_lo, qk_hi)):
                        for odd in range(2):
                            r = 32 * c + 16 * odd
                            sp.dma_start(K3[side][r:r + 16, :, :], ks[:, 2 + odd, :]).then_inc(k_placed, 16)
                elif name == "q_rows":
                    for c, qs in enumerate((qk_hi, qk_hi, qk_lo)):
                        for odd in range(2):
                            r = 32 * c + 16 * odd
                            sp.dma_start(Q3[side][r:r + 16, :, odd, :], qs[:, odd, :]).then_inc(q_placed, 16)
                elif name == "max_rows":
                    after_alone(sp, max_hi_done, b)
                    sp.dma_start(Q3[side][96:97], max_hi[:]).then_inc(max_placed, 16)
                    after_alone(sp, max_lo_done, b)
                    sp.dma_start(Q3[side][97:98], max_lo[:]).then_inc(max_placed, 16)
                elif name == "xmax_rows":
                    after_alone(sp, xmax_hi_done, b)
                    sp.dma_start(XQ3[side][96:97], xmax_hi[:]).then_inc(xmax_placed, 16)
                    after_alone(sp, xmax_lo_done, b)
                    sp.dma_start(XQ3[side][97:98], xmax_lo[:]).then_inc(xmax_placed, 16)
                elif name == "xk_rows":
                    if isinstance(b, int) and b == 0:
                        sp.wait_ge(consts_set, 2)
                    after_alone(sp, xqk_lo_done, b)
                    after_alone(sp, xpv_in, b - 2, 4, 3)
                    for c, ks in enumerate((xqk_hi, xqk_lo, xqk_hi)):
                        sp.dma_start(XK3[side][32 * c:32 * c + 32, :, :], ks[:, 1, :]).then_inc(xk_placed, 16)
                elif name == "xq_rows":
                    for c, qs in enumerate((xqk_hi, xqk_hi, xqk_lo)):
                        for hh in range(4):
                            r = 32 * c + 8 * hh
                            sp.dma_start(XQ3[side][r:r + 8, :, hh, :],
                                         qs[32 * hh:32 * hh + 32, 0, :]).then_inc(xq_placed, 16)
                elif name == "xv" and not (isinstance(b, int) and b + 2 >= B):
                    after_alone(sp, xv_in, b)
                    sp.dma_start(ctx_sb[side][:], ctx_in[b + 2]).then_inc(loaded_ctx[side], 16)
                elif name == "gT":
                    after_alone(sp, gatesT_done, b)
                    sp.dma_start(gates_dram[0:E, bass.ds(b * T, T)], gatesT[:]).then_inc(gates_stored, 16)

            for turn in turns(sp):
                for name, n in turn.steps("SP"):
                    step(turn, name, n)

            def load_weights(j, it):
                for side in range(2):
                    sp.wait_ge(w2_split, it * 2 - 1 + side)
                    sp.sem_inc(passed, 1)
                    sp.dma_start(w_sb[side][:], experts[j * 2 + side]).then_inc(w_loaded[side], 16)

            def load_roots(j, half, it):
                for side in range(2):
                    if not (isinstance(it, int) and it == 0):
                        sp.wait_ge(act1_done, it * 4 - 2 + 2 * side)
                        sp.sem_inc(passed, 1)
                    row = gates_dram[bass.ds(j * 2 + side, 1), 1024 * half:1024 * half + 1024]
                    sp.dma_start(probs[:, 8 * side:8 * side + 8, :].rearrange("p h t -> p (h t)"),
                                 row.to_broadcast([P, 1024])).then_inc(groot_loaded[side], 16)

            def store(half):
                for i in range(8 * half, 8 * half + 8, 2):
                    sp.wait_ge(half_added, i + 2)
                    sp.dma_start(out[i:i + 2].rearrange("b t d -> t b d"), xres[:, i:i + 2, :]).then_inc(out_stored, 16)

            sp.wait_ge(gates_stored, (B - 1) * 16)
            sp.wait_ge(ones_stored, 16)
            sp.wait_ge(pv_in, B)
            load_roots(0, 0, 0)
            with sp.Fori(1, ROUTED + 1) as j:
                load_weights(j, j)
                load_roots(j, 0, j)
            step(routing, "gT")
            with sp.Fori(ROUTED + 1, NE // 2) as j:
                load_weights(j, j)
                load_roots(j, 0, j)
            sp.wait_ge(gates_stored, B * 16)
            with sp.Fori(0, 2) as j:
                load_weights(j, j + NE // 2)
                load_roots(j, 1, j + NE // 2)
            store(0)
            with sp.Fori(2, NE // 2) as j:
                load_weights(j, j + NE // 2)
                load_roots(j, 1, j + NE // 2)
            store(1)
            sp.wait_ge(out_stored, 16 * B // 2)

        @block.gpsimd
        def _(pool):
            nc.gpsimd.memset(exponents[:, 0:E], 0.5)
            nc.gpsimd.memset(exponents[:, E:E + 1], -0.5)
            nc.gpsimd.memset(ones[:], 1.0).then_inc(pool_consts, 1)
            pool.wait_ge(pool_consts, 1)
            pool.dma_start(gates_dram[E:NE, :].rearrange("e (a t) -> (e a) t", a=64 // (NE - E)), ones[:]).then_inc(ones_stored, 16)
            def step(turn, name, n=0):
                b, side = turn.batch(STAGE_OF[name]), turn.side(STAGE_OF[name])
                if name in ("ln1a", "ln2a", "ln3a"):
                    i = int(name[2]) - 1
                    after_alone(pool, mv_done[i], b)
                    nc.gpsimd.tensor_scalar(var_eps[i][:], mean_var[i][:, 1:2], EPS, None, ALU.add).then_inc(ve_done[i], 1)
                    after(pool, ve_done[i], b)
                    nc.gpsimd.tensor_tensor(rstd[i][:], var_eps[i][:], exponents[:, E:E + 1],
                                            ALU.pow).then_inc(rstd_done[i], 1)
                elif name == "qk":
                    after(pool, qk_hi_done, b)
                    after(pool, q_placed, b - 1, 6, 5, 16)
                    after(pool, k_placed, b - 1, 6, 5, 16)
                    nc.gpsimd.tensor_tensor(qk_lo[:].bitcast(F32R), qk_full[:], qk_hi[:], ALU.subtract).then_inc(qk_lo_done, 1)
                elif name == "x_bo":
                    if isinstance(b, int):
                        pool.wait_ge(loaded_w, 11 * 16)
                        if b > 0:
                            pool.wait_ge(loaded_rest, 16)
                    after(pool, x1_done, b - 1)
                    nc.gpsimd.tensor_tensor(x_bo[:], xres[:, b, :], bo_sb[:], ALU.add).then_inc(x_bo_done, 1)
                elif name == "xqk":
                    after(pool, xqk_hi_done, b)
                    after(pool, xq_placed, b - 1, 12, 11, 16)
                    after(pool, xk_placed, b - 1, 3, 2, 16)
                    nc.gpsimd.tensor_tensor(xqk_lo[:].bitcast(F32R), xqk_full[:], xqk_hi[:],
                                            ALU.subtract).then_inc(xqk_lo_done, 1)
                elif name == "x3T":
                    after(pool, x3T_now_done, b)
                    nc.gpsimd.tensor_copy(x3T[:, :, bass.ds(b * T, T)], x3T_now[:]).then_inc(x3T_kept, 1)
                elif name == "root":
                    if n == 0:
                        after(pool, gate_steps, b, GATE_STEPS, GATE_STEPS - 1)
                        after(pool, gT_in, b - 1)
                    at = slice(n * E // ROOT_STEPS, (n + 1) * E // ROOT_STEPS)
                    nc.gpsimd.tensor_tensor(root_gates[:, at], gates[:, at], exponents[:, at], ALU.pow).then_inc(root_done, 1)

            def split(it, roots=False):
                for side in range(2):
                    first = isinstance(it, int) and it == 0
                    e = 2 * it + side
                    for w, (hi_done, split_done) in enumerate(((w1_hi_done, w1_split), (w2_hi_done, w2_split))):
                        at = slice(2 * w, 2 * w + 2)
                        if w == 0:
                            pool.wait_ge(w_loaded[side], (it + 1) * 16)
                        if not first:
                            pool.wait_ge((hidden_in, expert_added)[w], 4 * it - 2 + 2 * side)
                            pool.sem_inc(passed, 1)
                        nc.gpsimd.tensor_copy(w_hi[side][:, at].bitcast(F32R), w_sb[side][:, at]).then_inc(hi_done, 1)
                        pool.wait_ge(hi_done, e + 1)
                        nc.gpsimd.tensor_tensor(w_lo[side][:, at].bitcast(F32R), w_sb[side][:, at], w_hi[side][:, at],
                                                ALU.subtract).then_inc(split_done, 1)
                        if roots:
                            step(routing, "root", 2 * side + w)

            for turn in turns(pool):
                if isinstance(turn.it, int) and turn.it == routing.it - 1:
                    pool.wait_ge(pv_in, B)
                    split(0)
                for name, n in turn.steps("Pool"):
                    step(turn, name, n)
            step(routing, "ln3a")
            split(1)
            step(routing, "x3T")
            with pool.Fori(2, ROUTED - 1) as it:
                split(it)
            split(ROUTED - 1, roots=True)
            with pool.Fori(ROUTED, NE) as it:
                split(it)

        @block.scalar
        def _(act):
            nc.scalar.preload_act_table(ACT.Exp)
            def step(turn, name, n=0):
                b, side = turn.batch(STAGE_OF[name]), turn.side(STAGE_OF[name])
                if name == "xT":
                    after(act, xT_in, b)
                    after(act, v_in, b - 1)
                    nc.scalar.copy(xnT[:], A[:, 0:2 * T].rearrange("p (c t) -> p c t", c=2)).then_inc(xnT_done, 1)
                elif name == "qk":
                    after(act, qk_full_done, b)
                    after(act, qk_lo_done, b - 1)
                    after(act, q_placed, b - 1, 6, 5, 16)
                    after(act, k_placed, b - 1, 6, 5, 16)
                    nc.scalar.copy(qk_hi[:].bitcast(F32R), qk_full[:]).then_inc(qk_hi_done, 1)
                elif name == "v":
                    after(act, v_in, b)
                    after(act, pv_in, b - 2)
                    if isinstance(b, int) and b < 2:
                        act.wait_ge(consts_set, b + 1)
                    nc.scalar.copy(V1[side][:, :, 0:HD], A[:, 0:D].rearrange("p (h d) -> p h d", h=H)).then_inc(v_done, 1)
                elif name == "mT":
                    after(act, mT_in, b)
                    after(act, max_placed, b - 1, 2, 1, 16)
                    nc.scalar.copy(max_hi[:].bitcast(F32R), Bk[0:H, 0:T]).then_inc(max_hi_done, 1)
                elif name == "p2":
                    slot, k = ring(turn, EXPS, name, n)
                    act.wait_ge(exps_in, k)
                    if n == 0:
                        after(act, pv_in, b - 1)
                    nc.scalar.activation(probs[:, 4 * n:4 * n + 4, :], exp_ring[slot][:]
                                         .rearrange("p (h t) -> p h t", h=4), ACT.Exp, scale=SCALE).then_inc(exps_done, 1)
                elif name == "x2c":
                    g, kt, pair = n // 4, n // 2 % 2, n % 2
                    slot, k = ring(turn, EXPS, name, n)
                    act.wait_ge(exps_in, k)
                    if n % 4 == 0:
                        after(act, xpv_in, b - 1, 4, g)
                    h = 4 * g + 2 * pair
                    nc.scalar.activation(xprobs[:, kt, h:h + 2, :], exp_ring[slot][:]
                                         .rearrange("p (h t) -> p h t", h=2), ACT.Exp, scale=XSCALE).then_inc(exps_done, 1)
                elif name == "pv":
                    after(act, pv_in, b)
                    after(act, norm_in, b - 1)
                    nc.scalar.copy(pv_sb[:], pv_bank[0][:].rearrange("p (g t) -> p g t", g=4)).then_inc(pv_copied, 1)
                elif name == "xpv" and n % 2:
                    after(act, xpv_in, b, 4, n)
                    after(act, xnorm_in, b - 1, 2, 1)
                    nc.scalar.copy(xpv_sb[:, n - 1:n + 1, :], pv_bank[n // 2][:].rearrange("p (g t) -> p g t", g=2))\
                      .then_inc(xpv_copied, 1)
                elif name == "xqk":
                    after(act, xqk_full_done, b)
                    after(act, xqk_lo_done, b - 1)
                    after(act, xq_placed, b - 1, 12, 11, 16)
                    after(act, xk_placed, b - 1, 3, 2, 16)
                    nc.scalar.copy(xqk_hi[:].bitcast(F32R), xqk_full[:]).then_inc(xqk_hi_done, 1)
                elif name == "xmT":
                    after(act, xmT_in, b)
                    after(act, xmax_placed, b - 1, 2, 1, 16)
                    nc.scalar.copy(xmax_hi[:].bitcast(F32R), Bk[0:H, 0:D]).then_inc(xmax_hi_done, 1)
                elif name == "xattnT":
                    after(act, xattnT_in, b)
                    after(act, y_in, b - 1)
                    nc.scalar.activation(xattnT[:], A[:, 0:D], ACT.Identity, bias=xvb_sb[:, 0:1]).then_inc(xattnT_done, 1)
                elif name == "xv":
                    after(act, xv_in, b)
                    after(act, xpv_in, b - 2, 4, 3)
                    nc.scalar.copy(XV1[side][:, :, :, 0:XH], A[:, 0:D].rearrange("p (k h d) -> p k h d", k=NX, h=H))\
                      .then_inc(xv_done, 1)
                elif name == "x3T":
                    after(act, x3T_in, b)
                    after(act, x3T_kept, b - 1)
                    after(act, logits_in, b - 1)
                    nc.scalar.copy(x3T_now[:], A[:, 0:2 * T].rearrange("p (c t) -> p c t", c=2)).then_inc(x3T_now_done, 1)
                elif name == "logits":
                    after(act, logits_done, b)
                    nc.scalar.activation(neg_exp[:], logits[:], ACT.Exp, scale=-1.0).then_inc(neg_exp_done, 1)
                elif name == "gT":
                    after(act, gT_in, b)
                    after(act, gates_stored, b - 1, 1, 0, 16)
                    nc.scalar.copy(gatesT[:], A[0:E, 0:T]).then_inc(gatesT_done, 1)

            def split_input(block):
                act.wait_ge(x3T_kept, 4 * block + 4)
                at = slice(block * 512, block * 512 + 512)
                nc.scalar.copy(x3_hi[:, :, at].bitcast(F32R), x3T[:, :, at]).then_inc(x3_hi_done, 1)

            def squares(it):
                for u in range(4):
                    act.wait_ge(act1_done, it * 4 + u + 1)
                    if not (isinstance(it, int) and it == 0):
                        act.wait_ge(expert_added, it * 4 + u - 3)
                    nc.scalar.activation(act2_hi[u].bitcast(F32R), act1[u], ACT.Square).then_inc(act2_hi_done, 1)
                    nc.scalar.activation(act2[u], act1[u], ACT.Square).then_inc(act2_done, 1)

            for turn in turns(act):
                if isinstance(turn.it, int) and turn.it == routing.it - 1:
                    act.wait_ge(xpv_in, 4 * B - 4)
                    for block in range(3):
                        split_input(block)
                for name, n in turn.steps("ACT"):
                    step(turn, name, n)
            squares(0)
            step(routing, "x3T")
            squares(1)
            step(routing, "logits")
            with act.Fori(2, ROUTED) as it:
                squares(it)
            step(routing, "gT")
            split_input(3)
            with act.Fori(ROUTED, NE) as it:
                squares(it)

        @block.vector
        def _(dve):
            def clear(i):
                nc.vector.memset(Q3[i][:], 0.0)
                nc.vector.memset(K3[i][96:98], 1.0)
                nc.vector.memset(V1[i][:], 0.0).then_inc(cleared, 1)
                if i == 1:
                    for j in range(2):
                        nc.vector.memset(XQ3[j][:], 0.0)
                        nc.vector.memset(XK3[j][96:98], 1.0)
                        nc.vector.memset(XV1[j][:], 0.0).then_inc(cleared, 1)
                    nc.vector.memset(zeros[:], 0.0)
                    for c in range(4):
                        nc.vector.memset(group_w[:, c:c + 1], 9.0 - c)
                    nc.vector.memset(masked[:, 0:1], 9.0)
                    nc.vector.memset(masked[:, 1:2], 8.0)
                    dve.wait_ge(cleared, 4)
                    for j in range(2):
                        nc.vector.memset(XV1[j][:, :, :, XH:XH + 1], 1.0)
                else:
                    dve.wait_ge(cleared, 1)
                nc.vector.memset(V1[i][:, :, HD:HD + 1], 1.0).then_inc(consts_set, 1)

            def norm_rows(i, b):
                after(dve, rstd_done[i], b)
                nc.vector.tensor_scalar(xn[i][:], xres[:, b, :], mean_var[i][:, 0:1], rstd[i][:], ALU.subtract,
                                        ALU.mult).then_inc(xn_done[i], 1)

            def choose_experts(b, n):
                taken = 0

                def then(ins):
                    nonlocal taken
                    ins.then_inc(gate_steps, 1)
                    taken += 1

                if n == 0:
                    after(dve, neg_exp_done, b)
                elif n in (6, 7, 9, 10):
                    after_alone(dve, gate_steps, b, GATE_STEPS, GATE_PARTS[n] - 1)
                else:
                    after(dve, gate_steps, b, GATE_STEPS, GATE_PARTS[n] - 1)
                if n == 0:
                    then(nc.vector.tensor_scalar(one_plus[:], neg_exp[:], 1.0, None, ALU.add))
                elif n == 1:
                    then(nc.vector.reciprocal(sig[:], one_plus[:]))
                elif n == 2:
                    sg = sig[:].rearrange("p (g a c) -> p g a c", g=8, a=2)
                    then(nc.vector.tensor_tensor(pair_max[:], sg[:, :, :, 0], sg[:, :, :, 1], ALU.max))
                    then(nc.vector.tensor_tensor(pair_min[:], sg[:, :, :, 0], sg[:, :, :, 1], ALU.min))
                elif n == 3:
                    then(nc.vector.tensor_tensor(top1[:], pair_max[:, :, 0], pair_max[:, :, 1], ALU.max))
                    then(nc.vector.tensor_tensor(top2a[:], pair_max[:, :, 0], pair_max[:, :, 1], ALU.min))
                    then(nc.vector.tensor_tensor(top2b[:], pair_min[:, :, 0], pair_min[:, :, 1], ALU.max))
                elif n == 4:
                    then(nc.vector.tensor_tensor(top2[:], top2a[:], top2b[:], ALU.max))
                elif n == 5:
                    then(nc.vector.tensor_tensor(group_w[:, 4:12], top1[:], top2[:], ALU.add))
                elif n == 6:
                    then(nc.vector.max(top_groups[:], group_w[:]))
                elif n == 7:
                    then(nc.vector.match_replace(groups_marked[:], top_groups[:], group_w[:], -1.0))
                elif n == 8:
                    then(nc.vector.scalar_tensor_tensor(
                        out=masked[:, 2:2 + E].rearrange("p (g a) -> p g a", g=8),
                        in0=groups_marked[:, 4:12].unsqueeze(2).to_broadcast([P, 8, 4]), scalar=-1.0,
                        in1=sig[:].rearrange("p (g a) -> p g a", g=8), op0=ALU.is_equal, op1=ALU.mult))
                elif n == 9:
                    then(nc.vector.max(top_experts[:], masked[:]))
                elif n == 10:
                    then(nc.vector.match_replace(experts_marked[:], top_experts[:], masked[:], -1.0))
                elif n == 11:
                    then(nc.vector.scalar_tensor_tensor(out=chosen[:], in0=experts_marked[:, 2:2 + E], scalar=-1.0,
                                                        in1=sig[:], op0=ALU.is_equal, op1=ALU.mult))
                elif n == 12:
                    then(nc.vector.tensor_reduce(total[:], chosen[:], AX.X, ALU.add))
                elif n == 13:
                    then(nc.vector.tensor_scalar(total_eps[:], total[:], 1e-20, None, ALU.add))
                elif n == 14:
                    then(nc.vector.reciprocal(inv_total[:], total_eps[:]))
                else:
                    after(dve, root_done, b - 1, ROOT_STEPS, ROOT_STEPS - 1)
                    then(nc.vector.tensor_scalar(gates[:], chosen[:], inv_total[:], ROUTED_SCALE, ALU.mult, ALU.mult))
                assert taken == GATE_PARTS[n + 1] - GATE_PARTS[n]

            def step(turn, name, n=0):
                b, side = turn.batch(STAGE_OF[name]), turn.side(STAGE_OF[name])
                if name in ("ln1s", "ln2s", "ln3s"):
                    i = int(name[2]) - 1
                    if i == 0 and isinstance(b, int):
                        dve.wait_ge(loaded_x, 32)
                        if b > 0:
                            dve.wait_ge(loaded_rest, 16)
                    if i > 0:
                        after_alone(dve, (x1_done, x2_done)[i - 1], b)
                    after_alone(dve, mv_done[i], b - 1)
                    nc.vector.bn_stats(stats[i][:], xres[:, b, :]).then_inc(st_done[i], 1)
                elif name in ("ln1a", "ln2a", "ln3a"):
                    i = int(name[2]) - 1
                    after_alone(dve, st_done[i], b)
                    nc.vector.bn_aggr(mean_var[i][:], stats[i][:]).then_inc(mv_done[i], 1)
                elif name in ("ln1b", "ln2b", "ln3b"):
                    after(dve, {"ln1b": xT_in, "ln2b": xqk_in, "ln3b": x3T_in}[name], b - 1)
                    norm_rows(int(name[2]) - 1, b)
                elif name == "qk":
                    if isinstance(b, int):
                        dve.wait_ge(loaded_w, 11 * 16)
                    after(dve, qk_in, b)
                    after(dve, qk_lo_done, b - 1)
                    nc.vector.tensor_tensor(qk_full[:], Bk[:].rearrange("p (c t) -> p c t", c=4),
                                            qkb_sb[:].unsqueeze(2).to_broadcast([P, 4, T]), ALU.add).then_inc(qk_full_done, 1)
                elif name in SCORES:
                    slot, k = ring(turn, SCORES, name, n)
                    dve.wait_ge(scores_in, k)
                    scores = score_ring[slot][:].rearrange("p (c t) -> p c t", c=2)
                    if name == "p1":
                        if n == 0:
                            after(dve, mT_in, b - 1)
                        to = negmax[:, 2 * n:2 * n + 2]
                        at = n - min(n, 6)
                        scores = scores[:, :, at * T:(at + 1) * T]
                    else:
                        if n == 0:
                            after(dve, xmT_in, b - 1)
                        to = xnegmax[:, :, n]
                    nc.vector.tensor_reduce(to, scores, AX.X, ALU.max, negate=True).then_inc(scores_max, 1)
                elif name == "mT":
                    after(dve, max_hi_done, b)
                    after(dve, max_placed, b - 1, 2, 1, 16)
                    nc.vector.tensor_tensor(max_lo[:].bitcast(F32R), Bk[0:H, 0:T], max_hi[:], ALU.subtract)\
                      .then_inc(max_lo_done, 1)
                elif name == "rsum":
                    after(dve, norm_in, b)
                    a = A[:].rearrange("p (h c) -> p h c", h=H)
                    after(dve, attn_done, b - 1)
                    nc.vector.reciprocal(rsum[:].unsqueeze(2), a[:, :, HD:HD + 1]).then_inc(rsum_done, 1)
                elif name == "norm":
                    a = A[:].rearrange("p (h c) -> p h c", h=H)
                    after(dve, rsum_done, b)
                    after(dve, attnT_in, b - 1)
                    nc.vector.tensor_tensor(attn[:].rearrange("p (h d) -> p h d", h=H), a[:, :, 0:HD],
                                            rsum[:].unsqueeze(2).to_broadcast([P, H, HD]), ALU.mult).then_inc(attn_done, 1)
                elif name == "attnT":
                    after(dve, attnT_in, b)
                    after(dve, wo_in, b - 1)
                    nc.vector.tensor_tensor(attnT[:], Bk[:, 0:D].rearrange("p (c t) -> p c t", c=2),
                                            vb_sb[:].unsqueeze(2).to_broadcast([P, 2, T]), ALU.add).then_inc(attnT_done, 1)
                elif name == "wo":
                    after(dve, wo_in, b)
                    after(dve, x_bo_done, b)
                    nc.vector.tensor_tensor(xres[:, b, :], A[:, 0:D], x_bo[:], ALU.add).then_inc(x1_done, 1)
                elif name == "xqk":
                    after(dve, xqk_in, b)
                    after(dve, xqk_lo_done, b - 1)
                    nc.vector.tensor_tensor(xqk_full[:], Bk[:].rearrange("p (c t) -> p c t", c=2),
                                            xqkb_sb[:].unsqueeze(2).to_broadcast([P, 2, D]), ALU.add).then_inc(xqk_full_done, 1)
                elif name == "xmT":
                    after(dve, xmax_hi_done, b)
                    after(dve, xmax_placed, b - 1, 2, 1, 16)
                    nc.vector.tensor_tensor(xmax_lo[:].bitcast(F32R), Bk[0:H, 0:D], xmax_hi[:], ALU.subtract)\
                      .then_inc(xmax_lo_done, 1)
                elif name == "xrsum":
                    after(dve, xnorm_in, b, 2, n)
                    a = (A, Bk)[n][:].rearrange("p (h c) -> p h c", h=H)
                    after(dve, xattn_done, b - 1, 2, n)
                    nc.vector.reciprocal(xrsum[:, n, :].unsqueeze(2), a[:, :, XH:XH + 1]).then_inc(xrsum_done, 1)
                elif name == "xnorm":
                    a = (A, Bk)[n][:].rearrange("p (h c) -> p h c", h=H)
                    after(dve, xrsum_done, b, 2, n)
                    after(dve, xattnT_in, b - 1)
                    nc.vector.tensor_tensor(xattn[:, n, :].rearrange("p (h d) -> p h d", h=H), a[:, :, 0:XH],
                                            xrsum[:, n, :].unsqueeze(2).to_broadcast([P, H, XH]), ALU.mult)\
                      .then_inc(xattn_done, 1)
                elif name == "y":
                    after(dve, y_in, b)
                    nc.vector.scalar_tensor_tensor(out=xres[:, b, :], in0=Bk[:, 0:D], scalar=xbo_sb[:, 0:1],
                                                   in1=xres[:, b, :], op0=ALU.add, op1=ALU.add).then_inc(x2_done, 1)
                elif name == "logits":
                    after(dve, logits_in, b)
                    after(dve, neg_exp_done, b - 1)
                    nc.vector.tensor_tensor(logits[:], Bk[:, 0:E], br_sb[:], ALU.add).then_inc(logits_done, 1)
                elif name == "gates":
                    choose_experts(b, n)

            def split_input(block):
                at = slice(block * 512, block * 512 + 512)
                dve.wait_ge(x3_hi_done, block + 1)
                nc.vector.tensor_tensor(x3_lo[:, :, at].bitcast(F32R), x3T[:, :, at], x3_hi[:, :, at], ALU.subtract)\
                  .then_inc(x3_split, 1)

            def gated_relu(it, u):
                side, blk = u // 2, u % 2
                if blk == 0:
                    dve.wait_ge(groot_loaded[side], (it + 1) * 16)
                dve.wait_ge(hidden_in, it * 4 + u + 1)
                if not (isinstance(it, int) and it == 0):
                    dve.wait_ge(act2_done, it * 4 + u - 3)
                nc.vector.scalar_tensor_tensor(out=act1[u], in0=bank[4 + u][:], scalar=0.0, in1=groot[side][:, blk, :],
                                               op0=ALU.max, op1=ALU.mult).then_inc(act1_done, 1)

            def elementwise(it, more=True, gates=()):
                for u in range(4):
                    for part in gates[u * len(gates) // 4:(u + 1) * len(gates) // 4]:
                        step(routing, "gates", part)
                    if u < 3:
                        gated_relu(it, u + 1)
                    elif more:
                        gated_relu(it + 1, 0)
                    dve.wait_ge(act2_done, it * 4 + u + 1)
                    if not (isinstance(it, int) and it == 0):
                        dve.wait_ge(expert_added, it * 4 + u - 3)
                    dve.wait_ge(act2_hi_done, it * 4 + u + 1)
                    nc.vector.tensor_tensor(act2_lo[u].bitcast(F32R), act2[u], act2_hi[u], ALU.subtract).then_inc(act2_split, 1)

            def add_half(half):
                dve.wait_ge(half_in, half + 1)
                for t in range(8):
                    nc.vector.tensor_tensor(xres[:, 8 * half + t, :], bank[t // 2][:, (t % 2) * D:(t % 2 + 1) * D],
                                            xres[:, 8 * half + t, :], ALU.add).then_inc(half_added, 1)

            for turn in turns(dve):
                for name, n in turn.steps("DVE"):
                    step(turn, name, n)
                    if isinstance(turn.it, int) and turn.it == 0 and name == "ln1b":
                        clear(0)
                if isinstance(turn.it, int) and turn.it == 0:
                    clear(1)
            dve.wait_ge(xpv_in, 4 * B)
            for block in range(2):
                split_input(block)
            step(routing, "ln3s")
            gated_relu(0, 0)
            step(routing, "ln3a")
            elementwise(0)
            step(routing, "ln3b")
            elementwise(1)
            step(routing, "logits")
            elementwise(2, gates=range(0, 8))
            elementwise(3, gates=range(8, 16))
            with dve.Fori(4, ROUTED) as it:
                elementwise(it)
            for block in range(2, 4):
                split_input(block)
            with dve.Fori(ROUTED, NE // 2) as it:
                elementwise(it)
            add_half(0)
            with dve.Fori(NE // 2, NE - 1) as it:
                elementwise(it)
            elementwise(NE - 1, more=False)
            add_half(1)

        @block.tensor
        def _(pe):
            def r(ap):
                return ap.bitcast(F32R)

            def ring_slot(turn, kinds, name, n, read):
                slot, k = ring(turn, kinds, name, n)
                if not isinstance(k, int) or k > 2:
                    pe.wait_ge(read, k - 2)
                return slot

            pe.wait_ge(loaded_x, 32)
            pe.wait_ge(loaded_w, 11 * 16)
            def step(turn, name, n=0):
                b, side = turn.batch(STAGE_OF[name]), turn.side(STAGE_OF[name])
                if name == "p1":
                    if n == 0:
                        after(pe, q_placed, b, 6, 5, 16)
                        after(pe, k_placed, b, 6, 5, 16)
                    slot = ring_slot(turn, SCORES, name, n, scores_max)
                    g = min(n, 6)
                    for odd in range(2):
                        mm = pe.matmul(score_ring[slot][:, odd * 2 * T:(odd + 1) * 2 * T], r(Q3[side][0:96, n, odd, :]),
                                       r(K3[side][0:96, g:g + 2, :]), start=True, stop=True)
                    mm.then_inc(scores_in, 1)
                elif name == "p2":
                    if n == 0:
                        after(pe, max_placed, b, 2, 1, 16)
                    slot = ring_slot(turn, EXPS, name, n, exps_done)
                    for i in range(2):
                        g = 2 * n + i
                        mm = pe.matmul(exp_ring[slot][:, i * 2 * T:(i + 1) * 2 * T], r(K3[side][0:98, g, :]),
                                       r(Q3[side][0:98, g, :, :]), start=True, stop=True)
                    mm.then_inc(exps_in, 1)
                elif name == "x1c":
                    if n == 0:
                        after(pe, xq_placed, b, 12, 11, 16)
                        after(pe, xk_placed, b, 3, 2, 16)
                    slot = ring_slot(turn, SCORES, name, n, scores_max)
                    for qt in range(NX):
                        mm = pe.matmul(score_ring[slot][:, qt * D:(qt + 1) * D],
                                       r(XQ3[side][0:96, n // 4, n % 4, qt * P:(qt + 1) * P]),
                                       r(XK3[side][0:96, n // 4, :]), start=True, stop=True)
                    mm.then_inc(scores_in, 1)
                elif name == "x2c":
                    if n == 0:
                        after(pe, xmax_placed, b, 2, 1, 16)
                    g, kt, pair = n // 4, n // 2 % 2, n % 2
                    slot = ring_slot(turn, EXPS, name, n, exps_done)
                    pe.matmul(exp_ring[slot][:], r(XK3[side][0:98, g, kt * P:(kt + 1) * P]),
                              r(XQ3[side][0:98, g, 2 * pair:2 * pair + 2, :]), start=True, stop=True).then_inc(exps_in, 1)
                elif name == "xT":
                    after(pe, xn_done[0], b)
                    bank_free(pe, turn, A_USES, "xT")
                    for c in range(2):
                        mm = pe.transpose(A[:, c * T:(c + 1) * T], xn[0][:, c * P:(c + 1) * P], eye_sb[:])
                    mm.then_inc(xT_in, 1)
                elif name == "qk":
                    if n == 0:
                        after(pe, xnT_done, b)
                        bank_free(pe, turn, B_USES, "qk")
                    for m in (n,):
                        for c in range(2):
                            mm = pe.matmul(Bk[:, m * T:(m + 1) * T], wqkv_sb[:, c, m, :], xnT[:, c, :],
                                           start=(c == 0), stop=(c == 1))
                    if n == 3:
                        mm.then_inc(qk_in, 1)
                elif name == "v":
                    bank_free(pe, turn, A_USES, "v")
                    for c in range(2):
                        mm = pe.matmul(A[:, 0:D], xnT[:, c, :], wqkv_sb[:, c, 4:6, :], start=(c == 0), stop=(c == 1))
                    mm.then_inc(v_in, 1)
                elif name == "mT":
                    pe.wait_ge(scores_max, ring(turn, SCORES, "p1", 7)[1])
                    bank_free(pe, turn, B_USES, "mT")
                    pe.transpose(Bk[0:H, 0:T], negmax[:], eye_sb[:]).then_inc(mT_in, 1)
                elif name == "pv":
                    pe.wait_ge(exps_done, ring(turn, EXPS, "p2", n)[1])
                    if n == 0:
                        after(pe, v_done, b)
                        after(pe, pv_copied, b - 1)
                        if turn.has("X2"):
                            after(pe, xpv_copied, turn.batch("X2"), 2, 0)
                        else:
                            after(pe, xpv_copied, min(turn.batch("X2"), B - 1), 2, 0)
                    for g in (n,):
                        for j in range(4):
                            h = 4 * g + j
                            mm = pe.matmul(pv_bank[0][32 * j:32 * j + 32, g * T:(g + 1) * T], V1[side][:, h, :],
                                           probs[:, h, :], start=True, stop=True)
                    if n == 3:
                        mm.then_inc(pv_in, 1)
                elif name == "norm":
                    after(pe, pv_copied, b)
                    bank_free(pe, turn, A_USES, "norm")
                    for g in range(4):
                        mm = pe.transpose(A[:, g * P:(g + 1) * P], pv_sb[:, g, :], eye_sb[:])
                    mm.then_inc(norm_in, 1)
                elif name == "attnT":
                    after(pe, attn_done, b)
                    bank_free(pe, turn, B_USES, "attnT")
                    for c in range(2):
                        mm = pe.transpose(Bk[:, c * T:(c + 1) * T], attn[:, c * P:(c + 1) * P], eye_sb[:])
                    mm.then_inc(attnT_in, 1)
                elif name == "wo":
                    after(pe, attnT_done, b)
                    bank_free(pe, turn, A_USES, "wo")
                    for c in range(2):
                        mm = pe.matmul(A[:, 0:D], attnT[:, c, :], wo_sb[:, c, :], start=(c == 0), stop=(c == 1))
                    mm.then_inc(wo_in, 1)
                elif name == "xqk":
                    after(pe, xn_done[1], b)
                    pe.wait_ge(loaded_ctx[side], (turn.earlier_on_side("SB") + 1) * 16)
                    bank_free(pe, turn, B_USES, "xqk")
                    pe.matmul(Bk[:, 0:D], xw_sb[:, 0, :], xn[1][:], start=True, stop=True)
                    pe.matmul(Bk[:, D:2 * D], xw_sb[:, 1, :], ctx_sb[side][:], start=True, stop=True).then_inc(xqk_in, 1)
                elif name == "xv":
                    bank_free(pe, turn, A_USES, "xv")
                    for kt in range(NX):
                        mm = pe.matmul(A[:, kt * P:(kt + 1) * P], ctx_sb[side][:, kt * P:(kt + 1) * P], xw_sb[:, 2, :],
                                       start=True, stop=True)
                    mm.then_inc(xv_in, 1)
                elif name == "xmT":
                    pe.wait_ge(scores_max, ring(turn, SCORES, "x1c", 15)[1])
                    bank_free(pe, turn, B_USES, "xmT")
                    for qt in range(NX):
                        mm = pe.transpose(Bk[0:H, qt * P:(qt + 1) * P], xnegmax[:, qt, :], eye_sb[:])
                    mm.then_inc(xmT_in, 1)
                elif name == "xpv":
                    pe.wait_ge(exps_done, ring(turn, EXPS, "x2c", 4 * n + 3)[1])
                    if n == 0:
                        after(pe, xv_done, b)
                        if not isinstance(b, int) or 0 <= turn.batch("SB", 1) < B:
                            after(pe, pv_copied, turn.batch("SB", 1))
                        after(pe, xpv_copied, b - 1, 2, 0)
                    if n == 2:
                        after(pe, xpv_copied, b - 1, 2, 1)
                    for kt in range(NX):
                        for j in range(4):
                            h = 4 * n + j
                            mm = pe.matmul(pv_bank[n // 2][32 * j:32 * j + 32, (n % 2) * D:(n % 2 + 1) * D],
                                           XV1[side][:, kt, h, :], xprobs[:, kt, h, :], start=(kt == 0), stop=(kt == NX - 1))
                    mm.then_inc(xpv_in, 1)
                elif name == "xnorm":
                    if n == 0:
                        after(pe, xpv_copied, b, 2, 1)
                    bank_free(pe, turn, (A_USES, B_USES)[n], f"xnorm{n}")
                    for g in range(4):
                        mm = pe.transpose((A, Bk)[n][:, g * P:(g + 1) * P], xpv_sb[:, g, n * P:(n + 1) * P], eye_sb[:])
                    mm.then_inc(xnorm_in, 1)
                elif name == "xattnT":
                    after(pe, xattn_done, b, 2, 1)
                    bank_free(pe, turn, A_USES, "xattnT")
                    for qt in range(NX):
                        mm = pe.transpose(A[:, qt * P:(qt + 1) * P], xattn[:, qt, :], eye_sb[:])
                    mm.then_inc(xattnT_in, 1)
                elif name == "y":
                    after(pe, xattnT_done, b)
                    bank_free(pe, turn, B_USES, "y")
                    pe.matmul(Bk[:, 0:D], xw_sb[:, 3, :], xattnT[:], start=True, stop=True).then_inc(y_in, 1)
                elif name == "x3T":
                    after(pe, xn_done[2], b)
                    bank_free(pe, turn, A_USES, "x3T")
                    for c in range(2):
                        mm = pe.transpose(A[:, c * T:(c + 1) * T], xn[2][:, c * P:(c + 1) * P], eye_sb[:])
                    mm.then_inc(x3T_in, 1)
                elif name == "logits":
                    after(pe, x3T_now_done, b)
                    bank_free(pe, turn, B_USES, "logits")
                    for c in range(2):
                        mm = pe.matmul(Bk[:, 0:E], x3T_now[:, c, :], wr_sb[:, c, :], start=(c == 0), stop=(c == 1))
                    mm.then_inc(logits_in, 1)
                elif name == "gT":
                    after(pe, root_done, b, ROOT_STEPS, ROOT_STEPS - 1)
                    bank_free(pe, turn, A_USES, "gT")
                    pe.transpose(A[0:E, 0:T], root_gates[:], eye_sb[:]).then_inc(gT_in, 1)

            for turn in turns(pe):
                if isinstance(turn.it, int) and 1 <= turn.it <= 2:
                    pe.wait_ge(consts_set, turn.it)
                for name, n in turn.steps("PE"):
                    step(turn, name, n)

            pe.wait_ge(xpv_copied, 2 * B)

            def clear_half(half):
                if half:
                    pe.wait_ge(half_added, 8 * half)
                for i in range(4):
                    pe.matmul(bank[i][:], zeros[:, 0:P], zeros[:], start=True, stop=False, skip_group_check=True)

            def hidden(it, u, half):
                side, blk = u // 2, u % 2
                if blk == 0:
                    pe.wait_ge(w1_split, it * 2 + side + 1)
                if not (isinstance(it, int) and it == 0):
                    pe.wait_ge(act1_done, it * 4 + u - 3)
                elif side == 0:
                    pe.wait_ge(x3_hi_done, blk + 1)
                at = 1024 * half + 512 * blk
                parts = [(w, xs, c) for w, xs in ((w_hi, x3_hi), (w_lo, x3_hi), (w_hi, x3_lo)) for c in range(2)]
                for i, (w, xs, c) in enumerate(parts):
                    if i == 4 and isinstance(it, int) and it == 0 and side == 0:
                        pe.wait_ge(x3_split, blk + 1)
                    mm = pe.matmul(bank[4 + u][:], r(w[side][:, c, :]), r(xs[:, c, at:at + 512]), start=(i == 0),
                                   stop=(i == len(parts) - 1))
                mm.then_inc(hidden_in, 1)

            def output(it, u):
                side, blk = u // 2, u % 2
                if blk == 0:
                    pe.wait_ge(w2_split, it * 2 + side + 1)
                pe.wait_ge(act2_split, it * 4 + u + 1)
                for t in range(4):
                    tile = 4 * blk + t
                    for a, w in ((act2_hi, w_hi), (act2_hi, w_lo), (act2_lo, w_hi)):
                        mm = pe.matmul(bank[tile // 2][:, (tile % 2) * D:(tile % 2 + 1) * D], r(a[u][:, t * P:(t + 1) * P]),
                                       r(w[side][:, 2:4, :]), start=False, stop=False, skip_group_check=True)
                mm.then_inc(expert_added, 1)

            def expert_pair(it, half, next_half):
                for u in range(4):
                    if u < 2:
                        hidden(it, u + 2, half)
                    elif next_half is not None:
                        hidden(it + 1, u - 2, next_half)
                    output(it, u)

            def close_half():
                for i in range(4):
                    mm = pe.matmul(bank[i][:], zeros[:, 0:P], zeros[:], start=False, stop=True, skip_group_check=True)
                mm.then_inc(half_in, 1)

            clear_half(0)
            hidden(0, 0, 0)
            hidden(0, 1, 0)
            pe.wait_ge(xattnT_done, B)
            pe.wait_ge(gatesT_done, B - 1)
            pe.wait_ge(x2_done, B)
            expert_pair(0, 0, 0)
            step(routing, "x3T")
            pe.wait_ge(x3T_now_done, B)
            expert_pair(1, 0, 0)
            step(routing, "logits")
            pe.wait_ge(logits_done, B)
            with pe.Fori(2, ROUTED) as it:
                expert_pair(it, 0, 0)
            step(routing, "gT")
            pe.wait_ge(gatesT_done, B)
            with pe.Fori(ROUTED, NE // 2 - 1) as it:
                expert_pair(it, 0, 0)
            pe.wait_ge(x3_split, 4)
            expert_pair(NE // 2 - 1, 0, 1)
            close_half()
            clear_half(1)
            with pe.Fori(NE // 2, NE - 1) as it:
                expert_pair(it, 1, 1)
            expert_pair(NE - 1, 1, None)
            close_half()


def kernel(**inputs):
    import numpy as np
    import concourse.bacc as bacc
    from concourse.bass_utils import run_bass_kernel_spmd

    def f(name):
        return np.asarray(inputs[name])

    rows = np.arange(P)
    order = [(2 * (rows % 8) + odd) * 16 + rows // 8 for odd in range(2)]
    wq, wk, wv = f("L0_attn_wq"), f("L0_attn_wk"), f("L0_attn_wv")
    bq, bk = f("L0_attn_bq"), f("L0_attn_bk")
    cols = [wq[:, order[0]], wq[:, order[1]], wk[:, order[0]], wk[:, order[1]], wv[:, 0:P], wv[:, P:2 * P]]
    wqkv = np.stack(cols, axis=1).reshape(2, P, 6, P).transpose(1, 0, 2, 3)
    qk_bias = np.stack([bq[order[0]], bq[order[1]], bk[order[0]], bk[order[1]]], axis=1)
    xorder = (4 * (rows % 4) + rows // 32) * 8 + rows // 4 % 8
    xw = np.stack([f("L0_xattn_Wq")[xorder].T, f("L0_xattn_Wk")[xorder].T, f("L0_xattn_Wv").T, f("L0_xattn_Wo").T], axis=1)
    xqk_bias = np.stack([f("L0_xattn_bq")[xorder], f("L0_xattn_bk")[xorder]], axis=1)
    W1 = np.concatenate([f("L0_ffn_W1"), f("L0_ffn_Ws1").reshape(2, P, 256)])
    W2 = np.concatenate([f("L0_ffn_W2"), f("L0_ffn_Ws2").reshape(256, 2, P).transpose(1, 0, 2)])
    w1 = W1.transpose(0, 2, 1).reshape(-1, 2, P, P).transpose(0, 2, 1, 3)
    w2 = W2.transpose(0, 2, 1).reshape(-1, P, 2, P)
    arrays = {
        "x": f("x"), "ctx_in": f("ctx_2048"), "wqkv": wqkv, "qk_bias": qk_bias,
        "v_bias": f("L0_attn_bv").reshape(2, P).T,
        "wo": f("L0_attn_wo").reshape(2, P, 256).transpose(1, 0, 2),
        "bo": np.broadcast_to(f("L0_attn_bo"), (P, 256)),
        "xw": xw, "xqk_bias": xqk_bias, "xv_bias": f("L0_xattn_bv")[:, None], "xbo": f("L0_xattn_bo")[:, None],
        "wr": f("L0_ffn_Wr").T.reshape(2, P, -1).transpose(1, 0, 2),
        "br": np.broadcast_to(f("L0_ffn_br"), (P, 32)),
        "experts": np.concatenate([w1, w2], axis=2), "eye": np.eye(P, dtype=np.float32),
    }
    arrays = {k: np.ascontiguousarray(v) for k, v in arrays.items()}
    nc = bacc.Bacc("TRN2", target_bir_lowering=False, num_devices=1)
    args = [nc.dram_tensor(k, v.shape, mybir.dt.from_np(v.dtype), kind="ExternalInput").ap() for k, v in arrays.items()]
    out = nc.dram_tensor("out", (16, P, 256), F32, kind="ExternalOutput").ap()
    gates_dram = nc.dram_tensor("gates_dram", (34, 16 * P), F32, kind="Internal").ap()
    decoder_layer(nc, *args, out, gates_dram)
    r = run_bass_kernel_spmd(nc, [arrays], core_ids=[0])
    return r.results[0]["out"]
```

```python
from contextlib import ExitStack

import concourse.bass as bass
from concourse import mybir

F32 = mybir.dt.float32
F32R = mybir.dt.float32r
BF16 = mybir.dt.bfloat16
ALU = mybir.AluOpType
ACT = mybir.ActivationFunctionType
AX = mybir.AxisListType

P = 128
EPS = 1e-5
ROUTED_SCALE = 2.5
FIRST, LAST = 6, 16
LATE = 2
STAGES = ("SA", "SB", "X1", "X2", "X3", "R")

ORDER = {
    "PE": """
    p1 0, xnorm 0, p1 1, xnorm 1, x2c 0, x2c 1, x3T, p1 2, x2c 2, p1 3, p1 4, logits, xattnT, p1 5,
    p1 6, p1 7, x2c 3, xT, y, x2c 4, mT, xpv 0, x2c 5, x2c 6, qk 0, x2c 7, qk 1, x2c 8,
    xpv 1, x1c 0, x1c 1, x2c 9, qk 2, x1c 2, x1c 3, p2 0, qk 3, p2 1, x1c 4, p2 2, x1c 5, v,
    x1c 6, p2 3, pv 0, pv 1, x2c 10, x1c 7, pv 2, x2c 11, x1c 8, pv 3, x2c 12, x1c 9, x2c 13, x1c 10,
    norm, xpv 2, attnT, x1c 11, x2c 14, x1c 12, wo, x2c 15, x1c 13, x1c 14, x1c 15, xpv 3, xqk, gT,
    xmT, xv
    """,
    "DVE": """
    ln3s, ln1s, p1 0, ln3a, xrsum 0, p1 1, ln1a, xrsum 1, ln3b, xnorm 0, xnorm 1, p1 2, p1 3, p1 4,
    logits, ln1b, p1 5, gates 0, p1 6, gates 1, p1 7, gates 2, gates 3, y, gates 4, gates 5, mT, gates 6,
    gates 7, gates 8, gates 9, gates 10, gates 11, gates 12, x1c 0, x1c 1, x1c 2, gates 13, gates 14, x1c 3, qk, x1c 4,
    x1c 5, gates 15, x1c 6, x1c 7, x1c 8, x1c 9, rsum, norm, x1c 10, attnT, x1c 11, x1c 12, wo, ln2s,
    ln2a, x1c 13, ln2b, x1c 14, x1c 15, xqk, xmT
    """,
    "ACT": """
    x2c 0, x3T, x2c 1, x2c 2, logits, xattnT, xT, x2c 3, x2c 4, mT, x2c 5, x2c 6, x2c 7, x2c 8,
    xpv 1, x2c 9, p2 0, p2 1, qk, p2 2, p2 3, v, x2c 10, x2c 11, pv, x2c 12, x2c 13, x2c 14,
    x2c 15, xpv 3, gT, xqk, xmT, xv
    """,
    "Pool": """
    x_bo, ln3a, ln1a, x3T, qk, root 0, root 1, root 2, ln2a, root 3, xqk
    """,
    "SP": """
    max_rows, k_rows, q_rows, xmax_rows, xk_rows, xq_rows, gT, xv
    """,
}
ORDER = {engine: [s.strip() for s in text.replace("\n", " ").split(",")] for engine, text in ORDER.items()}
SCORES, EXPS = ("p1", "x1c"), ("p2", "x2c")
STEPS_OF = {
    "SA": "ln1s ln1a ln1b xT qk k_rows q_rows v",
    "SB": "p1 mT max_rows p2 x_bo pv rsum norm attnT wo ln2s ln2a ln2b xqk xk_rows xq_rows",
    "X1": "x1c xv xmT xmax_rows",
    "X2": "x2c xpv",
    "X3": "xrsum xnorm xattnT y",
    "R": "ln3s ln3a ln3b x3T logits gates root gT",
}
STAGE_OF = {name: stage for stage, names in STEPS_OF.items() for name in names.split()}


def decoder_layer(nc, x, ctx_in, wqkv, qk_bias, v_bias, wo, bo, xw, xqk_bias, xv_bias, xbo, wr, br, experts, eye,
                  out, gates_dram):
    B, T, D = x.shape
    H = 16
    HD = D // H
    XH = T // H
    E = wr.shape[2]
    NE = experts.shape[0]
    SCALE = float(D) ** -0.5
    XSCALE = float(T) ** -0.5
    NX = D // P
    assert T == P and D == 2 * P and 3 * 2 * HD == 96 and 3 * 4 * XH == 96 and NE % 2 == 0

    class Turn:

        def __init__(self, pair, parity):
            self.it = pair * 2 + parity
            self.pair = pair
            self.parity = parity

        def batch(self, stage, back=0):
            return self.it - (STAGES.index(stage) + back)

        def side(self, stage):
            return (self.parity + STAGES.index(stage)) % 2

        def earlier_on_side(self, stage):
            return self.pair + (self.parity - STAGES.index(stage)) // 2

        def has(self, stage, back=0):
            return not isinstance(self.it, int) or 0 <= self.batch(stage, back) < B - (LATE if stage == "R" else 0)

        def steps(self, engine):
            for s in ORDER[engine]:
                name, _, n = s.partition(" ")
                if self.has(STAGE_OF[name]):
                    yield name, int(n or 0)

    def turns(eng):
        for it in range(FIRST):
            yield Turn(it // 2, it % 2)
        with eng.Fori(FIRST // 2, LAST // 2) as pair:
            yield Turn(pair, 0)
            yield Turn(pair, 1)
        for it in range(LAST, B + len(STAGES) - 2):
            yield Turn(it // 2, it % 2)

    ROUTED = 6
    last = B + len(STAGES) - 3
    late = [Turn((last + k) // 2, (last + k) % 2) for k in range(LATE)]

    def ring(turn, kinds, step, n):
        def each(it):
            return sum(1 for s in ORDER["PE"] if s.split()[0] in kinds and 0 <= it - STAGES.index(STAGE_OF[s.split()[0]]) < B)
        if isinstance(turn.it, int):
            before = sum(each(it) for it in range(turn.it))
        else:
            before = (turn.it - FIRST) * each(FIRST) + sum(each(it) for it in range(FIRST))
        within = [s for s in turn.steps("PE") if s[0] in kinds].index((step, n))
        return within % 2, before + within + 1

    with ExitStack() as stack:
        def sb(name, shape, dt=F32):
            return stack.enter_context(nc.sbuf_tensor(name, shape, dt))

        def sem(name):
            return stack.enter_context(nc.semaphore(name))

        xres = sb("xres", [P, B, D])
        ctx_sb = [sb(f"ctx{i}", [P, D]) for i in range(2)]
        wqkv_sb = sb("wqkv_sb", [P, 2, 6, P])
        qkb_sb = sb("qkb_sb", [P, 4])
        vb_sb = sb("vb_sb", [P, 2])
        wo_sb = sb("wo_sb", [P, 2, D])
        bo_sb = sb("bo_sb", [P, D])
        xw_sb = sb("xw_sb", [P, 4, P])
        xqkb_sb = sb("xqkb_sb", [P, 2])
        xvb_sb = sb("xvb_sb", [P, 1])
        xbo_sb = sb("xbo_sb", [P, 1])
        wr_sb = sb("wr_sb", [P, 2, E])
        br_sb = sb("br_sb", [P, E])
        eye_sb = sb("eye_sb", [P, P])
        stats = [sb(f"stats{i}", [P, 6]) for i in range(3)]
        mean_var = [sb(f"mean_var{i}", [P, 2]) for i in range(3)]
        var_eps = [sb(f"var_eps{i}", [P, 1]) for i in range(3)]
        rstd = [sb(f"rstd{i}", [P, 1]) for i in range(3)]
        xn = [sb(f"xn{i}", [P, D]) for i in range(3)]
        exponents = sb("exponents", [P, E + 1])
        xnT = sb("xnT", [P, 2, T])
        qk_full = sb("qk_full", [P, 4, T])
        qk_hi = sb("qk_hi", [P, 4, T])
        qk_lo = sb("qk_lo", [P, 4, T])
        Q3 = [sb(f"Q3_{i}", [P, 8, 2, T]) for i in range(2)]
        K3 = [sb(f"K3_{i}", [P, 8, T]) for i in range(2)]
        V1 = [sb(f"V1_{i}", [P, H, 32]) for i in range(2)]
        negmax = sb("negmax", [P, H])
        max_hi = sb("max_hi", [H, T])
        max_lo = sb("max_lo", [H, T])
        probs = sb("probs", [P, H, T])
        pv_sb = sb("pv_sb", [P, 4, T])
        rsum = sb("rsum", [P, H])
        attn = sb("attn", [P, D])
        attnT = sb("attnT", [P, 2, T])
        x_bo = sb("x_bo", [P, D])
        xqk_full = sb("xqk_full", [P, 2, D])
        xqk_hi = sb("xqk_hi", [P, 2, D])
        xqk_lo = sb("xqk_lo", [P, 2, D])
        XQ3 = [sb(f"XQ3_{i}", [P, 4, 4, D]) for i in range(2)]
        XK3 = [sb(f"XK3_{i}", [P, 4, D]) for i in range(2)]
        XV1 = [sb(f"XV1_{i}", [P, NX, H, 32]) for i in range(2)]
        xnegmax = sb("xnegmax", [P, NX, H])
        xmax_hi = sb("xmax_hi", [H, D])
        xmax_lo = sb("xmax_lo", [H, D])
        xprobs = sb("xprobs", [P, NX, H, D])
        xpv_sb = sb("xpv_sb", [P, 4, D])
        xrsum = sb("xrsum", [P, NX, H])
        xattn = sb("xattn", [P, NX, P])
        xattnT = sb("xattnT", [P, D])
        x3T_now = sb("x3T_now", [P, 2, T])
        x3T = sb("x3T", [P, 2, B * T])
        logits = sb("logits", [P, E])
        neg_exp = sb("neg_exp", [P, E])
        one_plus = sb("one_plus", [P, E])
        sig = sb("sig", [P, E])
        pair_max = sb("pair_max", [P, 8, 2])
        pair_min = sb("pair_min", [P, 8, 2])
        top1 = sb("top1", [P, 8])
        top2a = sb("top2a", [P, 8])
        top2b = sb("top2b", [P, 8])
        top2 = sb("top2", [P, 8])
        group_w = sb("group_w", [P, 4 + 8])
        top_groups = sb("top_groups", [P, 8])
        groups_marked = sb("groups_marked", [P, 4 + 8])
        masked = sb("masked", [P, 2 + E])
        top_experts = sb("top_experts", [P, 8])
        experts_marked = sb("experts_marked", [P, 2 + E])
        chosen = sb("chosen", [P, E])
        total = sb("total", [P, 1])
        total_eps = sb("total_eps", [P, 1])
        inv_total = sb("inv_total", [P, 1])
        gates = sb("gates", [P, E])
        root_gates = sb("root_gates", [P, E])
        gatesT = sb("gatesT", [E, T])
        w_sb = [sb(f"w_sb{i}", [P, 4, P]) for i in range(2)]
        groot = [probs[:, 8 * i:8 * i + 8, :].rearrange("p (a h) t -> p a (h t)", a=2) for i in range(2)]
        act1, act2 = [[xprobs[:, k, 2 * i:2 * i + 2, :].rearrange("p a t -> p (a t)") for i in range(4)] for k in range(2)]
        act2_hi = [K3[i // 2][:, i % 2 * 4:i % 2 * 4 + 4, :].rearrange("p a t -> p (a t)") for i in range(4)]
        act2_lo = [XK3[i // 2][:, i % 2 * 2:i % 2 * 2 + 2, :].rearrange("p a t -> p (a t)") for i in range(4)]
        w_hi, w_lo = [[Q3[i][:, 2 * k:2 * k + 2].rearrange("p a b t -> p (a b) t") for i in range(2)] for k in range(2)]
        x3_hi, x3_lo = [XQ3[i][:].rearrange("p a b d -> p (a b d)").rearrange("p (c t) -> p c t", c=2) for i in range(2)]
        zeros = sb("zeros", [P, 512], BF16)
        ones = sb("ones", [64, (NE - E) * B * T // 64])

        bank = [stack.enter_context(nc.psum_tensor(f"bank{i}", [P, 512], F32)) for i in range(8)]
        score_ring, exp_ring, pv_bank, A, Bk = bank[0:2], bank[2:4], bank[4:6], bank[6], bank[7]

        loaded_qkv = sem("loaded_qkv")
        loaded_rest, cross_cleared, cross_set = sem("loaded_rest"), sem("cross_cleared"), sem("cross_set")
        loaded_w, loaded_x, loaded_ctx = sem("loaded_w"), sem("loaded_x"), [sem("loaded_ctx0"), sem("loaded_ctx1")]
        cleared, consts_set, pool_consts = sem("cleared"), sem("consts_set"), sem("pool_consts")
        st_done = [sem(f"stats{i}_done") for i in range(3)]
        mv_done = [sem(f"mean_var{i}_done") for i in range(3)]
        ve_done = [sem(f"var_eps{i}_done") for i in range(3)]
        rstd_done = [sem(f"rstd{i}_done") for i in range(3)]
        xn_done = [sem(f"xn{i}_done") for i in range(3)]
        scores_in, scores_max = sem("scores_in"), sem("scores_max")
        exps_in, exps_done = sem("exps_in"), sem("exps_done")
        xT_in, xnT_done = sem("xT_in"), sem("xnT_done")
        qk_in, qk_full_done, qk_hi_done, qk_lo_done = sem("qk_in"), sem("qk_full_done"), sem("qk_hi_done"), sem("qk_lo_done")
        q_placed, k_placed = sem("q_placed"), sem("k_placed")
        v_in, v_done = sem("v_in"), sem("v_done")
        mT_in, max_hi_done, max_lo_done, max_placed = sem("mT_in"), sem("max_hi_done"), sem("max_lo_done"), sem("max_placed")
        pv_in, pv_copied, norm_in = sem("pv_in"), sem("pv_copied"), sem("norm_in")
        rsum_done, attn_done, attnT_in, attnT_done = sem("rsum_done"), sem("attn_done"), sem("attnT_in"), sem("attnT_done")
        wo_in, x_bo_done, x1_done = sem("wo_in"), sem("x_bo_done"), sem("x1_done")
        xqk_in, xqk_full_done, xqk_hi_done, xqk_lo_done = sem("xqk_in"), sem("xqk_full_done"), sem("xqk_hi_done"), sem("xqk_lo_done")
        xq_placed, xk_placed = sem("xq_placed"), sem("xk_placed")
        xmT_in, xmax_hi_done, xmax_lo_done, xmax_placed = sem("xmT_in"), sem("xmax_hi_done"), sem("xmax_lo_done"), sem("xmax_placed")
        xv_in, xv_done = sem("xv_in"), sem("xv_done")
        xpv_in = sem("xpv_in")
        xpv_copied = sem("xpv_copied")
        xnorm_in, xrsum_done, xattn_done = sem("xnorm_in"), sem("xrsum_done"), sem("xattn_done")
        xattnT_in, xattnT_done, y_in, x2_done = sem("xattnT_in"), sem("xattnT_done"), sem("y_in"), sem("x2_done")
        x3T_in, x3T_now_done, x3T_kept = sem("x3T_in"), sem("x3T_now_done"), sem("x3T_kept")
        logits_in, logits_done, neg_exp_done = sem("logits_in"), sem("logits_done"), sem("neg_exp_done")
        gate_steps = sem("gate_steps")
        root_done, gT_in, gatesT_done, gates_stored = sem("root_done"), sem("gT_in"), sem("gatesT_done"), sem("gates_stored")
        GATE_PARTS = (0, 1, 2, 4) + tuple(range(7, 20))
        GATE_STEPS, ROOT_STEPS = GATE_PARTS[-1], 4
        ones_stored = sem("ones_stored")
        passed = sem("passed")
        w_loaded = [sem("w_loaded0"), sem("w_loaded1")]
        groot_loaded = [sem("groot_loaded0"), sem("groot_loaded1")]
        w1_hi_done, w2_hi_done = sem("w1_hi_done"), sem("w2_hi_done")
        w1_split, w2_split = sem("w1_split"), sem("w2_split")
        x3_hi_done, x3_split = sem("x3_hi_done"), sem("x3_split")
        hidden_in, act1_done, act2_done, expert_added = sem("hidden_in"), sem("act1_done"), sem("act2_done"), sem("expert_added")
        act2_hi_done, act2_split = sem("act2_hi_done"), sem("act2_split")
        half_in, half_added, out_stored = sem("half_in"), sem("half_added"), sem("out_stored")

        def after(eng, s, batch, n=1, k=0, by=1):
            if isinstance(batch, int) and batch < 0:
                return
            eng.wait_ge(s, (batch * n + k + 1) * by)

        def after_alone(eng, s, batch, n=1, k=0, by=1):
            if isinstance(batch, int):
                after(eng, s, batch, n, k, by)
            else:
                after(eng, s, batch, n, k, by)
                eng.sem_inc(passed, 1)

        A_USES = [("x3T", x3T_now_done, 1, 0), ("xT", xnT_done, 1, 0), ("v", v_done, 1, 0),
                  ("norm", attn_done, 1, 0), ("wo", x1_done, 1, 0), ("xnorm0", xattn_done, 2, 0), ("gT", gatesT_done, 1, 0),
                  ("xattnT", xattnT_done, 1, 0), ("xv", xv_done, 1, 0)]
        B_USES = [("mT", max_lo_done, 1, 0), ("logits", logits_done, 1, 0), ("qk", qk_full_done, 1, 0),
                  ("attnT", attnT_done, 1, 0), ("xnorm1", xattn_done, 2, 1), ("xqk", xqk_full_done, 1, 0),
                  ("xmT", xmax_lo_done, 1, 0), ("y", x2_done, 1, 0)]
        used = [s.replace("xnorm ", "xnorm") for s in ORDER["PE"]]
        for uses in (A_USES, B_USES):
            uses.sort(key=lambda use: next(i for i, s in enumerate(used) if s.split()[0] == use[0]))

        def bank_free(eng, turn, uses, name):
            at = [u[0] for u in uses].index(name)
            order = [(u, 0) for u in reversed(uses[:at])] + [(u, 1) for u in reversed(uses)]
            for (use, s, n, k), back in order:
                stage = STAGE_OF[use.rstrip("01")]
                if turn.has(stage, back):
                    after(eng, s, turn.batch(stage, back), n, k)
                    return

        block = stack.enter_context(nc.Block())

        @block.sync
        def _(sp):
            sp.dma_start(xres[:, 0, :], x[0]).then_inc(loaded_x, 16)
            for dst, src in ((eye_sb[:], eye), (wqkv_sb[:], wqkv)):
                sp.dma_start(dst, src).then_inc(loaded_qkv, 16)
            for dst, src in ((qkb_sb[:], qk_bias), (vb_sb[:], v_bias), (wo_sb[:], wo), (bo_sb[:], bo),
                             (xw_sb[:], xw), (xqkb_sb[:], xqk_bias), (xvb_sb[:], xv_bias), (xbo_sb[:], xbo), (wr_sb[:], wr),
                             (br_sb[:], br)):
                sp.dma_start(dst, src).then_inc(loaded_w, 16)
            sp.dma_start(xres[:, 1:B, :], x[1:B].rearrange("b t d -> t b d")).then_inc(loaded_rest, 16)
            for i in range(2):
                sp.dma_start(ctx_sb[i][:], ctx_in[i]).then_inc(loaded_ctx[i], 16)
            for i in range(2):
                sp.dma_start(w_sb[i][:], experts[i]).then_inc(w_loaded[i], 16)

            def step(turn, name, n=0):
                b, side = turn.batch(STAGE_OF[name]), turn.side(STAGE_OF[name])
                if name == "k_rows":
                    if isinstance(b, int) and b < 2:
                        sp.wait_ge(consts_set, b + 1)
                    after_alone(sp, qk_lo_done, b)
                    after_alone(sp, pv_in, b - 2)
                    for c, ks in enumerate((qk_hi, qk_lo, qk_hi)):
                        for odd in range(2):
                            r = 32 * c + 16 * odd
                            sp.dma_start(K3[side][r:r + 16, :, :], ks[:, 2 + odd, :]).then_inc(k_placed, 16)
                elif name == "q_rows":
                    sp.dma_start(Q3[side][96:98], Q3[side][98:100]).then_inc(q_placed, 16)
                    for c, qs in enumerate((qk_hi, qk_hi, qk_lo)):
                        for odd in range(2):
                            r = 32 * c + 16 * odd
                            sp.dma_start(Q3[side][r:r + 16, :, odd, :], qs[:, odd, :]).then_inc(q_placed, 16)
                elif name == "max_rows":
                    after_alone(sp, max_hi_done, b)
                    sp.dma_start(Q3[side][96:97], max_hi[:]).then_inc(max_placed, 16)
                    after_alone(sp, max_lo_done, b)
                    sp.dma_start(Q3[side][97:98], max_lo[:]).then_inc(max_placed, 16)
                elif name == "xmax_rows":
                    after_alone(sp, xmax_hi_done, b)
                    sp.dma_start(XQ3[side][96:97], xmax_hi[:]).then_inc(xmax_placed, 16)
                    after_alone(sp, xmax_lo_done, b)
                    sp.dma_start(XQ3[side][97:98], xmax_lo[:]).then_inc(xmax_placed, 16)
                elif name == "xk_rows":
                    if isinstance(b, int) and b == 0:
                        sp.wait_ge(cross_set, 2)
                    after_alone(sp, xqk_lo_done, b)
                    after_alone(sp, xpv_in, b - 2, 4, 3)
                    for c, ks in enumerate((xqk_hi, xqk_lo, xqk_hi)):
                        sp.dma_start(XK3[side][32 * c:32 * c + 32, :, :], ks[:, 1, :]).then_inc(xk_placed, 16)
                elif name == "xq_rows":
                    sp.dma_start(XQ3[side][96:98], XQ3[side][98:100]).then_inc(xq_placed, 16)
                    for c, qs in enumerate((xqk_hi, xqk_hi, xqk_lo)):
                        for hh in range(4):
                            r = 32 * c + 8 * hh
                            sp.dma_start(XQ3[side][r:r + 8, :, hh, :],
                                         qs[32 * hh:32 * hh + 32, 0, :]).then_inc(xq_placed, 16)
                elif name == "xv" and not (isinstance(b, int) and b + 2 >= B):
                    after_alone(sp, xv_in, b)
                    sp.dma_start(ctx_sb[side][:], ctx_in[b + 2]).then_inc(loaded_ctx[side], 16)
                elif name == "gT":
                    after_alone(sp, gatesT_done, b)
                    sp.dma_start(gates_dram[0:E, bass.ds(b * T, T)], gatesT[:]).then_inc(gates_stored, 16)

            def load_weights(j, it):
                for side in range(2):
                    sp.wait_ge(w2_split, it * 2 - 1 + side)
                    sp.sem_inc(passed, 1)
                    sp.dma_start(w_sb[side][:], experts[j * 2 + side]).then_inc(w_loaded[side], 16)

            def load_roots(j, half, it):
                for side in range(2):
                    if not (isinstance(it, int) and it == 0):
                        sp.wait_ge(act1_done, it * 4 - 2 + 2 * side)
                        sp.sem_inc(passed, 1)
                    row = gates_dram[bass.ds(j * 2 + side, 1), 1024 * half:1024 * half + 1024]
                    sp.dma_start(probs[:, 8 * side:8 * side + 8, :].rearrange("p h t -> p (h t)"),
                                 row.to_broadcast([P, 1024])).then_inc(groot_loaded[side], 16)

            def store(half):
                for i in range(8 * half, 8 * half + 8, 2):
                    sp.wait_ge(half_added, i + 2)
                    sp.dma_start(out[i:i + 2].rearrange("b t d -> t b d"), xres[:, i:i + 2, :]).then_inc(out_stored, 16)

            for turn in turns(sp):
                if isinstance(turn.it, int) and turn.it == last - 1:
                    sp.wait_ge(gates_stored, B // 2 * 16)
                    sp.wait_ge(ones_stored, 16)
                    sp.wait_ge(pv_in, B)
                    load_roots(0, 0, 0)
                for name, n in turn.steps("SP"):
                    step(turn, name, n)
            for k, turn in enumerate(late):
                with sp.Fori(ROUTED * k + 1, ROUTED * k + ROUTED + 1) as j:
                    load_weights(j, j)
                    load_roots(j, 0, j)
                step(turn, "gT")
            with sp.Fori(ROUTED * LATE + 1, NE // 2) as j:
                load_weights(j, j)
                load_roots(j, 0, j)
            sp.wait_ge(gates_stored, B * 16)
            with sp.Fori(0, 2) as j:
                load_weights(j, j + NE // 2)
                load_roots(j, 1, j + NE // 2)
            store(0)
            with sp.Fori(2, NE // 2) as j:
                load_weights(j, j + NE // 2)
                load_roots(j, 1, j + NE // 2)
            store(1)
            sp.wait_ge(out_stored, 16 * B // 2)

        @block.gpsimd
        def _(pool):
            nc.gpsimd.memset(exponents[:, 0:E], 0.5)
            nc.gpsimd.memset(exponents[:, E:E + 1], -0.5)
            nc.gpsimd.memset(ones[:], 1.0).then_inc(pool_consts, 1)
            def clear(i):
                nc.gpsimd.memset(XQ3[i][:], 0.0)
                nc.gpsimd.memset(XV1[i][:], 0.0).then_inc(cross_cleared, 1)
                pool.wait_ge(cross_cleared, i + 1)
                nc.gpsimd.memset(XV1[i][:, :, :, XH:XH + 1], 1.0).then_inc(cross_set, 1)

            clear(0)
            def step(turn, name, n=0):
                b, side = turn.batch(STAGE_OF[name]), turn.side(STAGE_OF[name])
                if name in ("ln1a", "ln2a", "ln3a"):
                    i = int(name[2]) - 1
                    after_alone(pool, mv_done[i], b)
                    nc.gpsimd.tensor_scalar(var_eps[i][:], mean_var[i][:, 1:2], EPS, None, ALU.add).then_inc(ve_done[i], 1)
                    after(pool, ve_done[i], b)
                    nc.gpsimd.tensor_tensor(rstd[i][:], var_eps[i][:], exponents[:, E:E + 1],
                                            ALU.pow).then_inc(rstd_done[i], 1)
                elif name == "qk":
                    after(pool, qk_hi_done, b)
                    after(pool, q_placed, b - 1, 7, 6, 16)
                    after(pool, k_placed, b - 1, 6, 5, 16)
                    nc.gpsimd.tensor_tensor(qk_lo[:].bitcast(F32R), qk_full[:], qk_hi[:], ALU.subtract).then_inc(qk_lo_done, 1)
                elif name == "x_bo":
                    if isinstance(b, int):
                        pool.wait_ge(loaded_w, 10 * 16)
                        if b > 0:
                            pool.wait_ge(loaded_rest, 16)
                    after(pool, x1_done, b - 1)
                    nc.gpsimd.tensor_tensor(x_bo[:], xres[:, b, :], bo_sb[:], ALU.add).then_inc(x_bo_done, 1)
                elif name == "xqk":
                    after(pool, xqk_hi_done, b)
                    after(pool, xq_placed, b - 1, 13, 12, 16)
                    after(pool, xk_placed, b - 1, 3, 2, 16)
                    nc.gpsimd.tensor_tensor(xqk_lo[:].bitcast(F32R), xqk_full[:], xqk_hi[:],
                                            ALU.subtract).then_inc(xqk_lo_done, 1)
                elif name == "x3T":
                    after(pool, x3T_now_done, b)
                    nc.gpsimd.tensor_copy(x3T[:, :, bass.ds(b * T, T)], x3T_now[:]).then_inc(x3T_kept, 1)
                elif name == "root":
                    if n == 0:
                        after(pool, gate_steps, b, GATE_STEPS, GATE_STEPS - 1)
                        after(pool, gT_in, b - 1)
                    at = slice(n * E // ROOT_STEPS, (n + 1) * E // ROOT_STEPS)
                    nc.gpsimd.tensor_tensor(root_gates[:, at], gates[:, at], exponents[:, at], ALU.pow).then_inc(root_done, 1)

            def split(it, roots=None, sides=range(2)):
                for side in sides:
                    first = isinstance(it, int) and it == 0
                    e = 2 * it + side
                    for w, (hi_done, split_done) in enumerate(((w1_hi_done, w1_split), (w2_hi_done, w2_split))):
                        at = slice(2 * w, 2 * w + 2)
                        if w == 0:
                            pool.wait_ge(w_loaded[side], (it + 1) * 16)
                        if not first:
                            pool.wait_ge((hidden_in, expert_added)[w], 4 * it - 2 + 2 * side)
                            pool.sem_inc(passed, 1)
                        nc.gpsimd.tensor_copy(w_hi[side][:, at].bitcast(F32R), w_sb[side][:, at]).then_inc(hi_done, 1)
                        pool.wait_ge(hi_done, e + 1)
                        nc.gpsimd.tensor_tensor(w_lo[side][:, at].bitcast(F32R), w_sb[side][:, at], w_hi[side][:, at],
                                                ALU.subtract).then_inc(split_done, 1)
                        if roots:
                            step(roots, "root", 2 * side + w)

            for turn in turns(pool):
                for name, n in turn.steps("Pool"):
                    step(turn, name, n)
                    if isinstance(turn.it, int) and turn.it == last - 1 and name == "x3T":
                        pool.wait_ge(pv_in, B)
                        split(0, sides=(0,))
                    if isinstance(turn.it, int) and turn.it == 0 and name == "ln1a":
                        clear(1)
                        pool.wait_ge(pool_consts, 1)
                        pool.dma_start(gates_dram[E:NE, :].rearrange("e (a t) -> (e a) t", a=64 // (NE - E)), ones[:]).then_inc(ones_stored, 16)
            split(0, sides=(1,))
            step(late[0], "ln3a")
            split(1)
            step(late[0], "x3T")
            step(late[1], "ln3a")
            with pool.Fori(2, ROUTED - 1) as it:
                split(it)
            split(ROUTED - 1, roots=late[0])
            with pool.Fori(ROUTED, ROUTED + 2) as it:
                split(it)
            step(late[1], "x3T")
            with pool.Fori(ROUTED + 2, 2 * ROUTED - 1) as it:
                split(it)
            split(2 * ROUTED - 1, roots=late[1])
            with pool.Fori(2 * ROUTED, NE) as it:
                split(it)

        @block.scalar
        def _(act):
            nc.scalar.preload_act_table(ACT.Exp)

            def step(turn, name, n=0):
                b, side = turn.batch(STAGE_OF[name]), turn.side(STAGE_OF[name])
                if name == "xT":
                    after(act, xT_in, b)
                    after(act, v_in, b - 1)
                    nc.scalar.copy(xnT[:], A[:, 0:2 * T].rearrange("p (c t) -> p c t", c=2)).then_inc(xnT_done, 1)
                elif name == "qk":
                    after(act, qk_full_done, b)
                    after(act, qk_lo_done, b - 1)
                    after(act, q_placed, b - 1, 7, 6, 16)
                    after(act, k_placed, b - 1, 6, 5, 16)
                    nc.scalar.copy(qk_hi[:].bitcast(F32R), qk_full[:]).then_inc(qk_hi_done, 1)
                elif name == "v":
                    after(act, v_in, b)
                    after(act, pv_in, b - 2)
                    if isinstance(b, int) and b < 2:
                        act.wait_ge(consts_set, b + 1)
                    nc.scalar.copy(V1[side][:, :, 0:HD], A[:, 0:D].rearrange("p (h d) -> p h d", h=H)).then_inc(v_done, 1)
                elif name == "mT":
                    after(act, mT_in, b)
                    after(act, max_placed, b - 1, 2, 1, 16)
                    nc.scalar.copy(max_hi[:].bitcast(F32R), Bk[0:H, 0:T]).then_inc(max_hi_done, 1)
                elif name == "p2":
                    slot, k = ring(turn, EXPS, name, n)
                    act.wait_ge(exps_in, k)
                    if n == 0:
                        after(act, pv_in, b - 1)
                    nc.scalar.activation(probs[:, 4 * n:4 * n + 4, :], exp_ring[slot][:]
                                         .rearrange("p (h t) -> p h t", h=4), ACT.Exp, scale=SCALE).then_inc(exps_done, 1)
                elif name == "x2c":
                    g, kt, pair = n // 4, n // 2 % 2, n % 2
                    slot, k = ring(turn, EXPS, name, n)
                    act.wait_ge(exps_in, k)
                    if n % 4 == 0:
                        after(act, xpv_in, b - 1, 4, g)
                    h = 4 * g + 2 * pair
                    nc.scalar.activation(xprobs[:, kt, h:h + 2, :], exp_ring[slot][:]
                                         .rearrange("p (h t) -> p h t", h=2), ACT.Exp, scale=XSCALE).then_inc(exps_done, 1)
                elif name == "pv":
                    after(act, pv_in, b)
                    after(act, norm_in, b - 1)
                    nc.scalar.copy(pv_sb[:], pv_bank[0][:].rearrange("p (g t) -> p g t", g=4)).then_inc(pv_copied, 1)
                elif name == "xpv" and n % 2:
                    after(act, xpv_in, b, 4, n)
                    after(act, xnorm_in, b - 1, 2, 1)
                    nc.scalar.copy(xpv_sb[:, n - 1:n + 1, :], pv_bank[n // 2][:].rearrange("p (g t) -> p g t", g=2))\
                      .then_inc(xpv_copied, 1)
                elif name == "xqk":
                    after(act, xqk_full_done, b)
                    after(act, xqk_lo_done, b - 1)
                    after(act, xq_placed, b - 1, 13, 12, 16)
                    after(act, xk_placed, b - 1, 3, 2, 16)
                    nc.scalar.copy(xqk_hi[:].bitcast(F32R), xqk_full[:]).then_inc(xqk_hi_done, 1)
                elif name == "xmT":
                    after(act, xmT_in, b)
                    after(act, xmax_placed, b - 1, 2, 1, 16)
                    nc.scalar.copy(xmax_hi[:].bitcast(F32R), Bk[0:H, 0:D]).then_inc(xmax_hi_done, 1)
                elif name == "xattnT":
                    after(act, xattnT_in, b)
                    after(act, y_in, b - 1)
                    nc.scalar.activation(xattnT[:], A[:, 0:D], ACT.Identity, bias=xvb_sb[:, 0:1]).then_inc(xattnT_done, 1)
                elif name == "xv":
                    after(act, xv_in, b)
                    after(act, xpv_in, b - 2, 4, 3)
                    if isinstance(b, int) and b == 0:
                        act.wait_ge(cross_set, 2)
                    nc.scalar.copy(XV1[side][:, :, :, 0:XH], A[:, 0:D].rearrange("p (k h d) -> p k h d", k=NX, h=H))\
                      .then_inc(xv_done, 1)
                elif name == "x3T":
                    after(act, x3T_in, b)
                    after(act, x3T_kept, b - 1)
                    after(act, logits_in, b - 1)
                    nc.scalar.copy(x3T_now[:], A[:, 0:2 * T].rearrange("p (c t) -> p c t", c=2)).then_inc(x3T_now_done, 1)
                elif name == "logits":
                    after(act, logits_done, b)
                    nc.scalar.activation(neg_exp[:], logits[:], ACT.Exp, scale=-1.0).then_inc(neg_exp_done, 1)
                elif name == "gT":
                    after(act, gT_in, b)
                    after(act, gates_stored, b - 1, 1, 0, 16)
                    nc.scalar.copy(gatesT[:], A[0:E, 0:T]).then_inc(gatesT_done, 1)

            def split_input(block):
                act.wait_ge(x3T_kept, 4 * block + 4)
                at = slice(block * 512, block * 512 + 512)
                nc.scalar.copy(x3_hi[:, :, at].bitcast(F32R), x3T[:, :, at]).then_inc(x3_hi_done, 1)

            def squares(it):
                for u in range(4):
                    act.wait_ge(act1_done, it * 4 + u + 1)
                    if not (isinstance(it, int) and it == 0):
                        act.wait_ge(expert_added, it * 4 + u - 3)
                    nc.scalar.activation(act2_hi[u].bitcast(F32R), act1[u], ACT.Square).then_inc(act2_hi_done, 1)
                    nc.scalar.activation(act2[u], act1[u], ACT.Square).then_inc(act2_done, 1)

            for turn in turns(act):
                if isinstance(turn.it, int) and turn.it == last:
                    act.wait_ge(xpv_in, 4 * B - 4)
                    for block in range(3):
                        split_input(block)
                for name, n in turn.steps("ACT"):
                    step(turn, name, n)
            for k, turn in enumerate(late):
                squares(ROUTED * k)
                step(turn, "x3T")
                squares(ROUTED * k + 1)
                step(turn, "logits")
                with act.Fori(ROUTED * k + 2, ROUTED * k + ROUTED) as it:
                    squares(it)
                step(turn, "gT")
            split_input(3)
            with act.Fori(ROUTED * LATE, NE) as it:
                squares(it)

        @block.vector
        def _(dve):
            def clear(i):
                nc.vector.memset(Q3[i][:], 0.0)
                nc.vector.memset(K3[i][96:P], 1.0)
                nc.vector.memset(V1[i][:], 0.0).then_inc(cleared, 1)
                if i == 1:
                    for j in range(2):
                        nc.vector.memset(XK3[j][96:P], 1.0)
                    nc.vector.memset(zeros[:], 0.0)
                    for c in range(4):
                        nc.vector.memset(group_w[:, c:c + 1], 9.0 - c)
                    nc.vector.memset(masked[:, 0:1], 9.0)
                    nc.vector.memset(masked[:, 1:2], 8.0)
                dve.wait_ge(cleared, i + 1)
                nc.vector.memset(V1[i][:, :, HD:HD + 1], 1.0).then_inc(consts_set, 1)

            def norm_rows(i, b):
                after(dve, rstd_done[i], b)
                nc.vector.tensor_scalar(xn[i][:], xres[:, b, :], mean_var[i][:, 0:1], rstd[i][:], ALU.subtract,
                                        ALU.mult).then_inc(xn_done[i], 1)

            def choose_experts(b, n):
                taken = 0

                def then(ins):
                    nonlocal taken
                    ins.then_inc(gate_steps, 1)
                    taken += 1

                if n == 0:
                    after(dve, neg_exp_done, b)
                elif n in (6, 7, 9, 10):
                    after_alone(dve, gate_steps, b, GATE_STEPS, GATE_PARTS[n] - 1)
                else:
                    after(dve, gate_steps, b, GATE_STEPS, GATE_PARTS[n] - 1)
                if n == 0:
                    then(nc.vector.tensor_scalar(one_plus[:], neg_exp[:], 1.0, None, ALU.add))
                elif n == 1:
                    then(nc.vector.reciprocal(sig[:], one_plus[:]))
                elif n == 2:
                    sg = sig[:].rearrange("p (g a c) -> p g a c", g=8, a=2)
                    then(nc.vector.tensor_tensor(pair_max[:], sg[:, :, :, 0], sg[:, :, :, 1], ALU.max))
                    then(nc.vector.tensor_tensor(pair_min[:], sg[:, :, :, 0], sg[:, :, :, 1], ALU.min))
                elif n == 3:
                    then(nc.vector.tensor_tensor(top1[:], pair_max[:, :, 0], pair_max[:, :, 1], ALU.max))
                    then(nc.vector.tensor_tensor(top2a[:], pair_max[:, :, 0], pair_max[:, :, 1], ALU.min))
                    then(nc.vector.tensor_tensor(top2b[:], pair_min[:, :, 0], pair_min[:, :, 1], ALU.max))
                elif n == 4:
                    then(nc.vector.tensor_tensor(top2[:], top2a[:], top2b[:], ALU.max))
                elif n == 5:
                    then(nc.vector.tensor_tensor(group_w[:, 4:12], top1[:], top2[:], ALU.add))
                elif n == 6:
                    then(nc.vector.max(top_groups[:], group_w[:]))
                elif n == 7:
                    then(nc.vector.match_replace(groups_marked[:], top_groups[:], group_w[:], -1.0))
                elif n == 8:
                    then(nc.vector.scalar_tensor_tensor(
                        out=masked[:, 2:2 + E].rearrange("p (g a) -> p g a", g=8),
                        in0=groups_marked[:, 4:12].unsqueeze(2).to_broadcast([P, 8, 4]), scalar=-1.0,
                        in1=sig[:].rearrange("p (g a) -> p g a", g=8), op0=ALU.is_equal, op1=ALU.mult))
                elif n == 9:
                    then(nc.vector.max(top_experts[:], masked[:]))
                elif n == 10:
                    then(nc.vector.match_replace(experts_marked[:], top_experts[:], masked[:], -1.0))
                elif n == 11:
                    then(nc.vector.scalar_tensor_tensor(out=chosen[:], in0=experts_marked[:, 2:2 + E], scalar=-1.0,
                                                        in1=sig[:], op0=ALU.is_equal, op1=ALU.mult))
                elif n == 12:
                    then(nc.vector.tensor_reduce(total[:], chosen[:], AX.X, ALU.add))
                elif n == 13:
                    then(nc.vector.tensor_scalar(total_eps[:], total[:], 1e-20, None, ALU.add))
                elif n == 14:
                    then(nc.vector.reciprocal(inv_total[:], total_eps[:]))
                else:
                    after(dve, root_done, b - 1, ROOT_STEPS, ROOT_STEPS - 1)
                    then(nc.vector.tensor_scalar(gates[:], chosen[:], inv_total[:], ROUTED_SCALE, ALU.mult, ALU.mult))
                assert taken == GATE_PARTS[n + 1] - GATE_PARTS[n]

            def step(turn, name, n=0):
                b, side = turn.batch(STAGE_OF[name]), turn.side(STAGE_OF[name])
                if name in ("ln1s", "ln2s", "ln3s"):
                    i = int(name[2]) - 1
                    if i == 0 and isinstance(b, int):
                        dve.wait_ge(loaded_x, 16)
                        if b > 0:
                            dve.wait_ge(loaded_rest, 16)
                    if i > 0:
                        after_alone(dve, (x1_done, x2_done)[i - 1], b)
                    after_alone(dve, mv_done[i], b - 1)
                    nc.vector.bn_stats(stats[i][:], xres[:, b, :]).then_inc(st_done[i], 1)
                elif name in ("ln1a", "ln2a", "ln3a"):
                    i = int(name[2]) - 1
                    after_alone(dve, st_done[i], b)
                    nc.vector.bn_aggr(mean_var[i][:], stats[i][:]).then_inc(mv_done[i], 1)
                elif name in ("ln1b", "ln2b", "ln3b"):
                    after(dve, {"ln1b": xT_in, "ln2b": xqk_in, "ln3b": x3T_in}[name], b - 1)
                    norm_rows(int(name[2]) - 1, b)
                elif name == "qk":
                    if isinstance(b, int):
                        dve.wait_ge(loaded_w, 10 * 16)
                    after(dve, qk_in, b)
                    after(dve, qk_lo_done, b - 1)
                    nc.vector.tensor_tensor(qk_full[:], Bk[:].rearrange("p (c t) -> p c t", c=4),
                                            qkb_sb[:].unsqueeze(2).to_broadcast([P, 4, T]), ALU.add).then_inc(qk_full_done, 1)
                elif name in SCORES:
                    slot, k = ring(turn, SCORES, name, n)
                    dve.wait_ge(scores_in, k)
                    scores = score_ring[slot][:].rearrange("p (c t) -> p c t", c=2)
                    if name == "p1":
                        if n == 0:
                            after(dve, mT_in, b - 1)
                        to = negmax[:, 2 * n:2 * n + 2]
                        at = n - min(n, 6)
                        scores = scores[:, :, at * T:(at + 1) * T]
                    else:
                        if n == 0:
                            after(dve, xmT_in, b - 1)
                        to = xnegmax[:, :, n]
                    nc.vector.tensor_reduce(to, scores, AX.X, ALU.max, negate=True).then_inc(scores_max, 1)
                elif name == "mT":
                    after(dve, max_hi_done, b)
                    after(dve, max_placed, b - 1, 2, 1, 16)
                    nc.vector.tensor_tensor(max_lo[:].bitcast(F32R), Bk[0:H, 0:T], max_hi[:], ALU.subtract)\
                      .then_inc(max_lo_done, 1)
                elif name == "rsum":
                    after(dve, norm_in, b)
                    a = A[:].rearrange("p (h c) -> p h c", h=H)
                    after(dve, attn_done, b - 1)
                    nc.vector.reciprocal(rsum[:].unsqueeze(2), a[:, :, HD:HD + 1]).then_inc(rsum_done, 1)
                elif name == "norm":
                    a = A[:].rearrange("p (h c) -> p h c", h=H)
                    after(dve, rsum_done, b)
                    after(dve, attnT_in, b - 1)
                    nc.vector.tensor_tensor(attn[:].rearrange("p (h d) -> p h d", h=H), a[:, :, 0:HD],
                                            rsum[:].unsqueeze(2).to_broadcast([P, H, HD]), ALU.mult).then_inc(attn_done, 1)
                elif name == "attnT":
                    after(dve, attnT_in, b)
                    after(dve, wo_in, b - 1)
                    nc.vector.tensor_tensor(attnT[:], Bk[:, 0:D].rearrange("p (c t) -> p c t", c=2),
                                            vb_sb[:].unsqueeze(2).to_broadcast([P, 2, T]), ALU.add).then_inc(attnT_done, 1)
                elif name == "wo":
                    after(dve, wo_in, b)
                    after(dve, x_bo_done, b)
                    nc.vector.tensor_tensor(xres[:, b, :], A[:, 0:D], x_bo[:], ALU.add).then_inc(x1_done, 1)
                elif name == "xqk":
                    after(dve, xqk_in, b)
                    after(dve, xqk_lo_done, b - 1)
                    nc.vector.tensor_tensor(xqk_full[:], Bk[:].rearrange("p (c t) -> p c t", c=2),
                                            xqkb_sb[:].unsqueeze(2).to_broadcast([P, 2, D]), ALU.add).then_inc(xqk_full_done, 1)
                elif name == "xmT":
                    after(dve, xmax_hi_done, b)
                    after(dve, xmax_placed, b - 1, 2, 1, 16)
                    nc.vector.tensor_tensor(xmax_lo[:].bitcast(F32R), Bk[0:H, 0:D], xmax_hi[:], ALU.subtract)\
                      .then_inc(xmax_lo_done, 1)
                elif name == "xrsum":
                    after(dve, xnorm_in, b, 2, n)
                    a = (A, Bk)[n][:].rearrange("p (h c) -> p h c", h=H)
                    after(dve, xattn_done, b - 1, 2, n)
                    nc.vector.reciprocal(xrsum[:, n, :].unsqueeze(2), a[:, :, XH:XH + 1]).then_inc(xrsum_done, 1)
                elif name == "xnorm":
                    a = (A, Bk)[n][:].rearrange("p (h c) -> p h c", h=H)
                    after(dve, xrsum_done, b, 2, n)
                    after(dve, xattnT_in, b - 1)
                    nc.vector.tensor_tensor(xattn[:, n, :].rearrange("p (h d) -> p h d", h=H), a[:, :, 0:XH],
                                            xrsum[:, n, :].unsqueeze(2).to_broadcast([P, H, XH]), ALU.mult)\
                      .then_inc(xattn_done, 1)
                elif name == "y":
                    after(dve, y_in, b)
                    nc.vector.scalar_tensor_tensor(out=xres[:, b, :], in0=Bk[:, 0:D], scalar=xbo_sb[:, 0:1],
                                                   in1=xres[:, b, :], op0=ALU.add, op1=ALU.add).then_inc(x2_done, 1)
                elif name == "logits":
                    after(dve, logits_in, b)
                    after(dve, neg_exp_done, b - 1)
                    nc.vector.tensor_tensor(logits[:], Bk[:, 0:E], br_sb[:], ALU.add).then_inc(logits_done, 1)
                elif name == "gates":
                    choose_experts(b, n)

            def split_input(block):
                at = slice(block * 512, block * 512 + 512)
                dve.wait_ge(x3_hi_done, block + 1)
                nc.vector.tensor_tensor(x3_lo[:, :, at].bitcast(F32R), x3T[:, :, at], x3_hi[:, :, at], ALU.subtract)\
                  .then_inc(x3_split, 1)

            def gated_relu(it, u):
                side, blk = u // 2, u % 2
                if blk == 0:
                    dve.wait_ge(groot_loaded[side], (it + 1) * 16)
                dve.wait_ge(hidden_in, it * 4 + u + 1)
                if not (isinstance(it, int) and it == 0):
                    dve.wait_ge(act2_done, it * 4 + u - 3)
                nc.vector.scalar_tensor_tensor(out=act1[u], in0=bank[4 + u][:], scalar=0.0, in1=groot[side][:, blk, :],
                                               op0=ALU.max, op1=ALU.mult).then_inc(act1_done, 1)

            def add_half(half, tiles=range(8)):
                dve.wait_ge(half_in, half + 1)
                for t in tiles:
                    nc.vector.tensor_tensor(xres[:, 8 * half + t, :], bank[t // 2][:, (t % 2) * D:(t % 2 + 1) * D],
                                            xres[:, 8 * half + t, :], ALU.add).then_inc(half_added, 1)

            def elementwise(it, more=True, turn=None, gates=(), add=False):
                for u in range(4):
                    for part in gates[u * len(gates) // 4:(u + 1) * len(gates) // 4]:
                        step(turn, "gates", part)
                    if u < 3:
                        gated_relu(it, u + 1)
                    elif more:
                        gated_relu(it + 1, 0)
                    dve.wait_ge(act2_done, it * 4 + u + 1)
                    if not (isinstance(it, int) and it == 0):
                        dve.wait_ge(expert_added, it * 4 + u - 3)
                    dve.wait_ge(act2_hi_done, it * 4 + u + 1)
                    nc.vector.tensor_tensor(act2_lo[u].bitcast(F32R), act2[u], act2_hi[u], ALU.subtract).then_inc(act2_split, 1)
                    if add and u < 2:
                        add_half(0, range(4 * u, 4 * u + 4))

            for turn in turns(dve):
                for name, n in turn.steps("DVE"):
                    step(turn, name, n)
                    if isinstance(turn.it, int) and turn.it == 0 and name == "ln1b":
                        clear(0)
                    if isinstance(turn.it, int) and turn.it == last and (name, n) == ("xnorm", 1):
                        dve.wait_ge(xpv_in, 4 * B)
                        split_input(0)
                        split_input(1)
                if isinstance(turn.it, int) and turn.it == 0:
                    clear(1)
            step(late[0], "ln3s")
            gated_relu(0, 0)
            step(late[0], "ln3a")
            step(late[0], "ln3b")
            elementwise(0)
            step(late[1], "ln3s")
            step(late[1], "ln3a")
            split_input(2)
            elementwise(1)
            step(late[0], "logits")
            step(late[1], "ln3b")
            elementwise(2, turn=late[0], gates=range(0, 8))
            elementwise(3, turn=late[0], gates=range(8, 16))
            with dve.Fori(4, ROUTED + 2) as it:
                elementwise(it)
            step(late[1], "logits")
            elementwise(ROUTED + 2, turn=late[1], gates=range(0, 8))
            elementwise(ROUTED + 3, turn=late[1], gates=range(8, 16))
            with dve.Fori(ROUTED + 4, 2 * ROUTED) as it:
                elementwise(it)
            split_input(3)
            with dve.Fori(2 * ROUTED, NE // 2) as it:
                elementwise(it)
            elementwise(NE // 2, add=True)
            with dve.Fori(NE // 2 + 1, NE - 1) as it:
                elementwise(it)
            elementwise(NE - 1, more=False)
            add_half(1)

        @block.tensor
        def _(pe):
            def r(ap):
                return ap.bitcast(F32R)

            def ring_slot(turn, kinds, name, n, read):
                slot, k = ring(turn, kinds, name, n)
                if not isinstance(k, int) or k > 2:
                    pe.wait_ge(read, k - 2)
                return slot

            pe.wait_ge(loaded_qkv, 32)

            def step(turn, name, n=0):
                b, side = turn.batch(STAGE_OF[name]), turn.side(STAGE_OF[name])
                if name == "p1":
                    if n == 0:
                        after(pe, q_placed, b, 7, 6, 16)
                        after(pe, k_placed, b, 6, 5, 16)
                    slot = ring_slot(turn, SCORES, name, n, scores_max)
                    g = min(n, 6)
                    for odd in range(2):
                        mm = pe.matmul(score_ring[slot][:, odd * 2 * T:(odd + 1) * 2 * T], r(Q3[side][:, n, odd, :]),
                                       r(K3[side][:, g:g + 2, :]), start=True, stop=True)
                    mm.then_inc(scores_in, 1)
                elif name == "p2":
                    if n == 0:
                        after(pe, max_placed, b, 2, 1, 16)
                    slot = ring_slot(turn, EXPS, name, n, exps_done)
                    for i in range(2):
                        g = 2 * n + i
                        mm = pe.matmul(exp_ring[slot][:, i * 2 * T:(i + 1) * 2 * T], r(K3[side][:, g, :]),
                                       r(Q3[side][:, g, :, :]), start=True, stop=True)
                    mm.then_inc(exps_in, 1)
                elif name == "x1c":
                    if n == 0:
                        after(pe, xq_placed, b, 13, 12, 16)
                        after(pe, xk_placed, b, 3, 2, 16)
                    slot = ring_slot(turn, SCORES, name, n, scores_max)
                    for qt in range(NX):
                        mm = pe.matmul(score_ring[slot][:, qt * D:(qt + 1) * D],
                                       r(XQ3[side][:, n // 4, n % 4, qt * P:(qt + 1) * P]),
                                       r(XK3[side][:, n // 4, :]), start=True, stop=True)
                    mm.then_inc(scores_in, 1)
                elif name == "x2c":
                    if n == 0:
                        after(pe, xmax_placed, b, 2, 1, 16)
                    g, kt, pair = n // 4, n // 2 % 2, n % 2
                    slot = ring_slot(turn, EXPS, name, n, exps_done)
                    pe.matmul(exp_ring[slot][:], r(XK3[side][:, g, kt * P:(kt + 1) * P]),
                              r(XQ3[side][:, g, 2 * pair:2 * pair + 2, :]), start=True, stop=True).then_inc(exps_in, 1)
                elif name == "xT":
                    after(pe, xn_done[0], b)
                    bank_free(pe, turn, A_USES, "xT")
                    for c in range(2):
                        mm = pe.transpose(A[:, c * T:(c + 1) * T], xn[0][:, c * P:(c + 1) * P], eye_sb[:])
                    mm.then_inc(xT_in, 1)
                elif name == "qk":
                    if n == 0:
                        after(pe, xnT_done, b)
                        bank_free(pe, turn, B_USES, "qk")
                    for c in range(2):
                        mm = pe.matmul(Bk[:, n * T:(n + 1) * T], wqkv_sb[:, c, n, :], xnT[:, c, :],
                                       start=(c == 0), stop=(c == 1))
                    if n == 3:
                        mm.then_inc(qk_in, 1)
                elif name == "v":
                    bank_free(pe, turn, A_USES, "v")
                    for c in range(2):
                        mm = pe.matmul(A[:, 0:D], xnT[:, c, :], wqkv_sb[:, c, 4:6, :], start=(c == 0), stop=(c == 1))
                    mm.then_inc(v_in, 1)
                elif name == "mT":
                    pe.wait_ge(scores_max, ring(turn, SCORES, "p1", 7)[1])
                    bank_free(pe, turn, B_USES, "mT")
                    pe.transpose(Bk[0:H, 0:T], negmax[:], eye_sb[:]).then_inc(mT_in, 1)
                elif name == "pv":
                    pe.wait_ge(exps_done, ring(turn, EXPS, "p2", n)[1])
                    if n == 0:
                        after(pe, v_done, b)
                        after(pe, pv_copied, b - 1)
                        if turn.has("X2"):
                            after(pe, xpv_copied, turn.batch("X2"), 2, 0)
                        else:
                            after(pe, xpv_copied, min(turn.batch("X2"), B - 1), 2, 0)
                    for j in range(4):
                        h = 4 * n + j
                        mm = pe.matmul(pv_bank[0][32 * j:32 * j + 32, n * T:(n + 1) * T], V1[side][:, h, :],
                                       probs[:, h, :], start=True, stop=True)
                    if n == 3:
                        mm.then_inc(pv_in, 1)
                elif name == "norm":
                    after(pe, pv_copied, b)
                    bank_free(pe, turn, A_USES, "norm")
                    for g in range(4):
                        mm = pe.transpose(A[:, g * P:(g + 1) * P], pv_sb[:, g, :], eye_sb[:])
                    mm.then_inc(norm_in, 1)
                elif name == "attnT":
                    after(pe, attn_done, b)
                    bank_free(pe, turn, B_USES, "attnT")
                    for c in range(2):
                        mm = pe.transpose(Bk[:, c * T:(c + 1) * T], attn[:, c * P:(c + 1) * P], eye_sb[:])
                    mm.then_inc(attnT_in, 1)
                elif name == "wo":
                    after(pe, attnT_done, b)
                    bank_free(pe, turn, A_USES, "wo")
                    for c in range(2):
                        mm = pe.matmul(A[:, 0:D], attnT[:, c, :], wo_sb[:, c, :], start=(c == 0), stop=(c == 1))
                    mm.then_inc(wo_in, 1)
                elif name == "xqk":
                    after(pe, xn_done[1], b)
                    pe.wait_ge(loaded_ctx[side], (turn.earlier_on_side("SB") + 1) * 16)
                    bank_free(pe, turn, B_USES, "xqk")
                    pe.matmul(Bk[:, 0:D], xw_sb[:, 0, :], xn[1][:], start=True, stop=True)
                    pe.matmul(Bk[:, D:2 * D], xw_sb[:, 1, :], ctx_sb[side][:], start=True, stop=True).then_inc(xqk_in, 1)
                elif name == "xv":
                    bank_free(pe, turn, A_USES, "xv")
                    for kt in range(NX):
                        mm = pe.matmul(A[:, kt * P:(kt + 1) * P], ctx_sb[side][:, kt * P:(kt + 1) * P], xw_sb[:, 2, :],
                                       start=True, stop=True)
                    mm.then_inc(xv_in, 1)
                elif name == "xmT":
                    pe.wait_ge(scores_max, ring(turn, SCORES, "x1c", 15)[1])
                    bank_free(pe, turn, B_USES, "xmT")
                    for qt in range(NX):
                        mm = pe.transpose(Bk[0:H, qt * P:(qt + 1) * P], xnegmax[:, qt, :], eye_sb[:])
                    mm.then_inc(xmT_in, 1)
                elif name == "xpv":
                    pe.wait_ge(exps_done, ring(turn, EXPS, "x2c", 4 * n + 3)[1])
                    if n == 0:
                        after(pe, xv_done, b)
                        if not isinstance(b, int) or 0 <= turn.batch("SB", 1) < B:
                            after(pe, pv_copied, turn.batch("SB", 1))
                        after(pe, xpv_copied, b - 1, 2, 0)
                    if n == 2:
                        after(pe, xpv_copied, b - 1, 2, 1)
                    for kt in range(NX):
                        for j in range(4):
                            h = 4 * n + j
                            mm = pe.matmul(pv_bank[n // 2][32 * j:32 * j + 32, (n % 2) * D:(n % 2 + 1) * D],
                                           XV1[side][:, kt, h, :], xprobs[:, kt, h, :], start=(kt == 0), stop=(kt == NX - 1))
                    mm.then_inc(xpv_in, 1)
                elif name == "xnorm":
                    if n == 0:
                        after(pe, xpv_copied, b, 2, 1)
                    bank_free(pe, turn, (A_USES, B_USES)[n], f"xnorm{n}")
                    for g in range(4):
                        mm = pe.transpose((A, Bk)[n][:, g * P:(g + 1) * P], xpv_sb[:, g, n * P:(n + 1) * P], eye_sb[:])
                    mm.then_inc(xnorm_in, 1)
                elif name == "xattnT":
                    after(pe, xattn_done, b, 2, 1)
                    bank_free(pe, turn, A_USES, "xattnT")
                    for qt in range(NX):
                        mm = pe.transpose(A[:, qt * P:(qt + 1) * P], xattn[:, qt, :], eye_sb[:])
                    mm.then_inc(xattnT_in, 1)
                elif name == "y":
                    after(pe, xattnT_done, b)
                    bank_free(pe, turn, B_USES, "y")
                    pe.matmul(Bk[:, 0:D], xw_sb[:, 3, :], xattnT[:], start=True, stop=True).then_inc(y_in, 1)
                elif name == "x3T":
                    after(pe, xn_done[2], b)
                    bank_free(pe, turn, A_USES, "x3T")
                    for c in range(2):
                        mm = pe.transpose(A[:, c * T:(c + 1) * T], xn[2][:, c * P:(c + 1) * P], eye_sb[:])
                    mm.then_inc(x3T_in, 1)
                elif name == "logits":
                    after(pe, x3T_now_done, b)
                    bank_free(pe, turn, B_USES, "logits")
                    for c in range(2):
                        mm = pe.matmul(Bk[:, 0:E], x3T_now[:, c, :], wr_sb[:, c, :], start=(c == 0), stop=(c == 1))
                    mm.then_inc(logits_in, 1)
                elif name == "gT":
                    after(pe, root_done, b, ROOT_STEPS, ROOT_STEPS - 1)
                    bank_free(pe, turn, A_USES, "gT")
                    pe.transpose(A[0:E, 0:T], root_gates[:], eye_sb[:]).then_inc(gT_in, 1)


            def clear(banks, added=0):
                if added:
                    pe.wait_ge(half_added, added)
                for i in banks:
                    pe.matmul(bank[i][:], zeros[:, 0:P], zeros[:], start=True, stop=False, skip_group_check=True)

            def hidden(it, u, half):
                side, blk = u // 2, u % 2
                if blk == 0:
                    pe.wait_ge(w1_split, it * 2 + side + 1)
                if not (isinstance(it, int) and it == 0):
                    pe.wait_ge(act1_done, it * 4 + u - 3)
                elif side == 0:
                    pe.wait_ge(x3_hi_done, blk + 1)
                at = 1024 * half + 512 * blk
                parts = [(w, xs, c) for w, xs in ((w_hi, x3_hi), (w_lo, x3_hi), (w_hi, x3_lo)) for c in range(2)]
                for i, (w, xs, c) in enumerate(parts):
                    if i == 4 and isinstance(it, int) and it == 0 and side == 0:
                        pe.wait_ge(x3_split, blk + 1)
                    mm = pe.matmul(bank[4 + u][:], r(w[side][:, c, :]), r(xs[:, c, at:at + 512]), start=(i == 0),
                                   stop=(i == len(parts) - 1))
                mm.then_inc(hidden_in, 1)

            def output(it, u):
                side, blk = u // 2, u % 2
                if blk == 0:
                    pe.wait_ge(w2_split, it * 2 + side + 1)
                pe.wait_ge(act2_split, it * 4 + u + 1)
                for t in range(4):
                    tile = 4 * blk + t
                    for a, w in ((act2_hi, w_hi), (act2_hi, w_lo), (act2_lo, w_hi)):
                        mm = pe.matmul(bank[tile // 2][:, (tile % 2) * D:(tile % 2 + 1) * D], r(a[u][:, t * P:(t + 1) * P]),
                                       r(w[side][:, 2:4, :]), start=False, stop=False, skip_group_check=True)
                mm.then_inc(expert_added, 1)

            def expert_pair(it, half, next_half, fresh=False):
                for u in range(4):
                    if u < 2:
                        hidden(it, u + 2, half)
                    elif next_half is not None:
                        hidden(it + 1, u - 2, next_half)
                    if fresh and u < 2:
                        clear((2 * u, 2 * u + 1), 4 * u + 4)
                    output(it, u)

            def close_half():
                for i in range(4):
                    mm = pe.matmul(bank[i][:], zeros[:, 0:P], zeros[:], start=False, stop=True, skip_group_check=True)
                mm.then_inc(half_in, 1)

            for turn in turns(pe):
                if isinstance(turn.it, int) and 1 <= turn.it <= 2:
                    pe.wait_ge(loaded_w, 10 * 16)
                    pe.wait_ge(consts_set, turn.it)
                    pe.wait_ge(cross_set, 2)
                for name, n in turn.steps("PE"):
                    step(turn, name, n)
                    if isinstance(turn.it, int) and turn.it == last:
                        if (name, n) == ("xnorm", 1):
                            pe.wait_ge(xpv_copied, 2 * B)
                            clear(range(4))
                            hidden(0, 0, 0)
                        elif name == "xattnT":
                            hidden(0, 1, 0)

            pe.wait_ge(xattnT_done, B)
            pe.wait_ge(gatesT_done, B - LATE)
            pe.wait_ge(x2_done, B)
            for k, turn in enumerate(late):
                b = turn.batch("R")
                expert_pair(ROUTED * k, 0, 0)
                step(turn, "x3T")
                after(pe, x3T_now_done, b)
                expert_pair(ROUTED * k + 1, 0, 0)
                step(turn, "logits")
                after(pe, logits_done, b)
                with pe.Fori(ROUTED * k + 2, ROUTED * k + ROUTED) as it:
                    expert_pair(it, 0, 0)
                step(turn, "gT")
                after(pe, gatesT_done, b)
            with pe.Fori(ROUTED * LATE, NE // 2 - 1) as it:
                expert_pair(it, 0, 0)
            pe.wait_ge(x3_split, 4)
            expert_pair(NE // 2 - 1, 0, 1)
            close_half()
            expert_pair(NE // 2, 1, 1, fresh=True)
            with pe.Fori(NE // 2 + 1, NE - 1) as it:
                expert_pair(it, 1, 1)
            expert_pair(NE - 1, 1, None)
            close_half()


def kernel(**inputs):
    import numpy as np
    import concourse.bacc as bacc
    from concourse.bass_utils import run_bass_kernel_spmd

    def f(name):
        return np.asarray(inputs[name])

    rows = np.arange(P)
    order = [(2 * (rows % 8) + odd) * 16 + rows // 8 for odd in range(2)]
    wq, wk, wv = f("L0_attn_wq"), f("L0_attn_wk"), f("L0_attn_wv")
    bq, bk = f("L0_attn_bq"), f("L0_attn_bk")
    cols = [wq[:, order[0]], wq[:, order[1]], wk[:, order[0]], wk[:, order[1]], wv[:, 0:P], wv[:, P:2 * P]]
    wqkv = np.stack(cols, axis=1).reshape(2, P, 6, P).transpose(1, 0, 2, 3)
    qk_bias = np.stack([bq[order[0]], bq[order[1]], bk[order[0]], bk[order[1]]], axis=1)
    xorder = (4 * (rows % 4) + rows // 32) * 8 + rows // 4 % 8
    xw = np.stack([f("L0_xattn_Wq")[xorder].T, f("L0_xattn_Wk")[xorder].T, f("L0_xattn_Wv").T, f("L0_xattn_Wo").T], axis=1)
    xqk_bias = np.stack([f("L0_xattn_bq")[xorder], f("L0_xattn_bk")[xorder]], axis=1)
    W1 = np.concatenate([f("L0_ffn_W1"), f("L0_ffn_Ws1").reshape(2, P, 256)])
    W2 = np.concatenate([f("L0_ffn_W2"), f("L0_ffn_Ws2").reshape(256, 2, P).transpose(1, 0, 2)])
    w1 = W1.transpose(0, 2, 1).reshape(-1, 2, P, P).transpose(0, 2, 1, 3)
    w2 = W2.transpose(0, 2, 1).reshape(-1, P, 2, P)
    arrays = {
        "x": f("x"), "ctx_in": f("ctx_2048"), "wqkv": wqkv, "qk_bias": qk_bias,
        "v_bias": f("L0_attn_bv").reshape(2, P).T,
        "wo": f("L0_attn_wo").reshape(2, P, 256).transpose(1, 0, 2),
        "bo": np.broadcast_to(f("L0_attn_bo"), (P, 256)),
        "xw": xw, "xqk_bias": xqk_bias, "xv_bias": f("L0_xattn_bv")[:, None], "xbo": f("L0_xattn_bo")[:, None],
        "wr": f("L0_ffn_Wr").T.reshape(2, P, -1).transpose(1, 0, 2),
        "br": np.broadcast_to(f("L0_ffn_br"), (P, 32)),
        "experts": np.concatenate([w1, w2], axis=2), "eye": np.eye(P, dtype=np.float32),
    }
    arrays = {k: np.ascontiguousarray(v) for k, v in arrays.items()}
    nc = bacc.Bacc("TRN2", target_bir_lowering=False, num_devices=1)
    args = [nc.dram_tensor(k, v.shape, mybir.dt.from_np(v.dtype), kind="ExternalInput").ap() for k, v in arrays.items()]
    out = nc.dram_tensor("out", (16, P, 256), F32, kind="ExternalOutput").ap()
    gates_dram = nc.dram_tensor("gates_dram", (34, 16 * P), F32, kind="Internal").ap()
    decoder_layer(nc, *args, out, gates_dram)
    r = run_bass_kernel_spmd(nc, [arrays], core_ids=[0])
    return r.results[0]["out"]
```
